# Optimizing a Trainium2 kernel written in Bass

```python
import numpy as np
import jax
import jax.numpy as jnp

def _softmax(x, axis=-1):
    return jax.nn.softmax(x, axis=axis)

def _gelu(x):
    return jax.nn.gelu(x, approximate=True)

def _silu(x):
    return jax.nn.silu(x)

def _sigmoid(x):
    return jax.nn.sigmoid(x)

def _layernorm(x, axis=-1, eps=1e-05):
    m = jnp.mean(x, axis=axis, keepdims=True)
    v = jnp.var(x, axis=axis, keepdims=True)
    return (x - m) / jnp.sqrt(v + eps)

def _scatter_add(tgt, idx, src, axis=0):
    return tgt.at[idx].add(src)

def _segment_sum(src, seg, n):
    return jax.ops.segment_sum(src, seg, n)
kernel_name = 'mk_flamingo_gated_d4_seqx_r4_c4c661'

def setup_inputs(seed: int=0):
    np.random.seed(seed)
    _w = jnp.asarray

    def _rec_inputs():
        import jax
        import jax.numpy as jnp
        _rk = jax.random.key(seed)
        x = -0.0005146 + 1 * jax.random.normal(jax.random.fold_in(_rk, 1), (8, 112, 256), jnp.float32)
        _lenS = 112 - jax.random.randint(jax.random.fold_in(_rk, 7), (8,), 0, max(1, 112 // 4) + 1, jnp.int32)
        _lenS2 = 375 - jax.random.randint(jax.random.fold_in(_rk, 8), (8,), 0, max(1, 375 // 4) + 1, jnp.int32)
        _ctx_1024P = jax.random.normal(jax.random.fold_in(_rk, 11), (8, 16, 256), jnp.float32)
        _ctx_1024c = jax.random.dirichlet(jax.random.fold_in(_rk, 511), 0.3 * jnp.ones((16,), jnp.float32), (8, 375))
        _ctx_1024t = jnp.einsum('bsk,bkd->bsd', _ctx_1024c, _ctx_1024P)
        _ctx_1024t = _ctx_1024t * jax.lax.rsqrt(jnp.mean(jnp.square(_ctx_1024t)) + 1e-12) * 0.953939
        ctx_1024 = -0.000392918 + 0.999932 * (_ctx_1024t + 0.3 * jax.random.normal(jax.random.fold_in(_rk, 611), (8, 375, 256), jnp.float32))
        fside_BxSxS2_0 = jax.random.uniform(jax.random.fold_in(_rk, 12), (8, 112, 375), jnp.float32, 0.0, 1)
        _validS = jnp.arange(112)[None, :] < _lenS[:, None]
        _validS2 = jnp.arange(375)[None, :] < _lenS2[:, None]
        _causal = jnp.tril(jnp.ones((112, 112), dtype=bool))
        mask_BxSxS2_ik1 = jnp.where(jnp.broadcast_to(_validS2[:, None, :], (8, 112, 375)), 1, 0).astype(jnp.int32)
        _g = jax.random.normal(jax.random.fold_in(_rk, 9001), (2, 4), jnp.float32)
        _g = jnp.sign(_g) * jnp.maximum(jnp.abs(_g), 1.0) + (_g == 0) * 1.0
        g_xattn = _g[0]
        g_ffn = _g[1]
        return (x, ctx_1024, fside_BxSxS2_0, mask_BxSxS2_ik1, g_xattn, g_ffn)
    x, ctx_1024, fside_BxSxS2_0, mask_BxSxS2_ik1, g_xattn, g_ffn = _rec_inputs()

    def _L0_xattn_setup():
        import jax, jax.numpy as jnp
        import numpy as np
        DIM = 256
        DIM_HEAD = 64
        HEADS = 16
        INNER = DIM_HEAD * HEADS
        EPS = 1e-05

        def layer_norm(x, g, b):
            m = jnp.mean(x, axis=-1, keepdims=True)
            v = jnp.mean(jnp.square(x - m), axis=-1, keepdims=True)
            return (x - m) * jax.lax.rsqrt(v + EPS) * g + b
        key = jax.random.key(seed)
        ks = jax.random.split(key, 8)
        B, N_IMG, N_LAT = (4, 1024, 128)
        std = 1.0 / np.sqrt(DIM)
        return {'image_embeds': jax.random.normal(ks[0], (B, N_IMG, DIM), dtype=jnp.float32), 'latents': jax.random.normal(ks[1], (B, N_LAT, DIM), dtype=jnp.float32), 'ln1_g': jnp.ones((DIM,), jnp.float32), 'ln1_b': jnp.zeros((DIM,), jnp.float32), 'ln2_g': jnp.ones((DIM,), jnp.float32), 'ln2_b': jnp.zeros((DIM,), jnp.float32), 'Wq': jax.random.normal(ks[2], (DIM, INNER), dtype=jnp.float32) * std, 'Wkv': jax.random.normal(ks[3], (DIM, 2 * INNER), dtype=jnp.float32) * std, 'Wo': jax.random.normal(ks[4], (INNER, DIM), dtype=jnp.float32) * std}
    _L0_xattn_all = _L0_xattn_setup()
    _L0_xattn_in = {k: v for k, v in _L0_xattn_all.items() if k in ('ln1_g', 'ln1_b', 'ln2_g', 'ln2_b', 'Wq', 'Wkv', 'Wo')}
    del _L0_xattn_all

    def _L0_ffn_setup():
        import jax, jax.numpy as jnp
        import numpy as np
        D_MODEL, D_FF, RANK = (256, 1024, 64)
        B, S = (4, 1024)
        key = jax.random.key(seed)
        ks = jax.random.split(key, 7)
        return {'x': jax.random.normal(ks[0], (B, S, D_MODEL), dtype=jnp.float32), 'U1': jax.random.normal(ks[1], (D_MODEL, RANK), dtype=jnp.float32) * 0.02, 'V1': jax.random.normal(ks[2], (RANK, D_FF), dtype=jnp.float32) * 0.02, 'b1': jnp.zeros((D_FF,), dtype=jnp.float32), 'U2': jax.random.normal(ks[3], (D_FF, RANK), dtype=jnp.float32) * 0.02, 'V2': jax.random.normal(ks[4], (RANK, D_MODEL), dtype=jnp.float32) * 0.02, 'b2': jnp.zeros((D_MODEL,), dtype=jnp.float32)}
    _L0_ffn_all = _L0_ffn_setup()
    _L0_ffn_in = {k: v for k, v in _L0_ffn_all.items() if k in ('U1', 'V1', 'b1', 'U2', 'V2', 'b2')}
    del _L0_ffn_all

    def _L1_xattn_setup():
        import jax, jax.numpy as jnp
        import numpy as np
        DIM = 256
        key = jax.random.key(seed)
        k1, k2, k3, k4 = jax.random.split(key, 4)
        B, Nq, Nkv = (4, 512, 512)
        x = jax.random.normal(k1, (B, Nq, DIM), dtype=jnp.float32)
        y = jax.random.normal(k2, (B, Nkv, DIM), dtype=jnp.float32)
        Wq = jax.random.normal(k3, (DIM, DIM), dtype=jnp.float32) / np.sqrt(DIM)
        Wkv = jax.random.normal(k4, (DIM, 2 * DIM), dtype=jnp.float32) / np.sqrt(DIM)
        return {'x': x, 'y': y, 'Wq': Wq, 'Wkv': Wkv}
    _L1_xattn_all = _L1_xattn_setup()
    _L1_xattn_in = {k: v for k, v in _L1_xattn_all.items() if k in ('Wq', 'Wkv')}
    del _L1_xattn_all

    def _L1_ffn_setup():
        import jax, jax.numpy as jnp
        import numpy as np
        DIM = 256

        def _reference_tuple_inner(x, W_r, W_k, W_v, mu_r, mu_k):
            B, T, C = x.shape
            x_prev = jnp.concatenate([jnp.zeros((B, 1, C), x.dtype), x[:, :-1, :]], axis=1)
            xr = mu_r * x + (1.0 - mu_r) * x_prev
            xk = mu_k * x + (1.0 - mu_k) * x_prev
            r = jax.nn.sigmoid(jnp.einsum('btc,dc->btd', xr, W_r))
            k = jnp.einsum('btc,dc->btd', xk, W_k)
            k_act = jnp.square(jax.nn.relu(k))
            out = r * jnp.einsum('btc,dc->btd', k_act, W_v)
            new_state = x[:, -1, :]
            return (out, new_state)
        key = jax.random.key(seed)
        ks = jax.random.split(key, 6)
        B, T, C = (8, 512, DIM)
        x = jax.random.normal(ks[0], (B, T, C), dtype=jnp.float32)
        s = 1.0 / np.sqrt(C)
        W_r = jax.random.uniform(ks[1], (C, C), jnp.float32, -s, s)
        W_k = jax.random.uniform(ks[2], (C, C), jnp.float32, -s, s)
        W_v = jax.random.uniform(ks[3], (C, C), jnp.float32, -s, s)
        mu_r = jax.random.uniform(ks[4], (C,), jnp.float32)
        mu_k = jax.random.uniform(ks[5], (C,), jnp.float32)
        return {'x': x, 'W_r': W_r, 'W_k': W_k, 'W_v': W_v, 'mu_r': mu_r, 'mu_k': mu_k}
    _L1_ffn_all = _L1_ffn_setup()
    _L1_ffn_in = {k: v for k, v in _L1_ffn_all.items() if k in ('W_r', 'W_k', 'W_v', 'mu_r', 'mu_k')}
    del _L1_ffn_all

    def _L2_xattn_setup():
        import jax, jax.numpy as jnp
        import numpy as np
        NUM_HEADS = 16
        HIDDEN = 256
        B, S = (2, 512)

        def _split_heads(x, H):
            b, s, d = x.shape
            return x.reshape(b, s, H, d // H).transpose(0, 2, 1, 3)
        key = jax.random.key(seed)
        ks = jax.random.split(key, 14)
        D = HIDDEN
        scale = 1.0 / np.sqrt(D)
        inp = {'query': jax.random.normal(ks[0], (B, S, D), jnp.float32), 'key_in': jax.random.normal(ks[1], (B, S, D), jnp.float32), 'value': jax.random.normal(ks[2], (B, S, D), jnp.float32), 'group_prob': jax.random.uniform(ks[3], (B, S, S), jnp.float32), 'mask': jax.random.randint(ks[4], (B, S, S), 0, 2, jnp.int32), 'wq_k': jax.random.normal(ks[5], (D, D), jnp.float32) * scale, 'wq_b': jnp.zeros((D,), jnp.float32), 'wk_k': jax.random.normal(ks[6], (D, D), jnp.float32) * scale, 'wk_b': jnp.zeros((D,), jnp.float32), 'wv_k': jax.random.normal(ks[7], (D, D), jnp.float32) * scale, 'wv_b': jnp.zeros((D,), jnp.float32), 'wo_k': jax.random.normal(ks[8], (D, D), jnp.float32) * scale, 'wo_b': jnp.zeros((D,), jnp.float32)}
        return inp
    _L2_xattn_all = _L2_xattn_setup()
    _L2_xattn_in = {k: v for k, v in _L2_xattn_all.items() if k in ('wq_k', 'wq_b', 'wk_k', 'wk_b', 'wv_k', 'wv_b', 'wo_k', 'wo_b')}
    del _L2_xattn_all

    def _L2_ffn_setup():
        import jax, jax.numpy as jnp
        import numpy as np
        NUM_EXPERTS = 8
        TOP_K = 2
        HIDDEN = 256
        INTER = 1024
        SOFTCAP = 30.0
        key = jax.random.key(seed)
        ks = jax.random.split(key, 5)
        hidden_states = jax.random.normal(ks[0], (1, 512, HIDDEN), dtype=jnp.float32)
        wg = jax.random.normal(ks[1], (NUM_EXPERTS, HIDDEN), dtype=jnp.float32) * 0.02
        w1 = jax.random.normal(ks[2], (NUM_EXPERTS, INTER, HIDDEN), dtype=jnp.float32) * 0.02
        w3 = jax.random.normal(ks[3], (NUM_EXPERTS, INTER, HIDDEN), dtype=jnp.float32) * 0.02
        w2 = jax.random.normal(ks[4], (NUM_EXPERTS, HIDDEN, INTER), dtype=jnp.float32) * 0.02
        return {'hidden_states': hidden_states, 'wg': wg, 'w1': w1, 'w3': w3, 'w2': w2}
    _L2_ffn_all = _L2_ffn_setup()
    _L2_ffn_in = {k: v for k, v in _L2_ffn_all.items() if k in ('wg', 'w1', 'w3', 'w2')}
    del _L2_ffn_all

    def _L3_xattn_setup():
        import jax, jax.numpy as jnp
        import numpy as np
        B, L, D, H = (4, 512, 256, 16)
        HD = D // H
        SCALE = 1.0 / (D / H) ** 0.5

        def _split_heads(x):
            b, l, _ = x.shape
            return x.reshape(b, l, H, HD).transpose(0, 2, 1, 3)
        key = jax.random.key(seed)
        ks = jax.random.split(key, 11)
        s = 1.0 / np.sqrt(D)
        return {'q': jax.random.normal(ks[0], (B, L, D), jnp.float32), 'k': jax.random.normal(ks[1], (B, L, D), jnp.float32), 'v': jax.random.normal(ks[2], (B, L, D), jnp.float32), 'Wq': jax.random.normal(ks[3], (D, D), jnp.float32) * s, 'bq': jnp.zeros((D,), jnp.float32), 'Wk': jax.random.normal(ks[4], (D, D), jnp.float32) * s, 'bk': jnp.zeros((D,), jnp.float32), 'Wv': jax.random.normal(ks[5], (D, D), jnp.float32) * s, 'bv': jnp.zeros((D,), jnp.float32), 'Wo': jax.random.normal(ks[6], (D, D), jnp.float32) * s, 'bo': jnp.zeros((D,), jnp.float32)}
    _L3_xattn_all = _L3_xattn_setup()
    _L3_xattn_in = {k: v for k, v in _L3_xattn_all.items() if k in ('Wq', 'bq', 'Wk', 'bk', 'Wv', 'bv', 'Wo', 'bo')}
    del _L3_xattn_all

    def _L3_ffn_setup():
        import jax, jax.numpy as jnp
        import numpy as np
        LN_EPS = 1e-05

        def layernorm(x, g, b):
            mu = jnp.mean(x, axis=-1, keepdims=True)
            var = jnp.mean((x - mu) ** 2, axis=-1, keepdims=True)
            return (x - mu) * jax.lax.rsqrt(var + LN_EPS) * g + b

        def act_quant_fake(x):
            scale = 127.0 / jnp.clip(jnp.max(jnp.abs(x), axis=-1, keepdims=True), 1e-05)
            return jnp.clip(jnp.round(x * scale), -128.0, 127.0) / scale

        def weight_quant_fake(w):
            scale = 1.0 / jnp.clip(jnp.mean(jnp.abs(w)), 1e-05)
            return jnp.clip(jnp.round(w * scale), -1.0, 1.0) / scale

        def bitlinear(x, w, b):
            dqx = act_quant_fake(x)
            dqw = weight_quant_fake(w)
            return jnp.einsum('btd,hd->bth', dqx, dqw) + b
        key = jax.random.key(seed)
        ks = jax.random.split(key, 5)
        B, T, D, H = (8, 1024, 256, 1024)
        return {'x': jax.random.normal(ks[0], (B, T, D), dtype=jnp.float32), 'ln1_g': jnp.ones((D,), jnp.float32), 'ln1_b': jnp.zeros((D,), jnp.float32), 'w1': jax.random.normal(ks[1], (H, D), dtype=jnp.float32) * (1.0 / np.sqrt(D)), 'b1': jax.random.normal(ks[2], (H,), dtype=jnp.float32) * 0.02, 'ln2_g': jnp.ones((H,), jnp.float32), 'ln2_b': jnp.zeros((H,), jnp.float32), 'w2': jax.random.normal(ks[3], (D, H), dtype=jnp.float32) * (1.0 / np.sqrt(H)), 'b2': jax.random.normal(ks[4], (D,), jnp.float32) * 0.02}
    _L3_ffn_all = _L3_ffn_setup()
    _L3_ffn_in = {k: v for k, v in _L3_ffn_all.items() if k in ('ln1_g', 'ln1_b', 'w1', 'b1', 'ln2_g', 'ln2_b', 'w2', 'b2')}
    del _L3_ffn_all
    return {'x': x, 'ctx_1024': ctx_1024, 'fside_BxSxS2_0': fside_BxSxS2_0, 'mask_BxSxS2_ik1': mask_BxSxS2_ik1, 'g_xattn': g_xattn, 'g_ffn': g_ffn, 'L0_xattn_ln1_g': _L0_xattn_in['ln1_g'], 'L0_xattn_ln1_b': _L0_xattn_in['ln1_b'], 'L0_xattn_ln2_g': _L0_xattn_in['ln2_g'], 'L0_xattn_ln2_b': _L0_xattn_in['ln2_b'], 'L0_xattn_Wq': _L0_xattn_in['Wq'], 'L0_xattn_Wkv': _L0_xattn_in['Wkv'], 'L0_xattn_Wo': _L0_xattn_in['Wo'], 'L0_ffn_U1': _L0_ffn_in['U1'], 'L0_ffn_V1': _L0_ffn_in['V1'], 'L0_ffn_b1': _L0_ffn_in['b1'], 'L0_ffn_U2': _L0_ffn_in['U2'], 'L0_ffn_V2': _L0_ffn_in['V2'], 'L0_ffn_b2': _L0_ffn_in['b2'], 'L1_xattn_Wq': _L1_xattn_in['Wq'], 'L1_xattn_Wkv': _L1_xattn_in['Wkv'], 'L1_ffn_W_r': _L1_ffn_in['W_r'], 'L1_ffn_W_k': _L1_ffn_in['W_k'], 'L1_ffn_W_v': _L1_ffn_in['W_v'], 'L1_ffn_mu_r': _L1_ffn_in['mu_r'], 'L1_ffn_mu_k': _L1_ffn_in['mu_k'], 'L2_xattn_wq_k': _L2_xattn_in['wq_k'], 'L2_xattn_wq_b': _L2_xattn_in['wq_b'], 'L2_xattn_wk_k': _L2_xattn_in['wk_k'], 'L2_xattn_wk_b': _L2_xattn_in['wk_b'], 'L2_xattn_wv_k': _L2_xattn_in['wv_k'], 'L2_xattn_wv_b': _L2_xattn_in['wv_b'], 'L2_xattn_wo_k': _L2_xattn_in['wo_k'], 'L2_xattn_wo_b': _L2_xattn_in['wo_b'], 'L2_ffn_wg': _L2_ffn_in['wg'], 'L2_ffn_w1': _L2_ffn_in['w1'], 'L2_ffn_w3': _L2_ffn_in['w3'], 'L2_ffn_w2': _L2_ffn_in['w2'], 'L3_xattn_Wq': _L3_xattn_in['Wq'], 'L3_xattn_bq': _L3_xattn_in['bq'], 'L3_xattn_Wk': _L3_xattn_in['Wk'], 'L3_xattn_bk': _L3_xattn_in['bk'], 'L3_xattn_Wv': _L3_xattn_in['Wv'], 'L3_xattn_bv': _L3_xattn_in['bv'], 'L3_xattn_Wo': _L3_xattn_in['Wo'], 'L3_xattn_bo': _L3_xattn_in['bo'], 'L3_ffn_ln1_g': _L3_ffn_in['ln1_g'], 'L3_ffn_ln1_b': _L3_ffn_in['ln1_b'], 'L3_ffn_w1': _L3_ffn_in['w1'], 'L3_ffn_b1': _L3_ffn_in['b1'], 'L3_ffn_ln2_g': _L3_ffn_in['ln2_g'], 'L3_ffn_ln2_b': _L3_ffn_in['ln2_b'], 'L3_ffn_w2': _L3_ffn_in['w2'], 'L3_ffn_b2': _L3_ffn_in['b2']}

def reference(x, ctx_1024, fside_BxSxS2_0, mask_BxSxS2_ik1, g_xattn, g_ffn, L0_xattn_ln1_g, L0_xattn_ln1_b, L0_xattn_ln2_g, L0_xattn_ln2_b, L0_xattn_Wq, L0_xattn_Wkv, L0_xattn_Wo, L0_ffn_U1, L0_ffn_V1, L0_ffn_b1, L0_ffn_U2, L0_ffn_V2, L0_ffn_b2, L1_xattn_Wq, L1_xattn_Wkv, L1_ffn_W_r, L1_ffn_W_k, L1_ffn_W_v, L1_ffn_mu_r, L1_ffn_mu_k, L2_xattn_wq_k, L2_xattn_wq_b, L2_xattn_wk_k, L2_xattn_wk_b, L2_xattn_wv_k, L2_xattn_wv_b, L2_xattn_wo_k, L2_xattn_wo_b, L2_ffn_wg, L2_ffn_w1, L2_ffn_w3, L2_ffn_w2, L3_xattn_Wq, L3_xattn_bq, L3_xattn_Wk, L3_xattn_bk, L3_xattn_Wv, L3_xattn_bv, L3_xattn_Wo, L3_xattn_bo, L3_ffn_ln1_g, L3_ffn_ln1_b, L3_ffn_w1, L3_ffn_b1, L3_ffn_ln2_g, L3_ffn_ln2_b, L3_ffn_w2, L3_ffn_b2):
    import jax
    import jax.numpy as jnp

    def _L0_xattn_ref(image_embeds, latents, ln1_g, ln1_b, ln2_g, ln2_b, Wq, Wkv, Wo):
        import jax, jax.numpy as jnp
        import numpy as np
        DIM = 256
        DIM_HEAD = 64
        HEADS = 16
        INNER = DIM_HEAD * HEADS
        EPS = 1e-05

        def layer_norm(x, g, b):
            m = jnp.mean(x, axis=-1, keepdims=True)
            v = jnp.mean(jnp.square(x - m), axis=-1, keepdims=True)
            return (x - m) * jax.lax.rsqrt(v + EPS) * g + b
        B, S_lat, _ = latents.shape
        x = layer_norm(image_embeds, ln1_g, ln1_b)
        l = layer_norm(latents, ln2_g, ln2_b)
        q = l @ Wq
        kv_in = jnp.concatenate([x, l], axis=1)
        kv = kv_in @ Wkv
        k, v = jnp.split(kv, 2, axis=-1)

        def to_heads(t):
            return t.reshape(t.shape[0], t.shape[1], HEADS, DIM_HEAD).transpose(0, 2, 1, 3)
        q, k, v = (to_heads(q), to_heads(k), to_heads(v))
        scale = 1.0 / np.sqrt(np.sqrt(DIM_HEAD))
        w = jnp.einsum('bhqd,bhkd->bhqk', q * scale, k * scale)
        w = jax.nn.softmax(w.astype(jnp.float32), axis=-1).astype(q.dtype)
        out = jnp.einsum('bhqk,bhkd->bhqd', w, v)
        out = out.transpose(0, 2, 1, 3).reshape(B, S_lat, INNER)
        return out @ Wo

    def _L0_ffn_ref(x, U1, V1, b1, U2, V2, b2):
        import jax, jax.numpy as jnp
        import numpy as np
        D_MODEL, D_FF, RANK = (256, 1024, 64)
        B, S = (4, 1024)
        P = jnp.einsum('bsd,dr->bsr', x, U1)
        H = jax.nn.gelu(jnp.einsum('bsr,rf->bsf', P, V1) + b1)
        Q = jnp.einsum('bsf,fr->bsr', H, U2)
        return jnp.einsum('bsr,rd->bsd', Q, V2) + b2

    def _L1_xattn_ref(x, y, Wq, Wkv):
        import jax, jax.numpy as jnp
        import numpy as np
        DIM = 256
        q = jnp.einsum('bnd,de->bne', x, Wq)
        kv = jnp.einsum('bnd,de->bne', y, Wkv)
        B, Nkv, _ = kv.shape
        kv = kv.reshape(B, Nkv, 2, DIM).transpose(2, 0, 1, 3)
        k, v = (kv[0], kv[1])
        scale = DIM ** (-0.5)
        attn = jnp.einsum('bqd,bkd->bqk', q * scale, k)
        attn = jax.nn.softmax(attn, axis=-1)
        out = jnp.einsum('bqk,bkd->bqd', attn, v)
        return out

    def _L1_ffn_ref(x, W_r, W_k, W_v, mu_r, mu_k):
        import jax, jax.numpy as jnp
        import numpy as np
        DIM = 256

        def _reference_tuple_inner(x, W_r, W_k, W_v, mu_r, mu_k):
            B, T, C = x.shape
            x_prev = jnp.concatenate([jnp.zeros((B, 1, C), x.dtype), x[:, :-1, :]], axis=1)
            xr = mu_r * x + (1.0 - mu_r) * x_prev
            xk = mu_k * x + (1.0 - mu_k) * x_prev
            r = jax.nn.sigmoid(jnp.einsum('btc,dc->btd', xr, W_r))
            k = jnp.einsum('btc,dc->btd', xk, W_k)
            k_act = jnp.square(jax.nn.relu(k))
            out = r * jnp.einsum('btc,dc->btd', k_act, W_v)
            new_state = x[:, -1, :]
            return (out, new_state)
        return _reference_tuple_inner(x, W_r, W_k, W_v, mu_r, mu_k)[0]

    def _L2_xattn_ref(query, key_in, value, group_prob, mask, wq_k, wq_b, wk_k, wk_b, wv_k, wv_b, wo_k, wo_b):
        import jax, jax.numpy as jnp
        import numpy as np
        NUM_HEADS = 16
        HIDDEN = 256
        B, S = (2, 512)

        def _split_heads(x, H):
            b, s, d = x.shape
            return x.reshape(b, s, H, d // H).transpose(0, 2, 1, 3)
        H = NUM_HEADS
        dh = query.shape[-1] // H
        q = _split_heads(query @ wq_k + wq_b, H)
        k = _split_heads(key_in @ wk_k + wk_b, H)
        v = _split_heads(value @ wv_k + wv_b, H)
        logits = jnp.einsum('bhqd,bhkd->bhqk', q, k) / jnp.sqrt(jnp.asarray(dh, q.dtype))
        neg = (1.0 - mask.astype(q.dtype)) * -1000000000.0
        logits = logits + neg[:, None, :, :]
        attn = jax.nn.softmax(logits, axis=-1)
        attn = attn * group_prob[:, None, :, :]
        out = jnp.einsum('bhqk,bhkd->bhqd', attn, v)
        out = out.transpose(0, 2, 1, 3).reshape(query.shape[0], -1, H * dh)
        return out @ wo_k + wo_b

    def _L2_ffn_ref(hidden_states, wg, w1, w3, w2):
        import jax, jax.numpy as jnp
        import numpy as np
        NUM_EXPERTS = 8
        TOP_K = 2
        HIDDEN = 256
        INTER = 1024
        SOFTCAP = 30.0
        orig_shape = hidden_states.shape
        x = hidden_states.reshape(-1, HIDDEN)
        T = x.shape[0]
        logits = x @ wg.T
        logits = SOFTCAP * jnp.tanh(logits / SOFTCAP)
        probs = jax.nn.softmax(logits, axis=-1)
        topk_vals, topk_ids = jax.lax.top_k(probs, TOP_K)
        topk_w = topk_vals / jnp.sum(topk_vals, axis=-1, keepdims=True)
        route = jnp.zeros((T, NUM_EXPERTS), dtype=x.dtype)
        route = route.at[jnp.arange(T)[:, None], topk_ids].set(topk_w)
        h1 = jnp.einsum('th,eih->tei', x, w1)
        h3 = jnp.einsum('th,eih->tei', x, w3)
        act = jax.nn.gelu(h1, approximate=False) * h3
        expert_out = jnp.einsum('tei,ehi->teh', act, w2)
        out = jnp.einsum('teh,te->th', expert_out, route)
        return out.reshape(orig_shape)

    def _L3_xattn_ref(q, k, v, Wq, bq, Wk, bk, Wv, bv, Wo, bo):
        import jax, jax.numpy as jnp
        import numpy as np
        B, L, D, H = (4, 512, 256, 16)
        HD = D // H
        SCALE = 1.0 / (D / H) ** 0.5

        def _split_heads(x):
            b, l, _ = x.shape
            return x.reshape(b, l, H, HD).transpose(0, 2, 1, 3)
        qh = _split_heads(q @ Wq.T + bq)
        kh = _split_heads(k @ Wk.T + bk)
        vh = _split_heads(v @ Wv.T + bv)
        scores = jnp.einsum('bhqd,bhkd->bhqk', qh, kh) * SCALE
        attn = jax.nn.softmax(scores, axis=-1)
        out = jnp.einsum('bhqk,bhkd->bhqd', attn, vh)
        out = out.transpose(0, 2, 1, 3).reshape(q.shape[0], q.shape[1], D)
        return out @ Wo.T + bo

    def _L3_ffn_ref(x, ln1_g, ln1_b, w1, b1, ln2_g, ln2_b, w2, b2):
        import jax, jax.numpy as jnp
        import numpy as np
        LN_EPS = 1e-05

        def layernorm(x, g, b):
            mu = jnp.mean(x, axis=-1, keepdims=True)
            var = jnp.mean((x - mu) ** 2, axis=-1, keepdims=True)
            return (x - mu) * jax.lax.rsqrt(var + LN_EPS) * g + b

        def act_quant_fake(x):
            scale = 127.0 / jnp.clip(jnp.max(jnp.abs(x), axis=-1, keepdims=True), 1e-05)
            return jnp.clip(jnp.round(x * scale), -128.0, 127.0) / scale

        def weight_quant_fake(w):
            scale = 1.0 / jnp.clip(jnp.mean(jnp.abs(w)), 1e-05)
            return jnp.clip(jnp.round(w * scale), -1.0, 1.0) / scale

        def bitlinear(x, w, b):
            dqx = act_quant_fake(x)
            dqw = weight_quant_fake(w)
            return jnp.einsum('btd,hd->bth', dqx, dqw) + b
        h = layernorm(x, ln1_g, ln1_b)
        h = bitlinear(h, w1, b1)
        h = jax.nn.gelu(h, approximate=False)
        h = layernorm(h, ln2_g, ln2_b)
        h = bitlinear(h, w2, b2)
        return h
    x = x + jnp.tanh(g_xattn[0]) * _L0_xattn_ref(ctx_1024, _layernorm(x, axis=-1), L0_xattn_ln1_g, L0_xattn_ln1_b, L0_xattn_ln2_g, L0_xattn_ln2_b, L0_xattn_Wq, L0_xattn_Wkv, L0_xattn_Wo)
    x = x + jnp.tanh(g_ffn[0]) * _L0_ffn_ref(_layernorm(x, axis=-1), L0_ffn_U1, L0_ffn_V1, L0_ffn_b1, L0_ffn_U2, L0_ffn_V2, L0_ffn_b2)
    x = x + jnp.tanh(g_xattn[1]) * _L1_xattn_ref(_layernorm(x, axis=-1), ctx_1024, L1_xattn_Wq, L1_xattn_Wkv)
    x = x + jnp.tanh(g_ffn[1]) * _L1_ffn_ref(_layernorm(x, axis=-1), L1_ffn_W_r, L1_ffn_W_k, L1_ffn_W_v, L1_ffn_mu_r, L1_ffn_mu_k)
    x = x + jnp.tanh(g_xattn[2]) * _L2_xattn_ref(_layernorm(x, axis=-1), ctx_1024, ctx_1024, fside_BxSxS2_0, mask_BxSxS2_ik1, L2_xattn_wq_k, L2_xattn_wq_b, L2_xattn_wk_k, L2_xattn_wk_b, L2_xattn_wv_k, L2_xattn_wv_b, L2_xattn_wo_k, L2_xattn_wo_b)
    x = x + jnp.tanh(g_ffn[2]) * _L2_ffn_ref(_layernorm(x, axis=-1), L2_ffn_wg, L2_ffn_w1, L2_ffn_w3, L2_ffn_w2)
    x = x + jnp.tanh(g_xattn[3]) * _L3_xattn_ref(_layernorm(x, axis=-1), ctx_1024, ctx_1024, L3_xattn_Wq, L3_xattn_bq, L3_xattn_Wk, L3_xattn_bk, L3_xattn_Wv, L3_xattn_bv, L3_xattn_Wo, L3_xattn_bo)
    x = x + jnp.tanh(g_ffn[3]) * _L3_ffn_ref(_layernorm(x, axis=-1), L3_ffn_ln1_g, L3_ffn_ln1_b, L3_ffn_w1, L3_ffn_b1, L3_ffn_ln2_g, L3_ffn_ln2_b, L3_ffn_w2, L3_ffn_b2)
    return x

_drawn_inputs = setup_inputs


def setup_inputs(seed=0):
    import zlib

    import numpy as np

    out = dict(_drawn_inputs(seed))
    spreads = {'L0_xattn_ln1_g': (1.0, 0.2),
     'L0_xattn_ln1_b': (0.0, 0.1),
     'L0_xattn_ln2_g': (1.0, 0.2),
     'L0_xattn_ln2_b': (0.0, 0.1),
     'L0_ffn_b1': (0.0, 0.786),
     'L0_ffn_b2': (0.0, 0.753),
     'L2_xattn_wq_b': (0.0, 2.0),
     'L2_xattn_wk_b': (0.0, 2.0),
     'L2_xattn_wv_b': (0.0, 2.0),
     'L2_xattn_wo_b': (0.0, 2.0),
     'L3_xattn_bq': (0.0, 2.0),
     'L3_xattn_bk': (0.0, 2.0),
     'L3_xattn_bv': (0.0, 2.0),
     'L3_xattn_bo': (0.0, 2.0),
     'L3_ffn_ln1_g': (1.0, 0.6),
     'L3_ffn_ln1_b': (0.0, 2.0),
     'L3_ffn_ln2_g': (1.0, 0.6),
     'L3_ffn_ln2_b': (0.0, 2.0)}
    factors = {'fside_BxSxS2_0': 148.872,
     'g_ffn': 24.168,
     'L0_ffn_U1': 8.0,
     'L0_ffn_V1': 8.0,
     'L0_ffn_U2': 6.581,
     'L0_ffn_V2': 6.717,
     'L1_ffn_W_r': 21.178,
     'L1_ffn_mu_r': 45.128,
     'L2_ffn_wg': 28.632,
     'L2_ffn_w1': 26.016,
     'L2_ffn_w3': 25.608,
     'L2_ffn_w2': 25.6,
     'L3_ffn_b1': 200.0,
     'L3_ffn_b2': 200.0,
     'L1_xattn_Wq': 2.896,
     'L1_ffn_W_k': 4.619,
     'L1_ffn_W_v': 5.0,
     'L1_ffn_mu_k': 8.0,
     'L3_xattn_Wq': 31.656,
     'L3_xattn_Wk': 29.512,
     'L2_xattn_wq_k': 8.0,
     'L2_xattn_wk_k': 5.021,
     'L2_xattn_wv_k': 3.777,
     'L2_xattn_wo_k': 2.696,
     'L3_xattn_Wv': 8.0,
     'L3_xattn_Wo': 8.0,
     'L3_ffn_w1': 8.0,
     'L3_ffn_w2': 8.0}
    for name, (base, spread) in spreads.items():
        noise = np.random.default_rng([zlib.crc32(name.encode()), seed]).standard_normal(out[name].shape)
        drawn = base * np.exp(spread * noise) if base else spread * noise
        out[name] = jnp.asarray(drawn.astype(out[name].dtype))
    for name, factor in factors.items():
        out[name] = (out[name] * factor).astype(out[name].dtype)
    return out
```

```python
from contextlib import ExitStack

import concourse.bass as bass
from concourse import mybir

ALU = mybir.AluOpType
ACT = mybir.ActivationFunctionType
AX = mybir.AxisListType.X
F32 = mybir.dt.float32
F32R = mybir.dt.float32r
BF16 = mybir.dt.bfloat16
I32 = mybir.dt.int32

P = 128
B = 8
T = 112
S2 = 375
D = 256
DC = D // P
R = B * T
CR = S2 // 3
EPS = 1e-5
ARENA = 47000


def after(eng, sem, count):
    if isinstance(count, int) and count <= 0:
        return
    eng.wait_ge(sem, count)


class Memory:

    def __init__(self, nc, ctx, st, phase, words=ARENA):
        self.nc, self.ctx, self.phase, self.words = nc, ctx, phase, words
        self.arena = ctx.enter_context(nc.sbuf_tensor(f"{phase}_arena", [P, words], F32)) if words else None
        self.banks = st["banks"]
        self.at, self.bank = 0, 0
        self.used = st["semaphores"]

    def sb(self, name, shape, dt=F32):
        size = 1
        for n in shape[1:]:
            size *= n
        words = size if dt != BF16 else size // 2
        view = self.arena[0:shape[0], self.at:self.at + words]
        self.at += words + words % 2
        assert self.at <= self.words, (self.phase, name, self.at)
        if dt != F32:
            view = view.bitcast(dt)
        if len(shape) > 2:
            names = "abcd"[:len(shape) - 1]
            view = view.rearrange(f"p ({' '.join(names)}) -> p {' '.join(names)}",
                                  **dict(zip(names, shape[1:])))
        return view

    def rounded(self, name, shape):
        return self.ctx.enter_context(self.nc.sbuf_tensor(f"{self.phase}_{name}", shape, F32R))

    def ps(self, name, banks=1):
        first = self.bank
        self.bank += banks
        assert self.bank <= 8
        return self.banks[:, first, :] if banks == 1 else self.banks[:, first:first + banks, :]

    def sem(self, name):
        self.used.append(self.nc.alloc_semaphore(name=f"{self.phase}_{name}"))
        return self.used[-1]


def recycle_semaphores(nc, st, most=90):
    if len(st["semaphores"]) > most:
        nc.clear_and_free_semaphores(st["semaphores"])
        nc.all_engine_barrier()
        st["semaphores"].clear()


def in_pairs(loop_engine, run):
    run(0, 0, True, False)
    with loop_engine.Fori(0, (B - 2) // 2) as i:
        run(i * 2 + 1, 1, False, False)
        run(i * 2 + 2, 0, False, False)
    run(B - 1, (B - 1) % 2, False, True)


def split_product(pe, out, stationary, moving, start, stop):
    (sh, sl), (mh, ml) = stationary, moving
    pe.matmul(out, sh, mh, start=start, stop=False)
    pe.matmul(out, sh, ml, start=False, stop=False)
    return pe.matmul(out, sl, mh, start=False, stop=stop)


def broadcast_rows(ap, rows):
    return bass.AP(tensor=ap.tensor, offset=ap.offset, ap=[[0, rows], *[list(d) for d in ap.ap]])


def normalize_phase(nc, st, phase, out, rounds=1, affine=None, keep_x=None):
    x, ident = st["x"], st["ident"]
    with ExitStack() as ctx:
        m = Memory(nc, ctx, st, phase + "n")
        stats = m.sb("stats", [T, B, 6])
        mv = m.sb("mv", [T, B, 2])
        ve = m.sb("ve", [T, B])
        rstd = m.sb("rstd", [T, B])
        half = m.sb("half", [T, B])
        xn = m.sb("xn", [T, B, D])
        psT = [m.ps(f"psT{j}")[:, 0:4 * T].rearrange("p (b t) -> p b t", b=4) for j in range(4)]
        gb = m.sb("gb", [P, 2, DC]) if affine else None
        half_set, gb_loaded = m.sem("half_set"), m.sem("gb_loaded")
        stats_done, mv_done, ve_done = m.sem("stats_done"), m.sem("mv_done"), m.sem("ve_done")
        rstd_done, xn_done = m.sem("rstd_done"), m.sem("xn_done")
        turned, evacuated = m.sem("turned"), m.sem("evacuated")
        block = ctx.enter_context(nc.Block())

        @block.sync
        def _(sp):
            if affine:
                for n, v in enumerate(affine):
                    sp.dma_start(gb[:, n, :], v.rearrange("(c p) -> p c", p=P),
                                 allow_slow_non_contiguous=True).then_inc(gb_loaded, 16)

        @block.gpsimd
        def _(pool):
            pool.memset(half[:], -0.5).then_inc(half_set, 1)
            pool.wait_ge(half_set, 1)
            for r in range(rounds):
                pool.wait_ge(ve_done, r + 1)
                pool.tensor_tensor(rstd[:], ve[:], half[:], ALU.pow).then_inc(rstd_done, 1)

        @block.vector
        def _(dve):
            for r in range(rounds):
                src = x if r == 0 else xn
                if r:
                    dve.wait_ge(xn_done, B * r)
                for b in range(B):
                    dve.bn_stats(stats[:, b, :], src[:, b, :]).then_inc(stats_done, 1)
                for b in range(B):
                    dve.wait_ge(stats_done, B * r + b + 1)
                    dve.bn_aggr(mv[:, b, :], stats[:, b, :]).then_inc(mv_done, 1)
                dve.wait_ge(mv_done, B * (r + 1))
                dve.tensor_scalar(ve[:], mv[:, :, 1], EPS, None, ALU.add).then_inc(ve_done, 1)
                dve.wait_ge(rstd_done, r + 1)
                for b in range(B):
                    dve.tensor_scalar(xn[:, b, :], src[:, b, :], mv[:, b, 0:1], rstd[:, b:b + 1],
                                      ALU.subtract, ALU.mult).then_inc(xn_done, 1)
            if affine:
                dve.wait_ge(gb_loaded, 32)
            for n in range(2 * DC):
                c, k = n // 2, n % 2
                dst = out[:, c, 4 * k * T:4 * (k + 1) * T].rearrange("p (b t) -> p b t", b=4)
                dve.wait_ge(turned, n + 1)
                if affine:
                    dve.tensor_scalar(dst, psT[n][:], gb[:, 0, c:c + 1], gb[:, 1, c:c + 1],
                                      ALU.mult, ALU.add).then_inc(evacuated, 1)
                else:
                    dve.tensor_copy(dst, psT[n][:]).then_inc(evacuated, 1)

        @block.tensor
        def _(pe):
            pe.wait_ge(xn_done, B * rounds)
            for n in range(2 * DC):
                c, k = n // 2, n % 2
                for j in range(4):
                    mm = pe.transpose(psT[n][:, j, :], xn[:, 4 * k + j, c * P:(c + 1) * P],
                                      ident[0:T, 0:T])
                mm.then_inc(turned, 1)


class Shape:

    def __init__(self, heads, width, keys, scale, look):
        self.heads, self.scale, self.look = heads, scale, look
        self.inner = heads * width
        self.width = width
        self.keys = keys
        n = -(-keys // P)
        size = -(-keys // n)
        self.chunks = [(c * size, min(size, keys - c * size)) for c in range(n)]
        self.size = size
        self.mc = self.inner // P


def attention_phase(nc, st, phase, A, xT, wq, wk, wv, wo=None, qb=None, kb=None, vb=None, ob=None,
                    ctxT=None, ctx_rows=None, ctx_gb=None, group=None, mask=None, gate=0):
    x, ident, tg = st["x"], st["ident"], st["tanh_g"]
    H, LA, NC, MC = A.heads, A.look, len(A.chunks), A.mc
    KEYS, SZ = A.keys, A.size
    RP = 4 if H % 4 == 0 else 2
    narrow = A.width < 64
    single = H == 1
    HG = P // A.width if narrow else 1
    VN = min(512, A.inner)

    pieces = []
    if ctx_rows is not None:
        pieces += [("C", 0), ("C", 1)]
    pieces += [("K", m) for m in range(MC)]
    QG = min(4, MC)
    pieces += [("Q", j) for j in range(MC // QG)]
    pieces += [("V", (c, f)) for c in range(NC) for f in range(A.inner // VN)]
    first_pieces = list(pieces)
    kq_end0 = 1 + max(j for j, p in enumerate(first_pieces) if p[0] in "KQ")
    if wo is not None:
        pieces.insert(3, ("O", 0))
    NP, NP0 = len(pieces), len(first_pieces)
    OUT = [p[0] for p in pieces].index("O") if wo is not None else None
    HAS_OUT = int(wo is not None)
    kq_end = 1 + max(j for j, p in enumerate(pieces) if p[0] in "KQ")
    steps = H - LA - 1 if H > 1 else 1
    at_step = [[] for _ in range(H)]
    for j in range(NP):
        at_step[1 + j * steps // NP if H > 1 else 0].append(j)

    def count_of(b, j, first, last):
        if first:
            return NP0 + j - (HAS_OUT and j > OUT)
        return NP0 - HAS_OUT + NP * b + (0 if last else j)

    def ring_of(u, j, first, last):
        return count_of(u if not first else 0, j, first, last) % 2

    def steps_pieces(h, first, last):
        found = []
        for j in at_step[h]:
            kind, arg = pieces[j]
            if kind == "O" and first or kind != "O" and last:
                continue
            found.append((j, kind, arg))
        return found

    def done_of(b, end, end0):
        if isinstance(b, int) and b == 0:
            return end0
        return NP0 - HAS_OUT + NP * (b - 1) + end

    with ExitStack() as ctx:
        m = Memory(nc, ctx, st, phase)
        wqs = m.sb("wq", [P, DC, A.inner])
        wks = m.sb("wk", [P, DC, A.inner])
        wvs = m.sb("wv", [P, DC, A.inner])
        wos = m.sb("wo", [P, MC, D]) if wo is not None else None
        kvT = [m.sb(f"kvT{u}", [P, DC, KEYS]) for u in range(2)]
        kT = [m.sb(f"kT{u}", [P, MC, KEYS]) for u in range(2)]
        hq = H // MC if not single else 1
        qm = [m.sb(f"qm{u}", [P, MC, hq, T]) for u in range(2)]
        if narrow:
            v = [m.sb(f"v{u}", [SZ, NC, MC, HG, P]) for u in range(2)]
            qs = m.sb("qs", [P, MC, T])
        else:
            v = [m.sb(f"v{u}", [SZ, NC, A.inner]) for u in range(2)]
        prob = [m.sb(f"prob{j}", [T, KEYS]) for j in range(RP)]
        probT = [m.sb(f"probT{j}", [SZ, NC, T]) for j in range(2)]
        oT = m.sb("oT", [P, MC, T]) if wo is not None else None
        negmax = m.sb("negmax", [T, RP])
        rowmax = m.sb("rowmax", [T, RP])
        total = m.sb("total", [T, RP])
        inv = m.sb("inv", [T, RP])
        qbs = m.sb("qb", [P, MC]) if qb is not None else None
        kbs = m.sb("kb", [P, MC]) if kb is not None else None
        vbs = m.sb("vb", [P, A.inner]) if vb is not None else None
        obs = m.sb("ob", [T, D]) if ob is not None else None
        if ctx_rows is not None:
            rows = m.sb("rows", [CR, 3 * B, D])
            cn = [m.sb(f"cn{u}", [CR, 3, D]) for u in range(2)]
            cstats = m.sb("cstats", [CR, 3 * B, 6])
            cmv = m.sb("cmv", [CR, 3 * B, 2])
            cve = m.sb("cve", [CR, 3 * B])
            crstd = m.sb("crstd", [CR, 3 * B])
            chalf = m.sb("chalf", [CR, 3 * B])
            cgb = m.sb("cgb", [P, 2, DC])
        if group is not None:
            gp = [m.sb(f"gp{u}", [T, KEYS]) for u in range(2)]
            mk = [m.sb(f"mk{u}", [T, KEYS], I32) for u in range(2)]
            neg = [m.sb(f"neg{u}", [T, KEYS]) for u in range(2)]
            scored = [m.sb(f"scored{j}", [T, KEYS]) for j in range(RP)]
        psS = [m.ps(f"psS{j}") for j in range(2)]
        psT = [m.ps(f"psT{j}") for j in range(2)]
        psO = [m.ps(f"psO{j}") for j in range(2)]
        psP = [m.ps(f"psP{j}") for j in range(2)]

        w_loaded, zeroed = m.sem("w_loaded"), m.sem("zeroed")
        ctx_loaded = [m.sem(f"ctx_loaded{u}") for u in range(2)]
        group_loaded = [m.sem(f"group_loaded{u}") for u in range(2)]
        rows_loaded = [m.sem(f"rows_loaded{q}") for q in range(4)]
        cstats_done, cmv_done, cve_done = m.sem("cstats_done"), m.sem("cmv_done"), m.sem("cve_done")
        crstd_done, cn_done, lat_copied = m.sem("crstd_done"), m.sem("cn_done"), m.sem("lat_copied")
        piece_ready, piece_evac, q_moved = m.sem("piece_ready"), m.sem("piece_evac"), m.sem("q_moved")
        s_ready, max_raw, max_ready = m.sem("s_ready"), m.sem("max_raw"), m.sem("max_ready")
        exp_done, inv_done, p_ready = m.sem("exp_done"), m.sem("inv_done"), m.sem("p_ready")
        t_ready, pt_copied, pv_done = m.sem("t_ready"), m.sem("pt_copied"), m.sem("pv_done")
        o_copied, x_updated, neg_made = m.sem("o_copied"), m.sem("x_updated"), m.sem("neg_made")
        biased, q_part, v_part = m.sem("biased"), m.sem("q_part"), m.sem("v_part")
        turn_cleared = m.sem("turn_cleared")
        headmask = st["headmask"]
        LAST_OUT = NP0 - HAS_OUT + NP * (B - 1) + 1
        ZEROED = 2 * (not single) + (ctx_rows is not None)
        UNEVEN = A.chunks[-1][1] != SZ

        def ring2(u, h):
            return u if single else h % 2

        def ring4(u, h):
            return u if single else h % 4

        def diagonal(flat, n, width):
            dims = [list(d) for d in flat.ap]
            return bass.AP(tensor=flat.tensor, offset=flat.offset,
                           ap=[dims[0], [P + width, n], [1, width]])

        block = ctx.enter_context(nc.Block())
        N_W = 3 + sum(z is not None for z in (wo, qb, kb, vb, ob)) + 2 * (ctx_gb is not None)
        G = MC if not single else 1
        GROUPS = 2 if not single else 1

        def later_batches(loop_engine, run):
            run(2, 0)
            with loop_engine.Fori(0, (B - 4) // 2) as i:
                run(i * 2 + 3, 1)
                run(i * 2 + 4, 0)
            run(B - 1, 1)

        @block.sync
        def _(sp):
            if ctx_rows is not None:
                for q in range(4):
                    sp.dma_start(rows[:, 6 * q:6 * q + 6, :],
                                 ctx_rows[2 * q:2 * q + 2].rearrange("b (c p) d -> p (b c) d", p=CR)
                                 ).then_inc(rows_loaded[q], 16)
                for n, z in enumerate(ctx_gb):
                    sp.dma_start(cgb[:, n, :], z.rearrange("(c p) -> p c", p=P),
                                 allow_slow_non_contiguous=True).then_inc(w_loaded, 16)
            else:
                for b in range(2):
                    sp.dma_start(kvT[b][:], ctxT[:, b].rearrange("(c p) s -> p c s", p=P)
                                 ).then_inc(ctx_loaded[b], 16)
            sp.dma_start(wks[:], wk.rearrange("(c p) n -> p c n", p=P)).then_inc(w_loaded, 16)
            sp.dma_start(wqs[:], wq.rearrange("(c p) n -> p c n", p=P)).then_inc(w_loaded, 16)
            sp.dma_start(wvs[:], wv.rearrange("(c p) n -> p c n", p=P)).then_inc(w_loaded, 16)
            if wo is not None:
                sp.dma_start(wos[:], wo.rearrange("(c p) n -> p c n", p=P)).then_inc(w_loaded, 16)
            for z, t in ((qb, qbs), (kb, kbs)):
                if z is not None:
                    sp.dma_start(t[:], z.rearrange("(c p) -> p c", p=P),
                                 allow_slow_non_contiguous=True).then_inc(w_loaded, 16)
            if vb is not None:
                sp.dma_start(vbs[:], broadcast_rows(vb, P)).then_inc(w_loaded, 16)
            if ob is not None:
                sp.dma_start(obs[:], broadcast_rows(ob, T)).then_inc(w_loaded, 16)

            def loads(b, u):
                if ctx_rows is None:
                    sp.wait_ge(piece_evac, done_of(b - 2, NP, NP0))
                    sp.dma_start(kvT[u][:], ctxT[:, bass.ds(b, 1)].rearrange(
                        "(c p) b s -> p c (b s)", p=P)).then_inc(ctx_loaded[u], 16)
                if group is not None:
                    sp.wait_ge(p_ready, (b - 1) * H)
                    sp.dma_start(gp[u][:], group[bass.ds(b, 1)].rearrange("b t s -> (b t) s")
                                 ).then_inc(group_loaded[u], 16)
                    sp.dma_start(mk[u][:], mask[bass.ds(b, 1)].rearrange("b t s -> (b t) s")
                                 ).then_inc(group_loaded[u], 16)

            if group is not None:
                for b in range(2):
                    sp.dma_start(gp[b][:], group[b]).then_inc(group_loaded[b], 16)
                    sp.dma_start(mk[b][:], mask[b]).then_inc(group_loaded[b], 16)
            if ctx_rows is None:
                later_batches(sp, loads)

        @block.gpsimd
        def _(pool):
            if ctx_rows is not None:
                pool.memset(chalf[:], -0.5).then_inc(zeroed, 1)
            for u in range(2):
                if narrow:
                    pool.memset(v[u][:], 0.0).then_inc(zeroed, 1)
                elif not single:
                    pool.memset(qm[u][:], 0.0).then_inc(zeroed, 1)
            if ctx_rows is not None:
                pool.wait_ge(zeroed, 1)
                pool.wait_ge(cve_done, 1)
                pool.tensor_tensor(crstd[:], cve[:], chalf[:], ALU.pow).then_inc(crstd_done, 1)

            if ctx_rows is not None:
                def latents(b, u):
                    if not isinstance(b, int) or b > 1:
                        pool.wait_ge(piece_evac, done_of(b - 2, NP, NP0))
                    pool.tensor_copy(kvT[u][:, :, S2:KEYS], xT[:, :, bass.ds(b * T, T)]
                                     ).then_inc(lat_copied, 1)

                latents(0, 0)
                latents(1, 1)
                later_batches(pool, latents)

        @block.tensor
        def _(pe):
            def piece(kind, arg, b, u, count, ring):
                ps = psP[ring]
                after(pe, piece_evac, count - 1)
                if kind == "C":
                    pe.wait_ge(cn_done, b * 3 + 3)
                    for r in range(3):
                        mm = pe.transpose(ps[:, CR * r:CR * r + CR], cn[u][:, r, P * arg:P * arg + P],
                                          ident[0:CR, 0:CR])
                elif kind == "K":
                    if ctx_rows is None:
                        pe.wait_ge(ctx_loaded[u], (b - u) * 8 + 16)
                    else:
                        if arg == 0:
                            pe.wait_ge(piece_evac, count)
                            pe.wait_ge(lat_copied, b + 1)
                    for k in range(DC):
                        mm = pe.matmul(ps[:, 0:KEYS], wks[:, k, P * arg:P * arg + P], kvT[u][:, k, :],
                                       start=(k == 0), stop=(k == DC - 1))
                elif kind == "Q":
                    for j in range(QG):
                        mq = QG * arg + j
                        for k in range(DC):
                            mm = pe.matmul(ps[:, j * T:(j + 1) * T], wqs[:, k, P * mq:P * mq + P],
                                           xT[:, k, bass.ds(b * T, T)],
                                           start=(k == 0), stop=(k == DC - 1))
                elif kind == "V":
                    (c, f) = arg
                    k0, ks = A.chunks[c]
                    for k in range(DC):
                        mm = pe.matmul(ps[0:ks, 0:VN], kvT[u][:, k, k0:k0 + ks],
                                       wvs[:, k, VN * f:VN * f + VN], start=(k == 0), stop=(k == DC - 1))
                else:
                    pe.wait_ge(o_copied, b * GROUPS + GROUPS)
                    for c in range(MC):
                        mm = pe.matmul(ps[0:T, 0:D], oT[:, c, :], wos[:, c, :],
                                       start=(c == 0), stop=(c == MC - 1))
                mm.then_inc(piece_ready, 1)

            def scores(b, u, h):
                n = b * H + h
                if h == 0:
                    pe.wait_ge(piece_evac, done_of(b, kq_end, kq_end0))
                if not single:
                    after(pe, exp_done, n - 1)
                else:
                    after(pe, exp_done, n)
                out = psS[ring2(u, h)][0:T, 0:KEYS]
                if single:
                    for c in range(MC):
                        mm = pe.matmul(out, qm[u][:, c, 0, :], kT[u][:, c, :], start=(c == 0),
                                       stop=(c == MC - 1))
                else:
                    mm = pe.matmul(out, qm[u][:, h // hq, h % hq, :], kT[u][:, h // hq, :],
                                   start=True, stop=True)
                mm.then_inc(s_ready, 1)

            def turn(b, u, h):
                n = b * H + h
                pe.wait_ge(p_ready, n + 1)
                if not single:
                    after(pe, pt_copied, n - 1)
                for c, (k0, ks) in enumerate(A.chunks):
                    mm = pe.transpose(psT[ring2(u, h)][0:ks, c * T:(c + 1) * T],
                                      prob[ring4(u, h)][:, k0:k0 + ks], ident[0:T, 0:T])
                mm.then_inc(t_ready, 1)

            def weigh(b, u, h):
                n = b * H + h
                if h == 0:
                    pe.wait_ge(piece_evac, done_of(b, NP, NP0))
                pe.wait_ge(pt_copied, n + 1)
                g = 0 if single else h // (H // 2)
                if not single and h % (H // 2) == 0:
                    after(pe, o_copied, (b - 1) * GROUPS + g + 1)
                for c, (k0, ks) in enumerate(A.chunks):
                    pt = probT[ring2(u, h)][0:ks, c, :]
                    if single:
                        mm = pe.matmul(psO[u][0:T, 0:D], pt, v[u][0:ks, c, :],
                                       start=(c == 0), stop=(c == NC - 1))
                    elif narrow:
                        mm = pe.matmul(psO[g][:, 0:T], v[u][0:ks, c, g, h % HG, :], pt,
                                       start=(c == 0 and h % HG == 0),
                                       stop=(c == NC - 1 and h % HG == HG - 1))
                    else:
                        p0 = A.width * (h % 2)
                        col = (h // 2) % (MC // 2) * T
                        mm = pe.matmul(psO[g][p0:p0 + A.width, col:col + T],
                                       v[u][0:ks, c, A.width * h:A.width * (h + 1)], pt,
                                       start=(c == 0), stop=(c == NC - 1))
                mm.then_inc(pv_done, 1)

            pe.wait_ge(w_loaded, 16 * N_W)
            after(pe, zeroed, ZEROED)
            if UNEVEN:
                pe.wait_ge(turn_cleared, 2)
            for j, (kind, arg) in enumerate(first_pieces):
                piece(kind, arg, 0, 0, j, j % 2)
            for h in range(LA):
                scores(0, 0, h)

            def run(b, u, first, last):
                for h in range(H):
                    if LA == 0:
                        scores(b, u, h)
                    elif h + LA < H:
                        scores(b, u, h + LA)
                    elif not last:
                        scores(b + 1, 1 - u, h + LA - H)
                    for j, kind, arg in steps_pieces(h, first, last):
                        count, ring = count_of(b, j, first, last), ring_of(u, j, first, last)
                        if kind == "O":
                            piece(kind, arg, b - 1, 1 - u, count, ring)
                        else:
                            piece(kind, arg, b + 1, 1 - u, count, ring)
                    turn(b, u, h)
                    if LA == 0:
                        weigh(b, u, h)
                    elif h:
                        weigh(b, u, h - 1)
                    elif not first:
                        weigh(b - 1, 1 - u, H - 1)

            in_pairs(pe, run)
            if LA:
                weigh(B - 1, 1, H - 1)
            if wo is not None:
                piece("O", 0, B - 1, 1, LAST_OUT, LAST_OUT % 2)

        @block.vector
        def _(dve):
            def evacuate(kind, arg, b, u, count, ring):
                ps = psP[ring]
                dve.wait_ge(piece_ready, count + 1)
                if kind == "C":
                    op = dve.tensor_scalar(kvT[u][:, arg, 0:S2], ps[:, 0:S2], cgb[:, 0, arg:arg + 1],
                                           cgb[:, 1, arg:arg + 1], ALU.mult, ALU.add)
                elif kind == "K":
                    if kb is not None:
                        op = dve.tensor_scalar(kT[u][:, arg, :], ps[:, 0:KEYS], kbs[:, arg:arg + 1], None,
                                               ALU.add)
                    else:
                        op = dve.tensor_copy(kT[u][:, arg, :], ps[:, 0:KEYS])
                elif kind == "Q":
                    q = ps[:, 0:QG * T].rearrange("p (m t) -> p m t", m=QG)
                    ms = slice(QG * arg, QG * arg + QG)
                    if narrow:
                        for j in range(QG):
                            if qb is not None:
                                dve.tensor_scalar(qs[:, j, :], q[:, j, :], qbs[:, j:j + 1], A.scale,
                                                  ALU.add, ALU.mult).then_inc(q_moved, 1)
                        dve.wait_ge(q_moved, b * 2 + 2)
                        for j in range(QG):
                            op = dve.tensor_tensor(
                                qm[u][:, j, :, :], qs[:, j, :].unsqueeze(1).to_broadcast([P, hq, T]),
                                headmask[:, :].unsqueeze(2).to_broadcast([P, hq, T]), ALU.mult)
                            if j < QG - 1:
                                op.then_inc(q_part, 1)
                    elif single:
                        op = dve.tensor_scalar(qm[u][:, ms, 0, :], q, A.scale, None, ALU.mult)
                    else:
                        dve.tensor_scalar(qm[u][0:64, ms, 0, :], q[0:64], A.scale, None,
                                          ALU.mult).then_inc(q_part, 1)
                        op = dve.tensor_scalar(qm[u][64:128, ms, 1, :], q[64:128], A.scale, None, ALU.mult)
                        dve.wait_ge(q_part, b * (MC // QG) + arg + 1)
                elif kind == "V":
                    (c, f) = arg
                    ks = A.chunks[c][1]
                    if narrow:
                        for g in range(MC):
                            dst = v[u][0:ks, c, g, :, :].rearrange("k h n -> k (h n)")
                            dst = diagonal(dst, HG, A.width)
                            src = ps[0:ks, P * g:P * g + P].rearrange("k (h n) -> k h n", h=HG)
                            bias = vbs[0:ks, P * g:P * g + P].rearrange("k (h n) -> k h n", h=HG)
                            op = dve.tensor_tensor(dst, src, bias, ALU.add)
                            if g < MC - 1:
                                op.then_inc(v_part, 1)
                    else:
                        op = dve.tensor_copy(v[u][0:ks, c, VN * f:VN * f + VN], ps[0:ks, 0:VN])
                else:
                    op = dve.scalar_tensor_tensor(x[:, bass.ds(b, 1), :], ps[0:T, 0:D].unsqueeze(1),
                                                  tg[0:T, gate:gate + 1], x[:, bass.ds(b, 1), :],
                                                  ALU.mult, ALU.add)
                op.then_inc(piece_evac, 1)

            def context_rows(b, u):
                for r in range(3):
                    n = b * 3 + r
                    op = dve.tensor_scalar(cn[u][:, r:r + 1, :], rows[:, bass.ds(n, 1), :],
                                           cmv[:, bass.ds(n, 1), 0:1].rearrange("p a b -> p (a b)"),
                                           crstd[:, bass.ds(n, 1)], ALU.subtract, ALU.mult)
                    op.then_inc(cn_done, 1)

            def masked(b, u):
                dve.wait_ge(group_loaded[u], (b - u) * 16 + 32)
                dve.tensor_scalar(neg[u][:], mk[u][:], -1.0, 1e9, ALU.add, ALU.mult).then_inc(neg_made, 1)

            def maximum(b, u, h):
                n, j = b * H + h, ring4(u, h)
                dve.wait_ge(s_ready, n + 1)
                src = psS[ring2(u, h)][0:T, 0:KEYS]
                if group is not None:
                    if h == 0:
                        dve.wait_ge(neg_made, b + 1)
                    dve.tensor_tensor(scored[j][:], src, neg[u][:], ALU.add).then_inc(max_raw, 1)
                    dve.wait_ge(max_raw, n + 1)
                    src = scored[j][:]
                dve.tensor_reduce(negmax[:, j:j + 1], src, AX, ALU.max, negate=True).then_inc(max_ready, 1)

            def normalize(b, u, h):
                n, j = b * H + h, ring4(u, h)
                dve.wait_ge(exp_done, n + 1)
                dve.reciprocal(inv[:, j:j + 1], total[:, j:j + 1]).then_inc(inv_done, 1)
                dve.wait_ge(inv_done, n + 1)
                if group is not None:
                    op = dve.scalar_tensor_tensor(prob[j][:], prob[j][:], inv[:, j:j + 1], gp[u][:],
                                                  ALU.mult, ALU.mult)
                else:
                    op = dve.tensor_scalar(prob[j][:], prob[j][:], inv[:, j:j + 1], None, ALU.mult)
                op.then_inc(p_ready, 1)

            if UNEVEN:
                for j in range(2):
                    dve.memset(psT[j][:], 0.0).then_inc(turn_cleared, 1)
            if ctx_rows is not None:
                for n in range(3 * B):
                    if n % 6 == 0:
                        dve.wait_ge(rows_loaded[n // 6], 16)
                    dve.bn_stats(cstats[:, n, :], rows[:, n, :]).then_inc(cstats_done, 1)
                for n in range(3 * B):
                    dve.wait_ge(cstats_done, n + 1)
                    dve.bn_aggr(cmv[:, n, :], cstats[:, n, :]).then_inc(cmv_done, 1)
                dve.wait_ge(cmv_done, 3 * B)
                dve.tensor_scalar(cve[:], cmv[:, :, 1], EPS, None, ALU.add).then_inc(cve_done, 1)
                dve.wait_ge(crstd_done, 1)
                context_rows(0, 0)
            dve.wait_ge(w_loaded, 16 * N_W)
            after(dve, zeroed, ZEROED)
            if ob is not None:
                dve.tensor_scalar(obs[:], obs[:], tg[0:T, gate:gate + 1], None,
                                  ALU.mult).then_inc(biased, 1)
                dve.wait_ge(biased, 1)
                dve.tensor_tensor(x[:], x[:], obs[:].unsqueeze(1).to_broadcast([T, B, D]),
                                  ALU.add).then_inc(biased, 1)
                dve.wait_ge(biased, 2)
            for j, (kind, arg) in enumerate(first_pieces):
                evacuate(kind, arg, 0, 0, j, j % 2)
            if group is not None:
                masked(0, 0)
            for h in range(LA):
                maximum(0, 0, h)
            if LA:
                normalize(0, 0, 0)

            def run(b, u, first, last):
                if ctx_rows is not None and not last:
                    context_rows(b + 1, 1 - u)
                if group is not None and not last:
                    masked(b + 1, 1 - u)
                for h in range(H):
                    if LA == 0:
                        maximum(b, u, h)
                    elif h + LA < H:
                        maximum(b, u, h + LA)
                    elif not last:
                        maximum(b + 1, 1 - u, h + LA - H)
                    for j, kind, arg in steps_pieces(h, first, last):
                        count, ring = count_of(b, j, first, last), ring_of(u, j, first, last)
                        if kind == "O":
                            evacuate(kind, arg, b - 1, 1 - u, count, ring)
                        else:
                            evacuate(kind, arg, b + 1, 1 - u, count, ring)
                    if LA == 0:
                        normalize(b, u, h)
                        dve.wait_ge(pv_done, b + 1)
                        dve.scalar_tensor_tensor(x[:, bass.ds(b, 1), :], psO[u][0:T, 0:D].unsqueeze(1),
                                                 tg[0:T, gate:gate + 1], x[:, bass.ds(b, 1), :],
                                                 ALU.mult, ALU.add).then_inc(o_copied, 1)
                    elif h + 1 < H:
                        normalize(b, u, h + 1)
                    elif not last:
                        normalize(b + 1, 1 - u, 0)

            in_pairs(dve, run)
            if wo is not None:
                evacuate("O", 0, B - 1, 1, LAST_OUT, LAST_OUT % 2)

        @block.scalar
        def _(act):
            def exponent(b, u, h):
                n, j = b * H + h, ring4(u, h)
                act.wait_ge(max_ready, n + 1)
                if LA:
                    after(act, t_ready, n - RP + 1)
                src = scored[j][:] if group is not None else psS[ring2(u, h)][0:T, 0:KEYS]
                act.activation(prob[j][:], src, ACT.Exp, bias=negmax[:, j:j + 1],
                               accum_out=total[:, j:j + 1]).then_inc(exp_done, 1)

            def copy_turned(b, u, h):
                n, r = b * H + h, ring2(u, h)
                act.wait_ge(t_ready, n + 1)
                if LA:
                    after(act, pv_done, n - 1)
                act.copy(probT[r][:].rearrange("k c t -> k (c t)"), psT[r][0:SZ, 0:NC * T]
                         ).then_inc(pt_copied, 1)

            def copy_out(b, g):
                act.wait_ge(pv_done, b * H + (g + 1) * (H // 2))
                act.copy(oT[:, g * (MC // 2):(g + 1) * (MC // 2), :],
                         psO[g][:, 0:MC // 2 * T].rearrange("p (m t) -> p m t", t=T)
                         ).then_inc(o_copied, 1)

            after(act, zeroed, ZEROED)
            for h in range(LA):
                exponent(0, 0, h)

            def run(b, u, first, last):
                for h in range(H):
                    if LA == 0:
                        exponent(b, u, h)
                    elif h + LA < H:
                        exponent(b, u, h + LA)
                    elif not last:
                        exponent(b + 1, 1 - u, h + LA - H)
                    copy_turned(b, u, h)
                    if LA and h == H // 2:
                        copy_out(b, 0)
                    elif LA and h == 0 and not first:
                        copy_out(b - 1, 1)

            in_pairs(act, run)
            if LA:
                copy_out(B - 1, 1)


HALF = R // 2


def columns(v):
    return v.rearrange("(c p) -> p c", p=P)


def add_bias(dve, st, bias, gate, sem):
    x, tg = st["x"], st["tanh_g"]
    dve.tensor_scalar(bias[:], bias[:], tg[0:T, gate:gate + 1], None, ALU.mult).then_inc(sem, 1)
    dve.wait_ge(sem, 1)
    dve.tensor_tensor(x[:], x[:], bias[:].unsqueeze(1).to_broadcast([T, B, D]), ALU.add).then_inc(sem, 1)
    dve.wait_ge(sem, 2)


def low_rank_ffn(nc, st, xT, io, gate=4):
    x, tg = st["x"], st["tanh_g"]
    RANK = io["L0_ffn_U1"].shape[1]
    FC = io["L0_ffn_V1"].shape[1] // P
    with ExitStack() as ctx:
        m = Memory(nc, ctx, st, "f0")
        u1 = m.sb("u1", [P, DC, RANK])
        v1 = m.sb("v1", [P, FC * P])
        b1 = m.sb("b1", [P, FC])
        u2 = m.sb("u2", [P, FC, RANK])
        v2 = m.sb("v2", [P, D])
        b2 = m.sb("b2", [T, D])
        pT = m.sb("pT", [P, R])
        qT = m.sb("qT", [P, R])
        hT = m.sb("hT", [P, FC, R])
        psA = [m.ps(f"psA{j}") for j in range(4)]
        psQ = [m.ps(f"psQ{j}") for j in range(2)]
        loaded, cleared, biased = m.sem("loaded"), m.sem("cleared"), m.sem("biased")
        p_ready, p_copied = m.sem("p_ready"), m.sem("p_copied")
        h_ready, h_done, q_ready, q_copied = m.sem("h_ready"), m.sem("h_done"), m.sem("q_ready"), m.sem("q_copied")
        y_ready, y_added = m.sem("y_ready"), m.sem("y_added")
        block = ctx.enter_context(nc.Block())

        @block.sync
        def _(sp):
            sp.dma_start(u1[:], io["L0_ffn_U1"].rearrange("(c p) r -> p c r", p=P)).then_inc(loaded, 16)
            sp.dma_start(v1[0:RANK, :], io["L0_ffn_V1"]).then_inc(loaded, 16)
            sp.dma_start(b1[:], columns(io["L0_ffn_b1"]), allow_slow_non_contiguous=True).then_inc(loaded, 16)
            sp.dma_start(u2[:], io["L0_ffn_U2"].rearrange("(c p) r -> p c r", p=P)).then_inc(loaded, 16)
            sp.dma_start(v2[0:RANK, :], io["L0_ffn_V2"]).then_inc(loaded, 16)
            sp.dma_start(b2[:], broadcast_rows(io["L0_ffn_b2"], T)).then_inc(loaded, 16)

        @block.gpsimd
        def _(pool):
            for t in (v1, v2, pT, qT):
                pool.memset(t[RANK:P, :], 0.0).then_inc(cleared, 1)

        @block.tensor
        def _(pe):
            pe.wait_ge(loaded, 96)
            pe.wait_ge(cleared, 4)
            for f in range(2):
                for k in range(DC):
                    mm = pe.matmul(psQ[f][0:RANK, 0:HALF], u1[:, k, :], xT[:, k, f * HALF:(f + 1) * HALF],
                                   start=(k == 0), stop=(k == DC - 1))
                mm.then_inc(p_ready, 1)
            for n in range(2 * FC):
                c, f = n // 2, n % 2
                pe.wait_ge(p_copied, f + 1)
                after(pe, h_done, n - 3)
                pe.matmul(psA[n % 4][:, 0:HALF], v1[:, c * P:(c + 1) * P], pT[:, f * HALF:(f + 1) * HALF],
                          start=True, stop=True).then_inc(h_ready, 1)
            for f in range(2):
                for c in range(FC):
                    pe.wait_ge(h_done, 2 * c + f + 1)
                    mm = pe.matmul(psQ[f][0:RANK, 0:HALF], u2[:, c, :], hT[:, c, f * HALF:(f + 1) * HALF],
                                   start=(c == 0), stop=(c == FC - 1))
                mm.then_inc(q_ready, 1)
            for b in range(B):
                pe.wait_ge(q_copied, b // (B // 2) + 1)
                after(pe, y_added, b - 3)
                pe.matmul(psA[b % 4][0:T, 0:D], qT[:, b * T:(b + 1) * T], v2[:],
                          start=True, stop=True).then_inc(y_ready, 1)

        @block.scalar
        def _(act):
            act.wait_ge(loaded, 96)
            for n in range(2 * FC):
                c, f = n // 2, n % 2
                act.wait_ge(h_ready, n + 1)
                act.activation(hT[:, c, f * HALF:(f + 1) * HALF], psA[n % 4][:, 0:HALF],
                               ACT.Gelu_apprx_tanh, bias=b1[:, c:c + 1]).then_inc(h_done, 1)

        @block.vector
        def _(dve):
            for f in range(2):
                dve.wait_ge(p_ready, f + 1)
                dve.tensor_copy(pT[0:RANK, f * HALF:(f + 1) * HALF], psQ[f][0:RANK, 0:HALF]).then_inc(p_copied, 1)
            dve.wait_ge(loaded, 96)
            add_bias(dve, st, b2, gate, biased)
            for f in range(2):
                dve.wait_ge(q_ready, f + 1)
                dve.tensor_copy(qT[0:RANK, f * HALF:(f + 1) * HALF], psQ[f][0:RANK, 0:HALF]).then_inc(q_copied, 1)
            for b in range(B):
                dve.wait_ge(y_ready, b + 1)
                dve.scalar_tensor_tensor(x[:, b, :], psA[b % 4][0:T, 0:D], tg[0:T, gate:gate + 1], x[:, b, :],
                                         ALU.mult, ALU.add).then_inc(y_added, 1)


def shift_ffn(nc, st, xT, io, gate=5):
    x, tg = st["x"], st["tanh_g"]
    with ExitStack() as ctx:
        m = Memory(nc, ctx, st, "f1")
        wr, wk, wv = (m.sb(n, [P, DC, D]) for n in ("wr", "wk", "wv"))
        mu = m.sb("mu", [P, 2, DC])
        rest = m.sb("rest", [P, 2, DC])
        mixed = [m.sb(f"mixed{j}", [P, DC, R]) for j in range(2)]
        relu = m.sb("relu", [P, 4, HALF])
        kT = m.sb("kT", [P, DC, R])
        r = m.sb("r", [T, B, D])
        y = m.sb("y", [T, 2, D])
        psA = [m.ps(f"psA{j}") for j in range(4)]
        psR = [m.ps(f"psR{j}") for j in range(4)]
        loaded, rest_made = m.sem("loaded"), m.sem("rest_made")
        scaled, mix_done = m.sem("scaled"), m.sem("mix_done")
        k_ready, relu_done, k_done = m.sem("k_ready"), m.sem("relu_done"), m.sem("k_done")
        r_ready, r_done, v_ready, y_made, y_added = (m.sem(n) for n in (
            "r_ready", "r_done", "v_ready", "y_made", "y_added"))
        block = ctx.enter_context(nc.Block())

        @block.sync
        def _(sp):
            for n, z in enumerate(("L1_ffn_mu_r", "L1_ffn_mu_k")):
                sp.dma_start(mu[:, n, :], columns(io[z]), allow_slow_non_contiguous=True).then_inc(loaded, 16)
            for t, z in ((wk, "L1_ffn_W_kT"), (wr, "L1_ffn_W_rT"), (wv, "L1_ffn_W_vT")):
                sp.dma_start(t[:], io[z].rearrange("(c p) n -> p c n", p=P)).then_inc(loaded, 16)

        @block.vector
        def _(dve):
            dve.wait_ge(loaded, 80)
            dve.tensor_scalar(rest[:], mu[:], -1.0, 1.0, ALU.mult, ALU.add).then_inc(rest_made, 1)
            for n, j in enumerate((1, 0)):
                for c in range(DC):
                    dve.tensor_scalar(mixed[j][:, c, :], xT[:, c, :], mu[:, j, c:c + 1], None,
                                      ALU.mult).then_inc(scaled, 1)
                dve.wait_ge(rest_made, 1)
                dve.wait_ge(scaled, 2 * n + 2)
                for c in range(DC):
                    new = mixed[j][:, c, :].rearrange("p (b t) -> p b t", t=T)[:, :, 1:T]
                    old = xT[:, c, :].rearrange("p (b t) -> p b t", t=T)[:, :, 0:T - 1]
                    dve.scalar_tensor_tensor(new, old, rest[:, j, c:c + 1], new, ALU.mult,
                                             ALU.add).then_inc(mix_done, 1)
            for n in range(4):
                c, f = n // 2, n % 2
                dve.wait_ge(relu_done, n + 1)
                dve.tensor_tensor(kT[:, c, f * HALF:(f + 1) * HALF], relu[:, n, :], relu[:, n, :],
                                  ALU.mult).then_inc(k_done, 1)
            for b in range(B):
                dve.wait_ge(r_done, b + 1)
                dve.wait_ge(v_ready, b + 1)
                dve.tensor_tensor(y[:, b % 2, :], psA[b % 4][0:T, 0:D], r[:, b, :], ALU.mult).then_inc(y_made, 1)
                dve.wait_ge(y_made, b + 1)
                dve.scalar_tensor_tensor(x[:, b, :], y[:, b % 2, :], tg[0:T, gate:gate + 1], x[:, b, :],
                                         ALU.mult, ALU.add).then_inc(y_added, 1)

        @block.tensor
        def _(pe):
            pe.wait_ge(mix_done, DC)
            for n in range(4):
                c, f = n // 2, n % 2
                for k in range(DC):
                    mm = pe.matmul(psA[n][:, 0:HALF], wk[:, k, c * P:(c + 1) * P],
                                   mixed[1][:, k, f * HALF:(f + 1) * HALF], start=(k == 0), stop=(k == DC - 1))
                mm.then_inc(k_ready, 1)
            pe.wait_ge(mix_done, 2 * DC)
            for b in range(B):
                after(pe, r_done, b - 3)
                for k in range(DC):
                    mm = pe.matmul(psR[b % 4][0:T, 0:D], mixed[0][:, k, b * T:(b + 1) * T], wr[:, k, :],
                                   start=(k == 0), stop=(k == DC - 1))
                mm.then_inc(r_ready, 1)
            pe.wait_ge(k_done, 4)
            for b in range(B):
                after(pe, y_made, b - 3)
                for k in range(DC):
                    mm = pe.matmul(psA[b % 4][0:T, 0:D], kT[:, k, b * T:(b + 1) * T], wv[:, k, :],
                                   start=(k == 0), stop=(k == DC - 1))
                mm.then_inc(v_ready, 1)

        @block.scalar
        def _(act):
            for n in range(4):
                act.wait_ge(k_ready, n + 1)
                act.activation(relu[:, n, :], psA[n][:, 0:HALF], ACT.Relu).then_inc(relu_done, 1)
            for b in range(B):
                act.wait_ge(r_ready, b + 1)
                act.activation(r[:, b, :], psR[b % 4][0:T, 0:D], ACT.Sigmoid).then_inc(r_done, 1)


def route_phase(nc, st, xT, io, route):
    E = io["L2_ffn_wgT"].shape[1]
    CAP = 30.0
    with ExitStack() as ctx:
        m = Memory(nc, ctx, st, "f2r")
        wg = m.sb("wg", [P, DC, E])
        names = ("capped", "shifted", "e", "p", "eq1", "w1", "one1", "p2", "eq2", "w2", "one2", "rev", "sel")
        z = {n: m.sb(n, [T, B, E]) for n in names}
        col = {n: m.sb("c_" + n, [T, B]) for n in ("max", "sum", "inv", "m1", "i1", "m2", "i2", "top", "itop")}
        psL = m.ps("psL")[:, 0:B * E].rearrange("p (b e) -> p b e", e=E)
        loaded, rev_made, l_ready = m.sem("loaded"), m.sem("rev_made"), m.sem("l_ready")
        capped, e_done, step = m.sem("capped"), m.sem("e_done"), m.sem("step")
        shifted = m.sem("shifted")
        block = ctx.enter_context(nc.Block())

        @block.sync
        def _(sp):
            sp.dma_start(wg[:], io["L2_ffn_wgT"].rearrange("(c p) e -> p c e", p=P)).then_inc(loaded, 16)

        @block.gpsimd
        def _(pool):
            for e in range(E):
                pool.memset(z["rev"][:, :, e:e + 1], float(E - e)).then_inc(rev_made, 1)

        @block.tensor
        def _(pe):
            pe.wait_ge(loaded, 16)
            for b in range(B):
                for k in range(DC):
                    mm = pe.matmul(psL[0:T, b, :], xT[:, k, b * T:(b + 1) * T], wg[:, k, :],
                                   start=(k == 0), stop=(k == DC - 1))
            mm.then_inc(l_ready, 1)

        @block.scalar
        def _(act):
            act.wait_ge(l_ready, 1)
            act.activation(z["capped"][:], psL[0:T, :, :], ACT.Tanh, scale=1.0 / CAP).then_inc(capped, 1)
            act.wait_ge(shifted, 1)
            act.activation(z["e"][:], z["shifted"][:], ACT.Exp, scale=CAP).then_inc(e_done, 1)

        @block.vector
        def _(dve):
            done = 0

            def wide(c):
                return c[:].unsqueeze(2).to_broadcast([T, B, E])

            dve.wait_ge(capped, 1)
            dve.tensor_reduce(col["max"][:], z["capped"][:], AX, ALU.max).then_inc(step, 1)
            dve.wait_ge(step, 1)
            dve.tensor_tensor(z["shifted"][:], z["capped"][:], wide(col["max"]), ALU.subtract).then_inc(shifted, 1)
            dve.wait_ge(e_done, 1)
            dve.tensor_reduce(col["sum"][:], z["e"][:], AX, ALU.add).then_inc(step, 1)
            dve.wait_ge(step, 2)
            dve.reciprocal(col["inv"][:], col["sum"][:]).then_inc(step, 1)
            dve.wait_ge(step, 3)
            dve.tensor_tensor(z["p"][:], z["e"][:], wide(col["inv"]), ALU.mult).then_inc(step, 1)
            dve.wait_ge(rev_made, E)
            done = 4
            for p, mx, eq, w, first, one in (("p", "m1", "eq1", "w1", "i1", "one1"),
                                             ("p2", "m2", "eq2", "w2", "i2", "one2")):
                dve.wait_ge(step, done)
                dve.tensor_reduce(col[mx][:], z[p][:], AX, ALU.max).then_inc(step, 1)
                dve.wait_ge(step, done + 1)
                dve.tensor_tensor(z[eq][:], z[p][:], wide(col[mx]), ALU.is_equal).then_inc(step, 1)
                dve.wait_ge(step, done + 2)
                dve.tensor_tensor(z[w][:], z[eq][:], z["rev"][:], ALU.mult).then_inc(step, 1)
                dve.wait_ge(step, done + 3)
                dve.tensor_reduce(col[first][:], z[w][:], AX, ALU.max).then_inc(step, 1)
                dve.wait_ge(step, done + 4)
                dve.tensor_tensor(z[one][:], z[w][:], wide(col[first]), ALU.is_equal).then_inc(step, 1)
                done += 5
                dve.wait_ge(step, done)
                if p == "p":
                    dve.scalar_tensor_tensor(z["p2"][:], z["one1"][:], -2.0, z["p"][:], ALU.mult,
                                             ALU.add).then_inc(step, 1)
                    done += 1
            dve.tensor_tensor(z["sel"][:], z["one1"][:], z["one2"][:], ALU.add).then_inc(step, 1)
            dve.tensor_tensor(col["top"][:], col["m1"][:], col["m2"][:], ALU.add).then_inc(step, 1)
            dve.wait_ge(step, done + 2)
            dve.reciprocal(col["itop"][:], col["top"][:]).then_inc(step, 1)
            dve.tensor_tensor(z["sel"][:], z["sel"][:], z["p"][:], ALU.mult).then_inc(step, 1)
            dve.wait_ge(step, done + 4)
            dve.tensor_tensor(route[:], z["sel"][:], wide(col["itop"]), ALU.mult).then_inc(step, 1)
            dve.wait_ge(step, done + 5)
            dve.tensor_scalar(route[:], route[:], st["tanh_g"][0:T, 6:7], None, ALU.mult).then_inc(step, 1)


def expert_ffn(nc, st, xT, io):
    x = st["x"]
    E, _, I = io["L2_ffn_w1T"].shape
    IC = I // P
    HB = B // 2
    UPS = 2 * IC
    SLAB = DC * I
    with ExitStack() as ctx:
        route = ctx.enter_context(nc.sbuf_tensor("f2_route", [T, B, E], F32))
        route_phase(nc, st, xT, io, route)
        m = Memory(nc, ctx, st, "f2x", words=2 * SLAB + 4 * HALF + 2)
        xs = [m.rounded(f"x_{k}", [P, DC, R]) for k in ("high", "low")]
        up_w = [[m.rounded(f"up{u}_{k}", [P, 2, DC, I]) for k in ("high", "low")] for u in range(2)]
        down_w = [[m.rounded(f"down{u}_{k}", [P, IC, D]) for k in ("high", "low")] for u in range(2)]
        hs = [[m.rounded(f"h{f}_{k}", [P, IC, HALF]) for k in ("high", "low")] for f in range(2)]
        raw = [m.sb(f"raw{j}", [P, SLAB]) for j in range(2)]
        gel = [m.sb(f"gel{j}", [P, HALF]) for j in range(2)]
        gated = [m.sb(f"gated{j}", [P, HALF]) for j in range(2)]
        spacer = m.sb("spacer", [P, 1])
        ps1 = [m.ps(f"ps1_{j}") for j in range(2)]
        ps3 = [m.ps(f"ps3_{j}") for j in range(2)]
        psY = [m.ps(f"psY{j}") for j in range(2)]
        raw_loaded = [m.sem(f"raw_loaded{j}") for j in range(2)]
        x_high, x_low, w_high, w_low = (m.sem(n) for n in ("x_high", "x_low", "w_high", "w_low"))
        up_ready, gel_done, gated_done = m.sem("up_ready"), m.sem("gel_done"), m.sem("gated_done")
        h_high, h_low = m.sem("h_high"), m.sem("h_low")
        y_ready, y_added = m.sem("y_ready"), m.sem("y_added")
        block = ctx.enter_context(nc.Block())

        def slab_parts(u, k):
            if k == 2:
                return [w[:].rearrange("p c d -> p (c d)") for w in down_w[u]]
            return [w[:, k].rearrange("p c i -> p (c i)") for w in up_w[u]]

        @block.sync
        def _(sp):
            def run(e, u, first, last):
                for k, z in enumerate(("L2_ffn_w1T", "L2_ffn_w3T", "L2_ffn_w2T")):
                    n, j = e * 3 + k, (u + k) % 2
                    after(sp, w_low, n - 1)
                    dst = raw[j].rearrange("p (c i) -> p c i", c=DC if k < 2 else IC)
                    sp.dma_start(dst, io[z][bass.ds(e, 1)].rearrange("e (c p) i -> p (e c) i", p=P)
                                 ).then_inc(raw_loaded[j], 16)

            in_pairs(sp, run)

        @block.gpsimd
        def _(pool):
            def low(e, u, k):
                n, j = e * 3 + k, (u + k) % 2
                high, rest = slab_parts(u, k)
                pool.wait_ge(w_high, n + 1)
                pool.tensor_tensor(rest, raw[j], high.bitcast(F32), ALU.subtract).then_inc(w_low, 1)

            for k in range(3):
                low(0, 0, k)

            def run(e, u, first, last):
                if not last:
                    for k in range(3):
                        low(e + 1, 1 - u, k)

            in_pairs(pool, run)

        @block.tensor
        def _(pe):
            def up(e, u, f, c):
                n = e * UPS + f * IC + c
                if c == 0 and f == 0:
                    pe.wait_ge(w_low, e * 3 + 2)
                after(pe, gated_done, n - 1)
                for k3, ps in enumerate((ps1, ps3)):
                    for k in range(DC):
                        mm = split_product(pe, ps[c % 2][:, 0:HALF],
                                           [w[:, k3, k, c * P:(c + 1) * P] for w in up_w[u]],
                                           [z[:, k, f * HALF:(f + 1) * HALF] for z in xs],
                                           start=(k == 0), stop=(k == DC - 1))
                mm.then_inc(up_ready, 1)

            def down(e, u, f, j):
                n = e * B + f * HB + j
                if j == 0:
                    pe.wait_ge(w_low, e * 3 + 3)
                    pe.wait_ge(h_low, e * UPS + (f + 1) * IC)
                pe.wait_ge(y_added, n + 1)
                for c in range(IC):
                    mm = split_product(pe, psY[j % 2][0:T, 0:D],
                                       [h[:, c, j * T:(j + 1) * T] for h in hs[f]],
                                       [w[:, c, :] for w in down_w[u]], start=(c == 0), stop=(c == IC - 1))
                mm.then_inc(y_ready, 1)

            pe.wait_ge(x_low, 1)

            def run(e, u, first, last):
                for f in range(2):
                    for c in range(IC):
                        up(e, u, f, c)
                        if c % 2 and f == 1:
                            down(e, u, 0, c // 2)
                        elif c % 2 and not first:
                            down(e - 1, 1 - u, 1, c // 2)

            in_pairs(pe, run)
            for j in range(HB):
                down(E - 1, 1, 1, j)

        @block.scalar
        def _(act):
            def split(e, u, k):
                n, j = e * 3 + k, (u + k) % 2
                act.wait_ge(raw_loaded[j], (n - j) * 8 + 16)
                if not (isinstance(e, int) and e < 2):
                    if k < 2:
                        act.wait_ge(up_ready, (e - 1) * UPS)
                    else:
                        act.wait_ge(y_ready, (e - 1) * B)
                act.copy(slab_parts(u, k)[0], raw[j]).then_inc(w_high, 1)

            def high(e, f, c):
                n = e * UPS + f * IC + c
                act.wait_ge(gated_done, n + 1)
                act.copy(hs[f][0][:, c, :], gated[c % 2]).then_inc(h_high, 1)

            act.copy(xs[0][:], xT[:]).then_inc(x_high, 1)
            for k in range(3):
                split(0, 0, k)

            def run(e, u, first, last):
                for f in range(2):
                    for c in range(IC):
                        n = e * UPS + f * IC + c
                        act.wait_ge(up_ready, n + 1)
                        act.activation(gel[c % 2], ps1[c % 2][:, 0:HALF], ACT.Gelu).then_inc(gel_done, 1)
                        if c:
                            high(e, f, c - 1)
                        elif f:
                            high(e, 0, IC - 1)
                        elif not first:
                            high(e - 1, 1, IC - 1)
                        if not last and (f, c) in ((0, 2), (0, 5), (1, 2)):
                            split(e + 1, 1 - u, ((0, 2), (0, 5), (1, 2)).index((f, c)))

            in_pairs(act, run)
            high(E - 1, 1, IC - 1)

        @block.vector
        def _(dve):
            def low(e, f, c):
                n = e * UPS + f * IC + c
                high, rest = hs[f]
                dve.wait_ge(h_high, n + 1)
                dve.tensor_tensor(rest[:, c, :], gated[c % 2], high[:, c, :].bitcast(F32),
                                  ALU.subtract).then_inc(h_low, 1)

            def add(e, f, j):
                b = f * HB + j
                dve.wait_ge(y_ready, e * B + b + 1)
                dve.scalar_tensor_tensor(x[:, b, :], psY[j % 2][0:T, 0:D], route[:, b, bass.ds(e, 1)], x[:, b, :],
                                         ALU.mult, ALU.add).then_inc(y_added, 1)

            dve.wait_ge(x_high, 1)
            dve.tensor_tensor(xs[1][:], xT[:], xs[0][:].bitcast(F32), ALU.subtract).then_inc(x_low, 1)
            dve.memset(spacer, 0.0).then_inc(y_added, 2)

            def run(e, u, first, last):
                for f in range(2):
                    for c in range(IC):
                        n = e * UPS + f * IC + c
                        after(dve, h_low, n - 1)
                        dve.wait_ge(gel_done, n + 1)
                        dve.tensor_tensor(gated[c % 2], ps3[c % 2][:, 0:HALF], gel[c % 2],
                                          ALU.mult).then_inc(gated_done, 1)
                        if c:
                            low(e, f, c - 1)
                        elif f:
                            low(e, 0, IC - 1)
                        elif not first:
                            low(e - 1, 1, IC - 1)
                        if c % 2 and f == 1:
                            add(e, 0, c // 2)
                        elif c % 2 and not first:
                            add(e - 1, 1, c // 2)

            in_pairs(dve, run)
            low(E - 1, 1, IC - 1)
            for j in range(HB):
                add(E - 1, 1, j)


def quantized_ffn(nc, st, io, gate=7):
    x, ident, tg = st["x"], st["ident"], st["tanh_g"]
    HID = io["L3_ffn_w1T"].shape[1]
    HC = HID // P
    ROUND = 1.5 * 2.0 ** 23
    with ExitStack() as ctx:
        m = Memory(nc, ctx, st, "f3")
        w1 = m.sb("w1", [P, DC * HID])
        w2 = m.sb("w2", [P, HC * D])
        q1 = m.sb("q1", [P, DC, HID], BF16)
        q2 = m.sb("q2", [P, HC, D], BF16)
        ones = m.sb("ones", [P, P])
        half = m.sb("half", [P, 2])
        identb = m.sb("identb", [P, P], BF16)
        spacer = m.sb("spacer", [T, 1])
        wsum = m.sb("wsum", [P, 2])
        wscale = m.sb("wscale", [P, 2])
        wmean = m.sb("wmean", [P, 2])
        g1, c1 = m.sb("g1", [T, D]), m.sb("c1", [T, D])
        g2, c2 = m.sb("g2", [T, HID]), m.sb("c2", [T, HID])
        b1, b2 = m.sb("b1", [T, HID]), m.sb("b2", [T, D])
        xn = m.sb("xn", [T, 2, D])
        hA = [m.sb(f"hA{u}", [T, D]) for u in range(2)]
        hB = [m.sb(f"hB{u}", [T, D], BF16) for u in range(2)]
        hT = [m.sb(f"hT{u}", [P, DC, T], BF16) for u in range(2)]
        z = [m.sb(f"z{u}", [T, HID]) for u in range(2)]
        zq = [m.sb(f"zq{u}", [T, HID], BF16) for u in range(2)]
        zT = [m.sb(f"zT{u}", [P, HC, T], BF16) for u in range(2)]
        stats = m.sb("stats", [T, 2, 4, 6])
        mv = m.sb("mv", [T, 2, 3, 2])
        ve = m.sb("ve", [T, 2, 3])
        rstd = m.sb("rstd", [T, 2, 3])
        top = m.sb("top", [T, 2, 2])
        unit = m.sb("unit", [T, 2, 2])
        qs = m.sb("qs", [T, 2, 2])
        back = m.sb("back", [T, 2, 2])
        psU = [m.ps(f"psU{j}", 2) for j in range(2)]
        psX = m.ps("psX").bitcast(BF16)[:, 0:DC * T].rearrange("p (c t) -> p c t", t=T)
        psZ = m.ps("psZ").bitcast(BF16)[:, 0:HC * T].rearrange("p (c t) -> p c t", t=T)
        psY = m.ps("psY")[:, 0:D]
        psW = m.ps("psW")[:, 0:2]
        w_loaded, v_loaded, made = m.sem("w_loaded"), m.sem("v_loaded"), m.sem("made")
        w_summed, w_total, w_step, biased = m.sem("w_summed"), m.sem("w_total"), m.sem("w_step"), m.sem("biased")
        step, ve_done, rstd_done = m.sem("step"), m.sem("ve_done"), m.sem("rstd_done")
        h_quantized, h_turned, h_copied = m.sem("h_quantized"), m.sem("h_turned"), m.sem("h_copied")
        u_ready, u_biased, gelu_done = m.sem("u_ready"), m.sem("u_biased"), m.sem("gelu_done")
        z_quantized, z_turned, z_copied = m.sem("z_quantized"), m.sem("z_turned"), m.sem("z_copied")
        y_ready, y_added, gated = m.sem("y_ready"), m.sem("y_added"), m.sem("gated")
        x_biased = m.sem("x_biased")
        block = ctx.enter_context(nc.Block())

        @block.sync
        def _(sp):
            sp.dma_start(w1[:].rearrange("p (c n) -> p c n", c=DC),
                         io["L3_ffn_w1T"].rearrange("(c p) n -> p c n", p=P)).then_inc(w_loaded, 16)
            sp.dma_start(w2[:].rearrange("p (c n) -> p c n", c=HC),
                         io["L3_ffn_w2T"].rearrange("(c p) n -> p c n", p=P)).then_inc(w_loaded, 16)
            for t, n in ((g1, "ln1_g"), (c1, "ln1_b"), (g2, "ln2_g"), (c2, "ln2_b"), (b1, "b1"), (b2, "b2")):
                sp.dma_start(t[:], broadcast_rows(io["L3_ffn_" + n], T)).then_inc(v_loaded, 16)

        @block.gpsimd
        def _(pool):
            pool.memset(ones[:], 1.0).then_inc(made, 1)
            pool.memset(half[:], -0.5).then_inc(made, 1)
            pool.tensor_copy(identb[:], ident[:]).then_inc(made, 1)
            pool.wait_ge(made, 3)

            def power(u, k, n):
                pool.wait_ge(ve_done, n)
                pool.tensor_tensor(rstd[:, u, k:k + 1], ve[:, u, k:k + 1], half[0:T, 0:1], ALU.pow
                                   ).then_inc(rstd_done, 1)

            def run(b, u, first, last):
                if not last:
                    power(1 - u, 0, b * 3 + 3)
                    power(1 - u, 1, b * 3 + 4)
                power(u, 2, b * 3 + (3 if last else 5))

            power(0, 0, 1)
            power(0, 1, 2)
            in_pairs(pool, run)

        @block.tensor
        def _(pe):
            pe.wait_ge(made, 3)
            pe.wait_ge(w_summed, 2)
            pe.matmul(psW, ones[:], wsum[:], start=True, stop=True).then_inc(w_total, 1)
            pe.wait_ge(w_step, 8)

            def first(b, u):
                pe.wait_ge(h_quantized, b + 1)
                for c in range(DC):
                    mm = pe.transpose(psX[:, c, :], hB[u][:, c * P:(c + 1) * P], identb[0:T, 0:T])
                mm.then_inc(h_turned, 1)
                pe.wait_ge(h_copied, b + 1)
                for f in range(2):
                    for k in range(DC):
                        mm = pe.matmul(psU[u][0:T, f, :], hT[u][:, k, :], q1[:, k, f * 512:(f + 1) * 512],
                                       start=(k == 0), stop=(k == DC - 1))
                mm.then_inc(u_ready, 1)

            def second(b, u):
                pe.wait_ge(z_quantized, b + 1)
                for c in range(HC):
                    mm = pe.transpose(psZ[:, c, :], zq[u][:, c * P:(c + 1) * P], identb[0:T, 0:T])
                mm.then_inc(z_turned, 1)
                pe.wait_ge(z_copied, b + 1)
                after(pe, y_added, b)
                for c in range(HC):
                    mm = pe.matmul(psY[0:T, :], zT[u][:, c, :], q2[:, c, :], start=(c == 0), stop=(c == HC - 1))
                mm.then_inc(y_ready, 1)

            def run(b, u, first_batch, last):
                if not last:
                    first(b + 1, 1 - u)
                second(b, u)

            first(0, 0)
            in_pairs(pe, run)

        @block.scalar
        def _(act):
            def copy_h(b, u):
                act.wait_ge(h_turned, b + 1)
                act.copy(hT[u][:], psX).then_inc(h_copied, 1)

            def run(b, u, first, last):
                act.wait_ge(u_biased, b + 1)
                act.activation(z[u][:], z[u][:], ACT.Gelu).then_inc(gelu_done, 1)
                if not last:
                    copy_h(b + 1, 1 - u)
                act.wait_ge(z_turned, b + 1)
                act.copy(zT[u][:], psZ).then_inc(z_copied, 1)

            copy_h(0, 0)
            in_pairs(act, run)

        @block.vector
        def _(dve):
            dve.wait_ge(w_loaded, 32)
            for j, w in enumerate((w1, w2)):
                dve.tensor_reduce(wsum[:, j:j + 1], w[:], AX, ALU.add, apply_absolute_value=True
                                  ).then_inc(w_summed, 1)
            dve.wait_ge(v_loaded, 96)
            dve.tensor_scalar(b2[:], b2[:], tg[0:T, gate:gate + 1], None, ALU.mult).then_inc(biased, 1)
            dve.wait_ge(biased, 1)
            dve.wait_ge(w_total, 1)
            dve.tensor_scalar(wmean[:], psW, 1.0 / (D * HID), 1e-5, ALU.mult, ALU.max).then_inc(w_step, 1)
            dve.wait_ge(w_step, 1)
            dve.reciprocal(wscale[:], wmean[:]).then_inc(w_step, 1)
            dve.wait_ge(w_step, 2)
            for j, w in enumerate((w1, w2)):
                dve.tensor_scalar(w[:], w[:], wscale[:, j:j + 1], ROUND, ALU.mult, ALU.add).then_inc(w_step, 1)
            dve.wait_ge(w_step, 4)
            for j, w in enumerate((w1, w2)):
                dve.tensor_scalar(w[:], w[:], -ROUND, 1.0, ALU.add, ALU.min).then_inc(w_step, 1)
            dve.wait_ge(w_step, 6)
            for w, q in ((w1, q1), (w2, q2)):
                dve.tensor_scalar(q[:].rearrange("p c n -> p (c n)"), w[:], -1.0, None, ALU.max).then_inc(w_step, 1)

            FIRST_OPS, SECOND_OPS = 13, 11

            def chain(base):
                count = [base]

                def link(op):
                    op.then_inc(step, 1)
                    count[0] = count[0] + 1
                    dve.wait_ge(step, count[0])
                return link

            def normalized(link, nth, u, k, src, slots):
                parts = src.rearrange("t (f n) -> t f n", f=len(slots))
                for j, s in enumerate(slots):
                    link(dve.bn_stats(stats[:, u, s, :], parts[:, j, :]))
                dve.memset(spacer[:], 0.0)
                link(dve.bn_aggr(mv[:, u, k, :], stats[:, u, slots[0]:slots[-1] + 1, :].rearrange("t s n -> t (s n)")))
                dve.tensor_scalar(ve[:, u, k:k + 1], mv[:, u, k, 1:2], EPS, None, ALU.add).then_inc(ve_done, 1)
                dve.wait_ge(rstd_done, nth)

            def quantize(link, u, j, src, out, sem):
                link(dve.tensor_reduce(top[:, u, j:j + 1], src, AX, ALU.max, apply_absolute_value=True))
                link(dve.tensor_scalar(unit[:, u, j:j + 1], top[:, u, j:j + 1], 1e-5, 1.0 / 127.0, ALU.max, ALU.mult))
                link(dve.reciprocal(qs[:, u, j:j + 1], unit[:, u, j:j + 1]))
                link(dve.tensor_scalar(back[:, u, j:j + 1], unit[:, u, j:j + 1], wmean[0:T, j:j + 1], None, ALU.mult))
                link(dve.tensor_scalar(src, src, qs[:, u, j:j + 1], ROUND, ALU.mult, ALU.add))
                link(dve.tensor_scalar(src, src, -ROUND, 127.0, ALU.add, ALU.min))
                dve.tensor_scalar(out, src, -128.0, None, ALU.max).then_inc(sem, 1)

            def first_half(b, u, base=None):
                link = chain(FIRST_OPS + (b - 1) * (FIRST_OPS + SECOND_OPS) if base is None else base)
                xb, xo = x[:, bass.ds(b, 1), :].rearrange("t b d -> t (b d)"), xn[:, u, :]
                nth = (b - 1) * 3 + 3 if base is None else 1
                normalized(link, nth, u, 0, xb, [0])
                link(dve.tensor_scalar(xo, xb, mv[:, u, 0, 0:1], rstd[:, u, 0:1], ALU.subtract, ALU.mult))
                normalized(link, nth + 1, u, 1, xo, [1])
                link(dve.scalar_tensor_tensor(hA[u][:], xo, mv[:, u, 1, 0:1], g1[:], ALU.subtract, ALU.mult))
                link(dve.scalar_tensor_tensor(hA[u][:], hA[u][:], rstd[:, u, 1:2], c1[:], ALU.mult, ALU.add))
                quantize(link, u, 0, hA[u][:], hB[u][:], h_quantized)

            def biased_half(b, u):
                dve.wait_ge(u_ready, b + 1)
                dve.scalar_tensor_tensor(z[u][:], psU[u][0:T, :, :].rearrange("t f n -> t (f n)"), back[:, u, 0:1],
                                         b1[:], ALU.mult, ALU.add).then_inc(u_biased, 1)
                xb = x[:, bass.ds(b, 1), :]
                dve.tensor_tensor(xb, xb, b2[:].unsqueeze(1), ALU.add).then_inc(x_biased, 1)

            def second_half(b, u, last):
                link = chain(b * (FIRST_OPS + SECOND_OPS) + FIRST_OPS + (0 if last else FIRST_OPS))
                dve.wait_ge(gelu_done, b + 1)
                normalized(link, b * 3 + (3 if last else 5), u, 2, z[u][:], [2, 3])
                link(dve.scalar_tensor_tensor(z[u][:], z[u][:], mv[:, u, 2, 0:1], g2[:], ALU.subtract, ALU.mult))
                link(dve.scalar_tensor_tensor(z[u][:], z[u][:], rstd[:, u, 2:3], c2[:], ALU.mult, ALU.add))
                quantize(link, u, 1, z[u][:], zq[u][:], z_quantized)

            def add(b, u):
                dve.wait_ge(y_ready, b + 1)
                dve.tensor_scalar(back[:, u, 1:2], back[:, u, 1:2], tg[0:T, gate:gate + 1], None,
                                  ALU.mult).then_inc(gated, 1)
                dve.wait_ge(gated, b + 1)
                dve.wait_ge(x_biased, b + 1)
                dve.scalar_tensor_tensor(x[:, bass.ds(b, 1), :], psY[0:T, :].unsqueeze(1), back[:, u, 1:2],
                                         x[:, bass.ds(b, 1), :], ALU.mult, ALU.add).then_inc(y_added, 1)

            def run(b, u, first, last):
                biased_half(b, u)
                if not first:
                    add(b - 1, 1 - u)
                if not last:
                    first_half(b + 1, 1 - u)
                second_half(b, u, last)

            first_half(0, 0, 0)
            in_pairs(dve, run)
            add(B - 1, 1)


FFN = {1: low_rank_ffn, 3: shift_ffn, 5: expert_ffn, 7: lambda nc, st, xT, io: quantized_ffn(nc, st, io)}


A0 = Shape(heads=16, width=64, keys=S2 + T, scale=0.125, look=2)
A1 = Shape(heads=1, width=256, keys=S2, scale=1.0 / 16, look=0)
A2 = Shape(heads=16, width=16, keys=S2, scale=0.25, look=2)


def start_phase(nc, st, io):
    x, ident, tg, headmask = st["x"], st["ident"], st["tanh_g"], st["headmask"]
    with ExitStack() as ctx:
        m = Memory(nc, ctx, st, "start")
        g = m.sb("g", [P, 8])
        loaded, made, done = m.sem("loaded"), m.sem("made"), m.sem("done")
        block = ctx.enter_context(nc.Block())

        @block.sync
        def _(sp):
            sp.dma_start(x[:], io["x"].rearrange("b t d -> t b d")).then_inc(loaded, 16)
            sp.dma_start(g[:, 0:4], broadcast_rows(io["g_xattn"], P)).then_inc(loaded, 16)
            sp.dma_start(g[:, 4:8], broadcast_rows(io["g_ffn"], P)).then_inc(loaded, 16)

        @block.gpsimd
        def _(pool):
            pool.memset(ident[:], 0.0).then_inc(made, 1)
            pool.memset(headmask[:], 1.0).then_inc(made, 1)
            pool.wait_ge(made, 2)
            pool.affine_select(out=ident[:], in_=ident[:], compare_op=ALU.not_equal, fill=1.0, base=0,
                               pattern=[[-1, P]], channel_multiplier=1).then_inc(made, 1)
            pool.affine_select(out=headmask[:], in_=headmask[:], compare_op=ALU.is_ge, fill=0.0, base=0,
                               pattern=[[-16, 8]], channel_multiplier=1).then_inc(made, 1)
            pool.wait_ge(made, 4)
            pool.affine_select(out=headmask[:], in_=headmask[:], compare_op=ALU.is_ge, fill=0.0, base=15,
                               pattern=[[16, 8]], channel_multiplier=-1).then_inc(made, 1)

        @block.scalar
        def _(act):
            act.wait_ge(loaded, 48)
            act.activation(tg[:], g[:], ACT.Tanh).then_inc(done, 1)


def store_phase(nc, st, out):
    with ExitStack() as ctx:
        m = Memory(nc, ctx, st, "store")
        stored = m.sem("stored")
        block = ctx.enter_context(nc.Block())

        @block.sync
        def _(sp):
            sp.dma_start(out.rearrange("b t d -> t b d"), st["x"][:]).then_inc(stored, 16)
            sp.wait_ge(stored, 16)


def flamingo_program(nc, io, out, layers=range(8)):
    with ExitStack() as ctx:
        def sb(name, shape):
            return ctx.enter_context(nc.sbuf_tensor(name, shape, F32))

        st = dict(x=sb("x", [T, B, D]), ident=sb("ident", [P, P]), tanh_g=sb("tanh_g", [P, 8]),
                  headmask=sb("headmask", [P, 8]),
                  banks=ctx.enter_context(nc.psum_tensor("banks", [P, 8, 512], F32)),
                  semaphores=[])
        xT = sb("xT", [P, DC, R])
        start_phase(nc, st, io)
        for n in layers:
            recycle_semaphores(nc, st)
            if n == 0:
                normalize_phase(nc, st, "a0", xT, rounds=2, affine=(io["L0_xattn_ln2_g"], io["L0_xattn_ln2_b"]))
                attention_phase(nc, st, "a0", A0, xT, io["L0_xattn_Wq"], io["L0_xattn_Wkv"][:, 0:A0.inner],
                                io["L0_xattn_Wkv"][:, A0.inner:2 * A0.inner], wo=io["L0_xattn_Wo"],
                                ctx_rows=io["ctx"], ctx_gb=(io["L0_xattn_ln1_g"], io["L0_xattn_ln1_b"]), gate=0)
            elif n == 2:
                normalize_phase(nc, st, "a1", xT)
                attention_phase(nc, st, "a1", A1, xT, io["L1_xattn_Wq"], io["L1_xattn_Wkv"][:, 0:D],
                                io["L1_xattn_Wkv"][:, D:2 * D], ctxT=io["ctxT"], gate=1)
            elif n == 4:
                normalize_phase(nc, st, "a2", xT)
                attention_phase(nc, st, "a2", A2, xT, io["L2_xattn_wq_k"], io["L2_xattn_wk_k"],
                                io["L2_xattn_wv_k"], wo=io["L2_xattn_wo_k"], qb=io["L2_xattn_wq_b"],
                                kb=io["L2_xattn_wk_b"], vb=io["L2_xattn_wv_b"], ob=io["L2_xattn_wo_b"],
                                ctxT=io["ctxT"], group=io["fside_BxSxS2_0"], mask=io["mask_BxSxS2_ik1"], gate=2)
            elif n == 6:
                normalize_phase(nc, st, "a3", xT)
                attention_phase(nc, st, "a3", A2, xT, io["L3_xattn_WqT"], io["L3_xattn_WkT"],
                                io["L3_xattn_WvT"], wo=io["L3_xattn_WoT"], qb=io["L3_xattn_bq"],
                                kb=io["L3_xattn_bk"], vb=io["L3_xattn_bv"], ob=io["L3_xattn_bo"],
                                ctxT=io["ctxT"], gate=3)
            else:
                if n != 7:
                    normalize_phase(nc, st, f"f{n // 2}", xT)
                FFN[n](nc, st, xT, io)
        store_phase(nc, st, out)


def laid_out(inputs):
    import numpy as np

    swap = {"L1_ffn_W_r": (1, 0), "L1_ffn_W_k": (1, 0), "L1_ffn_W_v": (1, 0),
            "L2_ffn_wg": (1, 0), "L2_ffn_w1": (0, 2, 1), "L2_ffn_w3": (0, 2, 1), "L2_ffn_w2": (0, 2, 1),
            "L3_xattn_Wq": (1, 0), "L3_xattn_Wk": (1, 0), "L3_xattn_Wv": (1, 0), "L3_xattn_Wo": (1, 0),
            "L3_ffn_w1": (1, 0), "L3_ffn_w2": (1, 0)}
    arrays = {}
    for name, a in inputs.items():
        a = np.asarray(a)
        if name == "ctx_1024":
            arrays["ctx"] = np.ascontiguousarray(a)
            arrays["ctxT"] = np.ascontiguousarray(np.transpose(a, (2, 0, 1)))
        elif name in swap:
            arrays[name + "T"] = np.ascontiguousarray(np.transpose(a, swap[name]))
        else:
            arrays[name] = np.ascontiguousarray(a)
    return arrays


def kernel(**inputs):
    import numpy as _np
    import concourse.bacc as _bacc
    from concourse import mybir as _mybir
    from concourse.bass_utils import run_bass_kernel_spmd as _run

    nc = _bacc.Bacc("TRN2", target_bir_lowering=False, num_devices=1)
    arrays = laid_out(inputs)
    io = {name: nc.dram_tensor(f"in_{name}", a.shape, _mybir.dt.from_np(a.dtype), kind="ExternalInput").ap()
          for name, a in arrays.items()}
    out = nc.dram_tensor("out_x", (B, T, D), _mybir.dt.float32, kind="ExternalOutput").ap()
    flamingo_program(nc, io, out)
    r = _run(nc, [{f"in_{name}": a for name, a in arrays.items()}], core_ids=[0])
    return r.results[0]["out_x"]
```

```python
from contextlib import ExitStack

import concourse.bass as bass
from concourse import mybir

ALU = mybir.AluOpType
ACT = mybir.ActivationFunctionType
AX = mybir.AxisListType.X
F32 = mybir.dt.float32
F32R = mybir.dt.float32r
BF16 = mybir.dt.bfloat16
I32 = mybir.dt.int32

P = 128
B = 8
T = 112
S2 = 375
D = 256
DC = D // P
R = B * T
CR = S2 // 3
EPS = 1e-5
ARENA = 47000


def after(eng, sem, count):
    if isinstance(count, int) and count <= 0:
        return
    eng.wait_ge(sem, count)


class Memory:

    def __init__(self, nc, ctx, st, phase, words=ARENA):
        self.nc, self.ctx, self.phase, self.words = nc, ctx, phase, words
        self.arena = ctx.enter_context(nc.sbuf_tensor(f"{phase}_arena", [P, words], F32)) if words else None
        self.banks = st["banks"]
        self.at, self.bank = 0, 0
        self.used = st["semaphores"]

    def sb(self, name, shape, dt=F32):
        size = 1
        for n in shape[1:]:
            size *= n
        words = size if dt != BF16 else size // 2
        view = self.arena[0:shape[0], self.at:self.at + words]
        self.at += words + words % 2
        assert self.at <= self.words, (self.phase, name, self.at)
        if dt != F32:
            view = view.bitcast(dt)
        if len(shape) > 2:
            names = "abcd"[:len(shape) - 1]
            view = view.rearrange(f"p ({' '.join(names)}) -> p {' '.join(names)}",
                                  **dict(zip(names, shape[1:])))
        return view

    def rounded(self, name, shape):
        return self.ctx.enter_context(self.nc.sbuf_tensor(f"{self.phase}_{name}", shape, F32R))

    def ps(self, name, banks=1):
        first = self.bank
        self.bank += banks
        assert self.bank <= 8
        return self.banks[:, first, :] if banks == 1 else self.banks[:, first:first + banks, :]

    def sem(self, name):
        self.used.append(self.nc.alloc_semaphore(name=f"{self.phase}_{name}"))
        return self.used[-1]


def recycle_semaphores(nc, st, most=90):
    if len(st["semaphores"]) > most:
        nc.clear_and_free_semaphores(st["semaphores"])
        nc.all_engine_barrier()
        st["semaphores"].clear()


def in_pairs(loop_engine, run):
    run(0, 0, True, False)
    with loop_engine.Fori(0, (B - 2) // 2) as i:
        run(i * 2 + 1, 1, False, False)
        run(i * 2 + 2, 0, False, False)
    run(B - 1, (B - 1) % 2, False, True)


def split_product(pe, out, stationary, moving, start, stop):
    (sh, sl), (mh, ml) = stationary, moving
    pe.matmul(out, sh, mh, start=start, stop=False)
    pe.matmul(out, sh, ml, start=False, stop=False)
    return pe.matmul(out, sl, mh, start=False, stop=stop)


def broadcast_rows(ap, rows):
    return bass.AP(tensor=ap.tensor, offset=ap.offset, ap=[[0, rows], *[list(d) for d in ap.ap]])


class Normalized:

    def __init__(self, m, st, out, banks, rounds=1, affine=None):
        self.x, self.ident, self.out = st["x"], st["ident"], out
        self.rounds, self.affine = rounds, affine
        self.stats = m.sb("n_stats", [T, B, 6])
        self.mv = m.sb("n_mv", [T, B, 2])
        self.ve, self.rstd, self.half = (m.sb(n, [T, B]) for n in ("n_ve", "n_rstd", "n_half"))
        self.xn = m.sb("n_xn", [T, B, D])
        self.banks = [ps[:, 0:4 * T].rearrange("p (b t) -> p b t", b=4) for ps in banks]
        self.gb = m.sb("n_gb", [P, 2, DC]) if affine else None
        self.half_set, self.gb_loaded = m.sem("n_half_set"), m.sem("n_gb_loaded")
        self.stats_done, self.mv_done, self.ve_done = m.sem("n_stats_done"), m.sem("n_mv_done"), m.sem("n_ve_done")
        self.rstd_done, self.xn_done = m.sem("n_rstd_done"), m.sem("n_xn_done")
        self.turned, self.evacuated = m.sem("n_turned"), m.sem("n_evacuated")

    def wait(self, eng):
        eng.wait_ge(self.evacuated, 2 * DC)

    def wait_power(self, eng):
        eng.wait_ge(self.rstd_done, self.rounds)

    def sync(self, sp):
        if self.affine:
            for n, v in enumerate(self.affine):
                sp.dma_start(self.gb[:, n, :], v.rearrange("(c p) -> p c", p=P),
                             allow_slow_non_contiguous=True).then_inc(self.gb_loaded, 16)

    def gpsimd(self, pool):
        self.gpsimd_start(pool)
        self.gpsimd_powers(pool)

    def gpsimd_start(self, pool):
        pool.memset(self.half, -0.5).then_inc(self.half_set, 1)

    def gpsimd_powers(self, pool):
        pool.wait_ge(self.half_set, 1)
        for r in range(self.rounds):
            pool.wait_ge(self.ve_done, r + 1)
            pool.tensor_tensor(self.rstd, self.ve, self.half, ALU.pow).then_inc(self.rstd_done, 1)

    def vector_statistics(self, dve, r=0):
        src = self.x if r == 0 else self.xn
        for b in range(B):
            if r:
                dve.wait_ge(self.xn_done, B * (r - 1) + b + 1)
            dve.bn_stats(self.stats[:, b, :], src[:, b, :]).then_inc(self.stats_done, 1)
        for b in range(B):
            dve.wait_ge(self.stats_done, B * r + b + 1)
            dve.bn_aggr(self.mv[:, b, :], self.stats[:, b, :]).then_inc(self.mv_done, 1)
        dve.wait_ge(self.mv_done, B * (r + 1))
        dve.tensor_scalar(self.ve, self.mv[:, :, 1], EPS, None, ALU.add).then_inc(self.ve_done, 1)

    def vector_rows(self, dve):
        for r in range(self.rounds):
            if r:
                self.vector_statistics(dve, r)
            src = self.x if r == 0 else self.xn
            dve.wait_ge(self.rstd_done, r + 1)
            for b in range(B):
                dve.tensor_scalar(self.xn[:, b, :], src[:, b, :], self.mv[:, b, 0:1], self.rstd[:, b:b + 1],
                                  ALU.subtract, ALU.mult).then_inc(self.xn_done, 1)

    def vector_output(self, dve):
        self.vector_rows(dve)
        if self.affine:
            dve.wait_ge(self.gb_loaded, 32)
        for n in range(2 * DC):
            k, c = n // 2, n % 2
            dst = self.out[:, c, 4 * k * T:4 * (k + 1) * T].rearrange("p (b t) -> p b t", b=4)
            dve.wait_ge(self.turned, n + 1)
            if self.affine:
                dve.tensor_scalar(dst, self.banks[n], self.gb[:, 0, c:c + 1], self.gb[:, 1, c:c + 1],
                                  ALU.mult, ALU.add).then_inc(self.evacuated, 1)
            else:
                dve.tensor_copy(dst, self.banks[n]).then_inc(self.evacuated, 1)

    def tensor(self, pe):
        for n in range(2 * DC):
            k, c = n // 2, n % 2
            pe.wait_ge(self.xn_done, B * (self.rounds - 1) + 4 * (k + 1))
            for j in range(4):
                mm = pe.transpose(self.banks[n][:, j, :], self.xn[:, 4 * k + j, c * P:(c + 1) * P],
                                  self.ident[0:T, 0:T])
            mm.then_inc(self.turned, 1)


class Shape:

    def __init__(self, heads, width, keys, scale, look):
        self.heads, self.scale, self.look = heads, scale, look
        self.inner = heads * width
        self.width = width
        self.keys = keys
        n = -(-keys // P)
        size = -(-keys // n)
        self.chunks = [(c * size, min(size, keys - c * size)) for c in range(n)]
        self.size = size
        self.mc = self.inner // P


def attention_phase(nc, st, phase, A, xT, wq, wk, wv, wo=None, qb=None, kb=None, vb=None, ob=None,
                    ctxT=None, ctx_rows=None, ctx_gb=None, group=None, mask=None, gate=0,
                    rounds=1, affine=None):
    x, ident, tg = st["x"], st["ident"], st["tanh_g"]
    H, LA, NC, MC = A.heads, A.look, len(A.chunks), A.mc
    KEYS, SZ = A.keys, A.size
    RP = 4 if H % 4 == 0 else 2
    narrow = A.width < 64
    single = H == 1
    HG = P // A.width if narrow else 1
    VN = min(512, A.inner)

    pieces = []
    if ctx_rows is not None:
        pieces += [("C", 0), ("C", 1)]
    pieces += [("K", m) for m in range(MC)]
    QG = min(4, MC)
    pieces += [("Q", j) for j in range(MC // QG)]
    pieces += [("V", (c, f)) for c in range(NC) for f in range(A.inner // VN)]
    first_pieces = sorted(pieces, key=lambda p: "CKVQ".index(p[0]))
    kq_end0 = len(first_pieces)
    if wo is not None:
        pieces.insert(3, ("O", 0))
    NP, NP0 = len(pieces), len(first_pieces)
    OUT = [p[0] for p in pieces].index("O") if wo is not None else None
    HAS_OUT = int(wo is not None)
    kq_end = 1 + max(j for j, p in enumerate(pieces) if p[0] in "KQ")
    start = 0 if single else 1 if ctx_rows is None else 2
    at_step = [[] for _ in range(H)]
    for j in range(NP):
        at_step[start + j * (H - LA - start) // NP].append(j)

    def count_of(b, j, first, last):
        if first:
            return NP0 + j - (HAS_OUT and j > OUT)
        return NP0 - HAS_OUT + NP * b + (0 if last else j)

    def ring_of(u, j, first, last):
        return count_of(u if not first else 0, j, first, last) % 2

    def steps_pieces(h, first, last):
        found = []
        for j in at_step[h]:
            kind, arg = pieces[j]
            if kind == "O" and first or kind != "O" and last:
                continue
            found.append((j, kind, arg))
        return found

    def done_of(b, end, end0):
        if isinstance(b, int) and b == 0:
            return end0
        return NP0 - HAS_OUT + NP * (b - 1) + end

    with ExitStack() as ctx:
        m = Memory(nc, ctx, st, phase)
        wqs = m.sb("wq", [P, DC, A.inner])
        wks = m.sb("wk", [P, DC, A.inner])
        wvs = m.sb("wv", [P, DC, A.inner])
        wos = m.sb("wo", [P, MC, D]) if wo is not None else None
        kvT = [m.sb(f"kvT{u}", [P, DC, KEYS]) for u in range(2)]
        kT = [m.sb(f"kT{u}", [P, MC, KEYS]) for u in range(2)]
        hq = H // MC if not single else 1
        qm = [m.sb(f"qm{u}", [P, MC, hq, T]) for u in range(2)]
        if narrow:
            v = [m.sb(f"v{u}", [SZ, NC, MC, HG, P]) for u in range(2)]
            qs = m.sb("qs", [P, MC, T])
        else:
            v = [m.sb(f"v{u}", [SZ, NC, A.inner]) for u in range(2)]
        prob = [m.sb(f"prob{j}", [T, KEYS]) for j in range(RP)]
        probT = [m.sb(f"probT{j}", [SZ, NC, T]) for j in range(2)]
        oT = m.sb("oT", [P, MC, T]) if wo is not None else None
        negmax = m.sb("negmax", [T, RP])
        rowmax = m.sb("rowmax", [T, RP])
        total = m.sb("total", [T, RP])
        inv = m.sb("inv", [T, RP])
        qbs = m.sb("qb", [P, MC]) if qb is not None else None
        kbs = m.sb("kb", [P, MC]) if kb is not None else None
        vbs = m.sb("vb", [P, A.inner]) if vb is not None else None
        obs = m.sb("ob", [T, D]) if ob is not None else None
        if ctx_rows is not None:
            rows = [m.sb(f"rows{u}", [CR, 3, D]) for u in range(2)]
            cn = [m.sb(f"cn{u}", [CR, 3, D]) for u in range(2)]
            cstats = [m.sb(f"cstats{u}", [CR, 3, 6]) for u in range(2)]
            cmv = [m.sb(f"cmv{u}", [CR, 3, 2]) for u in range(2)]
            cve, crstd = ([m.sb(f"{n}{u}", [CR, 3]) for u in range(2)] for n in ("cve", "crstd"))
            chalf = m.sb("chalf", [CR, 3])
            spacer = m.sb("spacer", [CR, 1])
            cgb = m.sb("cgb", [P, 2, DC])
        if group is not None:
            gp = [m.sb(f"gp{u}", [T, KEYS]) for u in range(2)]
            mk = [m.sb(f"mk{u}", [T, KEYS], I32) for u in range(2)]
            neg = [m.sb(f"neg{u}", [T, KEYS]) for u in range(2)]
            scored = [m.sb(f"scored{j}", [T, KEYS]) for j in range(RP)]
        psS = [m.ps(f"psS{j}") for j in range(2)]
        psT = [m.ps(f"psT{j}") for j in range(2)]
        psO = [m.ps(f"psO{j}") for j in range(2)]
        psP = [m.ps(f"psP{j}") for j in range(2)]

        w_loaded = {n: m.sem(f"w_{n}_loaded") for n in ("k", "q", "v", "o")}
        small_loaded, zeroed = m.sem("small_loaded"), m.sem("zeroed")
        norm = Normalized(m, st, xT, psS + psT, rounds, affine)
        ctx_loaded = [m.sem(f"ctx_loaded{u}") for u in range(2)]
        group_loaded = [m.sem(f"group_loaded{u}") for u in range(2)]
        rows_loaded = [m.sem(f"rows_loaded{u}") for u in range(2)]
        cstats_done, cmv_done, cve_done = m.sem("cstats_done"), m.sem("cmv_done"), m.sem("cve_done")
        crstd_done, cn_done, lat_copied = m.sem("crstd_done"), m.sem("cn_done"), m.sem("lat_copied")
        piece_ready, piece_evac, q_moved = m.sem("piece_ready"), m.sem("piece_evac"), m.sem("q_moved")
        s_ready, max_raw, max_ready = m.sem("s_ready"), m.sem("max_raw"), m.sem("max_ready")
        exp_done, inv_done, p_ready = m.sem("exp_done"), m.sem("inv_done"), m.sem("p_ready")
        t_ready, pt_copied, pv_done = m.sem("t_ready"), m.sem("pt_copied"), m.sem("pv_done")
        o_copied, x_updated, neg_made = m.sem("o_copied"), m.sem("x_updated"), m.sem("neg_made")
        biased, q_part, v_part = m.sem("biased"), m.sem("q_part"), m.sem("v_part")
        turn_cleared = m.sem("turn_cleared")
        headmask = st["headmask"]
        LAST_OUT = NP0 - HAS_OUT + NP * (B - 1) + 1
        ZEROED = 2 * (not single) + (ctx_rows is not None)
        padded = v if narrow else qm
        UNEVEN = A.chunks[-1][1] != SZ

        def ring2(u, h):
            return u if single else h % 2

        def ring4(u, h):
            return u if single else h % 4

        def diagonal(flat, n, width):
            dims = [list(d) for d in flat.ap]
            return bass.AP(tensor=flat.tensor, offset=flat.offset,
                           ap=[dims[0], [P + width, n], [1, width]])

        block = ctx.enter_context(nc.Block())
        SMALL = sum(z is not None for z in (qb, kb, vb, ob)) + 2 * (ctx_gb is not None)
        G = MC if not single else 1
        GROUPS = 2 if not single else 1

        def later_batches(loop_engine, run):
            run(2, 0)
            with loop_engine.Fori(0, (B - 4) // 2) as i:
                run(i * 2 + 3, 1)
                run(i * 2 + 4, 0)
            run(B - 1, 1)

        @block.sync
        def _(sp):
            def load_rows(b, u):
                sp.dma_start(rows[u], ctx_rows[bass.ds(b, 1)].rearrange("b (c p) d -> p (b c) d", p=CR)
                             ).then_inc(rows_loaded[u], 16)

            norm.sync(sp)
            if ctx_rows is not None:
                load_rows(0, 0)
                for n, z in enumerate(ctx_gb):
                    sp.dma_start(cgb[:, n, :], z.rearrange("(c p) -> p c", p=P),
                                 allow_slow_non_contiguous=True).then_inc(small_loaded, 16)
            else:
                for b in range(2):
                    sp.dma_start(kvT[b][:], ctxT[:, b].rearrange("(c p) s -> p c s", p=P)
                                 ).then_inc(ctx_loaded[b], 16)
            for z, t in ((qb, qbs), (kb, kbs)):
                if z is not None:
                    sp.dma_start(t[:], z.rearrange("(c p) -> p c", p=P),
                                 allow_slow_non_contiguous=True).then_inc(small_loaded, 16)
            if vb is not None:
                sp.dma_start(vbs[:], broadcast_rows(vb, P)).then_inc(small_loaded, 16)
            if ob is not None:
                sp.dma_start(obs[:], broadcast_rows(ob, T)).then_inc(small_loaded, 16)
            for n, t, z in (("k", wks, wk), ("v", wvs, wv), ("q", wqs, wq), ("o", wos, wo)):
                if z is not None:
                    sp.dma_start(t[:], z.rearrange("(c p) n -> p c n", p=P)).then_inc(w_loaded[n], 16)
            if ctx_rows is not None:
                load_rows(1, 1)

            def loads(b, u):
                if ctx_rows is not None:
                    sp.wait_ge(cn_done, (b - 1) * 3)
                    load_rows(b, u)
                else:
                    sp.wait_ge(piece_evac, done_of(b - 2, NP, NP0))
                    sp.dma_start(kvT[u][:], ctxT[:, bass.ds(b, 1)].rearrange(
                        "(c p) b s -> p c (b s)", p=P)).then_inc(ctx_loaded[u], 16)
                if group is not None:
                    sp.wait_ge(p_ready, (b - 1) * H)
                    sp.dma_start(gp[u][:], group[bass.ds(b, 1)].rearrange("b t s -> (b t) s")
                                 ).then_inc(group_loaded[u], 16)
                    sp.dma_start(mk[u][:], mask[bass.ds(b, 1)].rearrange("b t s -> (b t) s")
                                 ).then_inc(group_loaded[u], 16)

            if group is not None:
                for b in range(2):
                    sp.dma_start(gp[b][:], group[b]).then_inc(group_loaded[b], 16)
                    sp.dma_start(mk[b][:], mask[b]).then_inc(group_loaded[b], 16)
            later_batches(sp, loads)

        @block.gpsimd
        def _(pool):
            if ctx_rows is not None:
                pool.memset(chalf[:], -0.5).then_inc(zeroed, 1)
            if not single:
                pool.memset(padded[0], 0.0).then_inc(zeroed, 1)
                pool.wait_ge(zeroed, ZEROED - 1)
            norm.gpsimd(pool)
            if not single:
                norm.wait_power(pool)
                pool.memset(padded[1], 0.0).then_inc(zeroed, 1)
            if ctx_rows is not None:
                def latents(b, u):
                    if not isinstance(b, int) or b > 1:
                        pool.wait_ge(piece_evac, done_of(b - 2, NP, NP0))
                    pool.tensor_copy(kvT[u][:, :, S2:KEYS], xT[:, :, bass.ds(b * T, T)]
                                     ).then_inc(lat_copied, 1)

                def power(b, u):
                    pool.wait_ge(cve_done, b + 1)
                    pool.tensor_tensor(crstd[u], cve[u], chalf, ALU.pow).then_inc(crstd_done, 1)

                pool.wait_ge(zeroed, 1)
                power(0, 0)
                norm.wait(pool)
                latents(0, 0)
                latents(1, 1)
                power(1, 1)

                def later(b, u):
                    latents(b, u)
                    power(b, u)

                later_batches(pool, later)

        @block.tensor
        def _(pe):
            def piece(kind, arg, b, u, count, ring):
                ps = psP[ring]
                after(pe, piece_evac, count - 1)
                if kind == "C":
                    pe.wait_ge(cn_done, b * 3 + 3)
                    for r in range(3):
                        mm = pe.transpose(ps[:, CR * r:CR * r + CR], cn[u][:, r, P * arg:P * arg + P],
                                          ident[0:CR, 0:CR])
                elif kind == "K":
                    if ctx_rows is None:
                        pe.wait_ge(ctx_loaded[u], (b - u) * 8 + 16)
                    else:
                        if arg == 0:
                            pe.wait_ge(piece_evac, count)
                            pe.wait_ge(lat_copied, b + 1)
                    for k in range(DC):
                        mm = pe.matmul(ps[:, 0:KEYS], wks[:, k, P * arg:P * arg + P], kvT[u][:, k, :],
                                       start=(k == 0), stop=(k == DC - 1))
                elif kind == "Q":
                    for j in range(QG):
                        mq = QG * arg + j
                        for k in range(DC):
                            mm = pe.matmul(ps[:, j * T:(j + 1) * T], wqs[:, k, P * mq:P * mq + P],
                                           xT[:, k, bass.ds(b * T, T)],
                                           start=(k == 0), stop=(k == DC - 1))
                elif kind == "V":
                    (c, f) = arg
                    k0, ks = A.chunks[c]
                    for k in range(DC):
                        mm = pe.matmul(ps[0:ks, 0:VN], kvT[u][:, k, k0:k0 + ks],
                                       wvs[:, k, VN * f:VN * f + VN], start=(k == 0), stop=(k == DC - 1))
                else:
                    pe.wait_ge(o_copied, b * GROUPS + GROUPS)
                    for c in range(MC):
                        mm = pe.matmul(ps[0:T, 0:D], oT[:, c, :], wos[:, c, :],
                                       start=(c == 0), stop=(c == MC - 1))
                mm.then_inc(piece_ready, 1)

            def scores(b, u, h):
                n = b * H + h
                if h == 0:
                    pe.wait_ge(piece_evac, done_of(b, kq_end, kq_end0))
                if not single:
                    after(pe, exp_done, n - 1)
                else:
                    after(pe, exp_done, n)
                out = psS[ring2(u, h)][0:T, 0:KEYS]
                if single:
                    for c in range(MC):
                        mm = pe.matmul(out, qm[u][:, c, 0, :], kT[u][:, c, :], start=(c == 0),
                                       stop=(c == MC - 1))
                else:
                    mm = pe.matmul(out, qm[u][:, h // hq, h % hq, :], kT[u][:, h // hq, :],
                                   start=True, stop=True)
                mm.then_inc(s_ready, 1)

            def turn(b, u, h):
                n = b * H + h
                pe.wait_ge(p_ready, n + 1)
                if not single:
                    after(pe, pt_copied, n - 1)
                for c, (k0, ks) in enumerate(A.chunks):
                    mm = pe.transpose(psT[ring2(u, h)][0:ks, c * T:(c + 1) * T],
                                      prob[ring4(u, h)][:, k0:k0 + ks], ident[0:T, 0:T])
                mm.then_inc(t_ready, 1)

            def weigh(b, u, h):
                n = b * H + h
                if h == 0:
                    pe.wait_ge(piece_evac, done_of(b, NP, NP0))
                pe.wait_ge(pt_copied, n + 1)
                g = 0 if single else h // (H // 2)
                if not single and h % (H // 2) == 0:
                    after(pe, o_copied, (b - 1) * GROUPS + g + 1)
                for c, (k0, ks) in enumerate(A.chunks):
                    pt = probT[ring2(u, h)][0:ks, c, :]
                    if single:
                        mm = pe.matmul(psO[u][0:T, 0:D], pt, v[u][0:ks, c, :],
                                       start=(c == 0), stop=(c == NC - 1))
                    elif narrow:
                        mm = pe.matmul(psO[g][:, 0:T], v[u][0:ks, c, g, h % HG, :], pt,
                                       start=(c == 0 and h % HG == 0),
                                       stop=(c == NC - 1 and h % HG == HG - 1))
                    else:
                        p0 = A.width * (h % 2)
                        col = (h // 2) % (MC // 2) * T
                        mm = pe.matmul(psO[g][p0:p0 + A.width, col:col + T],
                                       v[u][0:ks, c, A.width * h:A.width * (h + 1)], pt,
                                       start=(c == 0), stop=(c == NC - 1))
                mm.then_inc(pv_done, 1)

            if UNEVEN:
                pe.wait_ge(turn_cleared, 2)
            early = 0
            if ctx_rows is None:
                early = sum(kind in "KV" for kind, arg in first_pieces)
            else:
                norm.tensor(pe)
                norm.wait(pe)
            for j, (kind, arg) in enumerate(first_pieces):
                if j == early and early:
                    norm.tensor(pe)
                    norm.wait(pe)
                if kind in "KQV" and (j == 0 or first_pieces[j - 1][0] != kind):
                    pe.wait_ge(w_loaded[kind.lower()], 16)
                piece(kind, arg, 0, 0, j, j % 2)
            if wo is not None:
                pe.wait_ge(w_loaded["o"], 16)
            after(pe, zeroed, ZEROED)
            for h in range(LA):
                scores(0, 0, h)

            def run(b, u, first, last):
                for h in range(H):
                    if LA == 0:
                        scores(b, u, h)
                    elif h + LA < H:
                        scores(b, u, h + LA)
                    elif not last:
                        scores(b + 1, 1 - u, h + LA - H)
                    for j, kind, arg in steps_pieces(h, first, last):
                        count, ring = count_of(b, j, first, last), ring_of(u, j, first, last)
                        if kind == "O":
                            piece(kind, arg, b - 1, 1 - u, count, ring)
                        else:
                            piece(kind, arg, b + 1, 1 - u, count, ring)
                    turn(b, u, h)
                    if LA == 0:
                        weigh(b, u, h)
                    elif h:
                        weigh(b, u, h - 1)
                    elif not first:
                        weigh(b - 1, 1 - u, H - 1)

            in_pairs(pe, run)
            if LA:
                weigh(B - 1, 1, H - 1)
            if wo is not None:
                piece("O", 0, B - 1, 1, LAST_OUT, LAST_OUT % 2)

        @block.vector
        def _(dve):
            def evacuate(kind, arg, b, u, count, ring):
                ps = psP[ring]
                dve.wait_ge(piece_ready, count + 1)
                if kind == "C":
                    op = dve.tensor_scalar(kvT[u][:, arg, 0:S2], ps[:, 0:S2], cgb[:, 0, arg:arg + 1],
                                           cgb[:, 1, arg:arg + 1], ALU.mult, ALU.add)
                elif kind == "K":
                    if kb is not None:
                        op = dve.tensor_scalar(kT[u][:, arg, :], ps[:, 0:KEYS], kbs[:, arg:arg + 1], None,
                                               ALU.add)
                    else:
                        op = dve.tensor_copy(kT[u][:, arg, :], ps[:, 0:KEYS])
                elif kind == "Q":
                    q = ps[:, 0:QG * T].rearrange("p (m t) -> p m t", m=QG)
                    ms = slice(QG * arg, QG * arg + QG)
                    if narrow:
                        for j in range(QG):
                            if qb is not None:
                                dve.tensor_scalar(qs[:, j, :], q[:, j, :], qbs[:, j:j + 1], A.scale,
                                                  ALU.add, ALU.mult).then_inc(q_moved, 1)
                        dve.wait_ge(q_moved, b * 2 + 2)
                        for j in range(QG):
                            op = dve.tensor_tensor(
                                qm[u][:, j, :, :], qs[:, j, :].unsqueeze(1).to_broadcast([P, hq, T]),
                                headmask[:, :].unsqueeze(2).to_broadcast([P, hq, T]), ALU.mult)
                            if j < QG - 1:
                                op.then_inc(q_part, 1)
                    elif single:
                        op = dve.tensor_scalar(qm[u][:, ms, 0, :], q, A.scale, None, ALU.mult)
                    else:
                        dve.tensor_scalar(qm[u][0:64, ms, 0, :], q[0:64], A.scale, None,
                                          ALU.mult).then_inc(q_part, 1)
                        op = dve.tensor_scalar(qm[u][64:128, ms, 1, :], q[64:128], A.scale, None, ALU.mult)
                        dve.wait_ge(q_part, b * (MC // QG) + arg + 1)
                elif kind == "V":
                    (c, f) = arg
                    ks = A.chunks[c][1]
                    if narrow:
                        for g in range(MC):
                            dst = v[u][0:ks, c, g, :, :].rearrange("k h n -> k (h n)")
                            dst = diagonal(dst, HG, A.width)
                            src = ps[0:ks, P * g:P * g + P].rearrange("k (h n) -> k h n", h=HG)
                            bias = vbs[0:ks, P * g:P * g + P].rearrange("k (h n) -> k h n", h=HG)
                            op = dve.tensor_tensor(dst, src, bias, ALU.add)
                            if g < MC - 1:
                                op.then_inc(v_part, 1)
                    else:
                        op = dve.tensor_copy(v[u][0:ks, c, VN * f:VN * f + VN], ps[0:ks, 0:VN])
                else:
                    op = dve.scalar_tensor_tensor(x[:, bass.ds(b, 1), :], ps[0:T, 0:D].unsqueeze(1),
                                                  tg[0:T, gate:gate + 1], x[:, bass.ds(b, 1), :],
                                                  ALU.mult, ALU.add)
                op.then_inc(piece_evac, 1)

            def context_statistics(b, u):
                dve.wait_ge(rows_loaded[u], (b - u) * 8 + 16)
                for r in range(3):
                    dve.bn_stats(cstats[u][:, r, :], rows[u][:, r, :]).then_inc(cstats_done, 1)
                dve.wait_ge(cstats_done, b * 3 + 3)
                dve.memset(spacer, 0.0)
                for r in range(3):
                    dve.bn_aggr(cmv[u][:, r, :], cstats[u][:, r, :]).then_inc(cmv_done, 1)
                dve.wait_ge(cmv_done, b * 3 + 3)
                dve.tensor_scalar(cve[u], cmv[u][:, :, 1], EPS, None, ALU.add).then_inc(cve_done, 1)

            def context_rows(b, u):
                dve.wait_ge(crstd_done, b + 1)
                for r in range(3):
                    dve.tensor_scalar(cn[u][:, r, :], rows[u][:, r, :], cmv[u][:, r, 0:1], crstd[u][:, r:r + 1],
                                      ALU.subtract, ALU.mult).then_inc(cn_done, 1)

            def masked(b, u):
                dve.wait_ge(group_loaded[u], (b - u) * 16 + 32)
                dve.tensor_scalar(neg[u][:], mk[u][:], -1.0, 1e9, ALU.add, ALU.mult).then_inc(neg_made, 1)

            def maximum(b, u, h):
                n, j = b * H + h, ring4(u, h)
                dve.wait_ge(s_ready, n + 1)
                src = psS[ring2(u, h)][0:T, 0:KEYS]
                if group is not None:
                    if h == 0:
                        dve.wait_ge(neg_made, b + 1)
                    dve.tensor_tensor(scored[j][:], src, neg[u][:], ALU.add).then_inc(max_raw, 1)
                    dve.wait_ge(max_raw, n + 1)
                    src = scored[j][:]
                dve.tensor_reduce(negmax[:, j:j + 1], src, AX, ALU.max, negate=True).then_inc(max_ready, 1)

            def normalize(b, u, h):
                n, j = b * H + h, ring4(u, h)
                dve.wait_ge(exp_done, n + 1)
                dve.reciprocal(inv[:, j:j + 1], total[:, j:j + 1]).then_inc(inv_done, 1)
                dve.wait_ge(inv_done, n + 1)
                if group is not None:
                    op = dve.scalar_tensor_tensor(prob[j][:], prob[j][:], inv[:, j:j + 1], gp[u][:],
                                                  ALU.mult, ALU.mult)
                else:
                    op = dve.tensor_scalar(prob[j][:], prob[j][:], inv[:, j:j + 1], None, ALU.mult)
                op.then_inc(p_ready, 1)

            if UNEVEN:
                for j in range(2):
                    dve.memset(psT[j][:], 0.0).then_inc(turn_cleared, 1)
            norm.vector_statistics(dve)
            if ctx_rows is not None:
                context_statistics(0, 0)
                norm.vector_output(dve)
                context_rows(0, 0)
            after(dve, small_loaded, 16 * SMALL)
            after(dve, zeroed, ZEROED - 1)
            early = 0 if ctx_rows is not None else sum(kind in "KV" for kind, arg in first_pieces)
            for j, (kind, arg) in enumerate(first_pieces):
                if j == early and early:
                    norm.vector_output(dve)
                evacuate(kind, arg, 0, 0, j, j % 2)
            after(dve, zeroed, ZEROED)
            if ob is not None:
                dve.tensor_scalar(obs[:], obs[:], tg[0:T, gate:gate + 1], None,
                                  ALU.mult).then_inc(biased, 1)
                dve.wait_ge(biased, 1)
                dve.tensor_tensor(x[:], x[:], obs[:].unsqueeze(1).to_broadcast([T, B, D]),
                                  ALU.add).then_inc(biased, 1)
                dve.wait_ge(biased, 2)
            if group is not None:
                masked(0, 0)
            for h in range(LA):
                maximum(0, 0, h)
            if LA:
                normalize(0, 0, 0)

            def run(b, u, first, last):
                if ctx_rows is not None and not last:
                    context_statistics(b + 1, 1 - u)
                if group is not None and not last:
                    masked(b + 1, 1 - u)
                for h in range(H):
                    if LA == 0:
                        maximum(b, u, h)
                    elif h + LA < H:
                        maximum(b, u, h + LA)
                    elif not last:
                        maximum(b + 1, 1 - u, h + LA - H)
                    if ctx_rows is not None and not last and h == 1:
                        context_rows(b + 1, 1 - u)
                    for j, kind, arg in steps_pieces(h, first, last):
                        count, ring = count_of(b, j, first, last), ring_of(u, j, first, last)
                        if kind == "O":
                            evacuate(kind, arg, b - 1, 1 - u, count, ring)
                        else:
                            evacuate(kind, arg, b + 1, 1 - u, count, ring)
                    if LA == 0:
                        normalize(b, u, h)
                        dve.wait_ge(pv_done, b + 1)
                        dve.scalar_tensor_tensor(x[:, bass.ds(b, 1), :], psO[u][0:T, 0:D].unsqueeze(1),
                                                 tg[0:T, gate:gate + 1], x[:, bass.ds(b, 1), :],
                                                 ALU.mult, ALU.add).then_inc(o_copied, 1)
                    elif h + 1 < H:
                        normalize(b, u, h + 1)
                    elif not last:
                        normalize(b + 1, 1 - u, 0)

            in_pairs(dve, run)
            if wo is not None:
                evacuate("O", 0, B - 1, 1, LAST_OUT, LAST_OUT % 2)

        @block.scalar
        def _(act):
            def exponent(b, u, h):
                n, j = b * H + h, ring4(u, h)
                act.wait_ge(max_ready, n + 1)
                if LA:
                    after(act, t_ready, n - RP + 1)
                src = scored[j][:] if group is not None else psS[ring2(u, h)][0:T, 0:KEYS]
                act.activation(prob[j][:], src, ACT.Exp, bias=negmax[:, j:j + 1],
                               accum_out=total[:, j:j + 1]).then_inc(exp_done, 1)

            def copy_turned(b, u, h):
                n, r = b * H + h, ring2(u, h)
                act.wait_ge(t_ready, n + 1)
                if LA:
                    after(act, pv_done, n - 1)
                act.copy(probT[r][:].rearrange("k c t -> k (c t)"), psT[r][0:SZ, 0:NC * T]
                         ).then_inc(pt_copied, 1)

            def copy_out(b, g):
                act.wait_ge(pv_done, b * H + (g + 1) * (H // 2))
                act.copy(oT[:, g * (MC // 2):(g + 1) * (MC // 2), :],
                         psO[g][:, 0:MC // 2 * T].rearrange("p (m t) -> p m t", t=T)
                         ).then_inc(o_copied, 1)

            for h in range(LA):
                exponent(0, 0, h)

            def run(b, u, first, last):
                for h in range(H):
                    if LA == 0:
                        exponent(b, u, h)
                    elif h + LA < H:
                        exponent(b, u, h + LA)
                    elif not last:
                        exponent(b + 1, 1 - u, h + LA - H)
                    copy_turned(b, u, h)
                    if LA and h == H // 2:
                        copy_out(b, 0)
                    elif LA and h == 0 and not first:
                        copy_out(b - 1, 1)

            in_pairs(act, run)
            if LA:
                copy_out(B - 1, 1)


HALF = R // 2


def columns(v):
    return v.rearrange("(c p) -> p c", p=P)


def add_bias(dve, st, bias, gate, sem):
    x, tg = st["x"], st["tanh_g"]
    dve.tensor_scalar(bias[:], bias[:], tg[0:T, gate:gate + 1], None, ALU.mult).then_inc(sem, 1)
    dve.wait_ge(sem, 1)
    dve.tensor_tensor(x[:], x[:], bias[:].unsqueeze(1).to_broadcast([T, B, D]), ALU.add).then_inc(sem, 1)
    dve.wait_ge(sem, 2)


def low_rank_ffn(nc, st, xT, io, gate=4):
    x, tg = st["x"], st["tanh_g"]
    RANK = io["L0_ffn_U1"].shape[1]
    FC = io["L0_ffn_V1"].shape[1] // P
    with ExitStack() as ctx:
        m = Memory(nc, ctx, st, "f0")
        u1 = m.sb("u1", [P, DC, RANK])
        v1 = m.sb("v1", [P, FC * P])
        b1 = m.sb("b1", [P, FC])
        u2 = m.sb("u2", [P, FC, RANK])
        v2 = m.sb("v2", [P, D])
        b2 = m.sb("b2", [T, D])
        pT = m.sb("pT", [P, R])
        qT = m.sb("qT", [P, R])
        hT = m.sb("hT", [P, FC, R])
        psA = [m.ps(f"psA{j}") for j in range(4)]
        psQ = [m.ps(f"psQ{j}") for j in range(2)]
        loaded, cleared, biased = m.sem("loaded"), m.sem("cleared"), m.sem("biased")
        p_ready, p_copied = m.sem("p_ready"), m.sem("p_copied")
        h_ready, h_done, q_ready, q_copied = m.sem("h_ready"), m.sem("h_done"), m.sem("q_ready"), m.sem("q_copied")
        y_ready, y_added = m.sem("y_ready"), m.sem("y_added")
        norm = Normalized(m, st, xT, psA)
        block = ctx.enter_context(nc.Block())

        @block.sync
        def _(sp):
            sp.dma_start(u1[:], io["L0_ffn_U1"].rearrange("(c p) r -> p c r", p=P)).then_inc(loaded, 16)
            sp.dma_start(v1[0:RANK, :], io["L0_ffn_V1"]).then_inc(loaded, 16)
            sp.dma_start(b1[:], columns(io["L0_ffn_b1"]), allow_slow_non_contiguous=True).then_inc(loaded, 16)
            sp.dma_start(u2[:], io["L0_ffn_U2"].rearrange("(c p) r -> p c r", p=P)).then_inc(loaded, 16)
            sp.dma_start(v2[0:RANK, :], io["L0_ffn_V2"]).then_inc(loaded, 16)
            sp.dma_start(b2[:], broadcast_rows(io["L0_ffn_b2"], T)).then_inc(loaded, 16)

        @block.gpsimd
        def _(pool):
            for t in (v1, v2, pT, qT):
                pool.memset(t[RANK:P, :], 0.0).then_inc(cleared, 1)
            pool.wait_ge(cleared, 4)
            norm.gpsimd(pool)

        @block.tensor
        def _(pe):
            pe.wait_ge(loaded, 96)
            pe.wait_ge(cleared, 4)
            norm.tensor(pe)
            norm.wait(pe)
            for f in range(2):
                for k in range(DC):
                    mm = pe.matmul(psQ[f][0:RANK, 0:HALF], u1[:, k, :], xT[:, k, f * HALF:(f + 1) * HALF],
                                   start=(k == 0), stop=(k == DC - 1))
                mm.then_inc(p_ready, 1)
            for n in range(2 * FC):
                c, f = n // 2, n % 2
                pe.wait_ge(p_copied, f + 1)
                after(pe, h_done, n - 3)
                pe.matmul(psA[n % 4][:, 0:HALF], v1[:, c * P:(c + 1) * P], pT[:, f * HALF:(f + 1) * HALF],
                          start=True, stop=True).then_inc(h_ready, 1)
            for f in range(2):
                for c in range(FC):
                    pe.wait_ge(h_done, 2 * c + f + 1)
                    mm = pe.matmul(psQ[f][0:RANK, 0:HALF], u2[:, c, :], hT[:, c, f * HALF:(f + 1) * HALF],
                                   start=(c == 0), stop=(c == FC - 1))
                mm.then_inc(q_ready, 1)
            for b in range(B):
                pe.wait_ge(q_copied, b // (B // 2) + 1)
                after(pe, y_added, b - 3)
                pe.matmul(psA[b % 4][0:T, 0:D], qT[:, b * T:(b + 1) * T], v2[:],
                          start=True, stop=True).then_inc(y_ready, 1)

        @block.scalar
        def _(act):
            act.wait_ge(loaded, 96)
            for n in range(2 * FC):
                c, f = n // 2, n % 2
                act.wait_ge(h_ready, n + 1)
                act.activation(hT[:, c, f * HALF:(f + 1) * HALF], psA[n % 4][:, 0:HALF],
                               ACT.Gelu_apprx_tanh, bias=b1[:, c:c + 1]).then_inc(h_done, 1)

        @block.vector
        def _(dve):
            norm.vector_statistics(dve)
            norm.vector_output(dve)
            for f in range(2):
                dve.wait_ge(p_ready, f + 1)
                dve.tensor_copy(pT[0:RANK, f * HALF:(f + 1) * HALF], psQ[f][0:RANK, 0:HALF]).then_inc(p_copied, 1)
            dve.wait_ge(loaded, 96)
            add_bias(dve, st, b2, gate, biased)
            for f in range(2):
                dve.wait_ge(q_ready, f + 1)
                dve.tensor_copy(qT[0:RANK, f * HALF:(f + 1) * HALF], psQ[f][0:RANK, 0:HALF]).then_inc(q_copied, 1)
            for b in range(B):
                dve.wait_ge(y_ready, b + 1)
                dve.scalar_tensor_tensor(x[:, b, :], psA[b % 4][0:T, 0:D], tg[0:T, gate:gate + 1], x[:, b, :],
                                         ALU.mult, ALU.add).then_inc(y_added, 1)


def shift_ffn(nc, st, xT, io, gate=5):
    x, tg = st["x"], st["tanh_g"]
    with ExitStack() as ctx:
        m = Memory(nc, ctx, st, "f1")
        wr, wk, wv = (m.sb(n, [P, DC, D]) for n in ("wr", "wk", "wv"))
        mu = m.sb("mu", [P, 2, DC])
        rest = m.sb("rest", [P, 2, DC])
        mixed = [m.sb(f"mixed{j}", [P, DC, R]) for j in range(2)]
        relu = m.sb("relu", [P, 4, HALF])
        kT = m.sb("kT", [P, DC, R])
        r = m.sb("r", [T, B, D])
        y = m.sb("y", [T, 2, D])
        psA = [m.ps(f"psA{j}") for j in range(4)]
        psR = [m.ps(f"psR{j}") for j in range(4)]
        loaded, rest_made = m.sem("loaded"), m.sem("rest_made")
        scaled, mix_done = m.sem("scaled"), m.sem("mix_done")
        k_ready, relu_done, k_done = m.sem("k_ready"), m.sem("relu_done"), m.sem("k_done")
        r_ready, r_done, v_ready, y_made, y_added = (m.sem(n) for n in (
            "r_ready", "r_done", "v_ready", "y_made", "y_added"))
        norm = Normalized(m, st, xT, psA)
        block = ctx.enter_context(nc.Block())

        @block.sync
        def _(sp):
            for n, z in enumerate(("L1_ffn_mu_r", "L1_ffn_mu_k")):
                sp.dma_start(mu[:, n, :], columns(io[z]), allow_slow_non_contiguous=True).then_inc(loaded, 16)
            for t, z in ((wk, "L1_ffn_W_kT"), (wr, "L1_ffn_W_rT"), (wv, "L1_ffn_W_vT")):
                sp.dma_start(t[:], io[z].rearrange("(c p) n -> p c n", p=P)).then_inc(loaded, 16)

        @block.gpsimd
        def _(pool):
            norm.gpsimd(pool)

        @block.vector
        def _(dve):
            norm.vector_statistics(dve)
            norm.vector_output(dve)
            norm.wait(dve)
            dve.wait_ge(loaded, 80)
            dve.tensor_scalar(rest[:], mu[:], -1.0, 1.0, ALU.mult, ALU.add).then_inc(rest_made, 1)
            for n, j in enumerate((1, 0)):
                for c in range(DC):
                    dve.tensor_scalar(mixed[j][:, c, :], xT[:, c, :], mu[:, j, c:c + 1], None,
                                      ALU.mult).then_inc(scaled, 1)
                dve.wait_ge(rest_made, 1)
                dve.wait_ge(scaled, 2 * n + 2)
                for c in range(DC):
                    new = mixed[j][:, c, :].rearrange("p (b t) -> p b t", t=T)[:, :, 1:T]
                    old = xT[:, c, :].rearrange("p (b t) -> p b t", t=T)[:, :, 0:T - 1]
                    dve.scalar_tensor_tensor(new, old, rest[:, j, c:c + 1], new, ALU.mult,
                                             ALU.add).then_inc(mix_done, 1)
            for n in range(4):
                c, f = n // 2, n % 2
                dve.wait_ge(relu_done, n + 1)
                dve.tensor_tensor(kT[:, c, f * HALF:(f + 1) * HALF], relu[:, n, :], relu[:, n, :],
                                  ALU.mult).then_inc(k_done, 1)
            for b in range(B):
                dve.wait_ge(r_done, b + 1)
                dve.wait_ge(v_ready, b + 1)
                dve.tensor_tensor(y[:, b % 2, :], psA[b % 4][0:T, 0:D], r[:, b, :], ALU.mult).then_inc(y_made, 1)
                dve.wait_ge(y_made, b + 1)
                dve.scalar_tensor_tensor(x[:, b, :], y[:, b % 2, :], tg[0:T, gate:gate + 1], x[:, b, :],
                                         ALU.mult, ALU.add).then_inc(y_added, 1)

        @block.tensor
        def _(pe):
            norm.tensor(pe)
            pe.wait_ge(mix_done, DC)
            for n in range(4):
                c, f = n // 2, n % 2
                for k in range(DC):
                    mm = pe.matmul(psA[n][:, 0:HALF], wk[:, k, c * P:(c + 1) * P],
                                   mixed[1][:, k, f * HALF:(f + 1) * HALF], start=(k == 0), stop=(k == DC - 1))
                mm.then_inc(k_ready, 1)
            pe.wait_ge(mix_done, 2 * DC)
            for b in range(B):
                after(pe, r_done, b - 3)
                for k in range(DC):
                    mm = pe.matmul(psR[b % 4][0:T, 0:D], mixed[0][:, k, b * T:(b + 1) * T], wr[:, k, :],
                                   start=(k == 0), stop=(k == DC - 1))
                mm.then_inc(r_ready, 1)
            pe.wait_ge(k_done, 4)
            for b in range(B):
                after(pe, y_made, b - 3)
                for k in range(DC):
                    mm = pe.matmul(psA[b % 4][0:T, 0:D], kT[:, k, b * T:(b + 1) * T], wv[:, k, :],
                                   start=(k == 0), stop=(k == DC - 1))
                mm.then_inc(v_ready, 1)

        @block.scalar
        def _(act):
            for n in range(4):
                act.wait_ge(k_ready, n + 1)
                act.activation(relu[:, n, :], psA[n][:, 0:HALF], ACT.Relu).then_inc(relu_done, 1)
            for b in range(B):
                act.wait_ge(r_ready, b + 1)
                act.activation(r[:, b, :], psR[b % 4][0:T, 0:D], ACT.Sigmoid).then_inc(r_done, 1)


def route_phase(nc, st, xT, io, route):
    E = io["L2_ffn_wgT"].shape[1]
    CAP = 30.0
    with ExitStack() as ctx:
        m = Memory(nc, ctx, st, "f2r")
        wg = m.sb("wg", [P, DC, E])
        names = ("capped", "shifted", "e", "p", "eq1", "w1", "one1", "p2", "eq2", "w2", "one2", "rev", "sel")
        z = {n: m.sb(n, [T, B, E]) for n in names}
        col = {n: m.sb("c_" + n, [T, B]) for n in ("max", "sum", "inv", "m1", "i1", "m2", "i2", "top", "itop")}
        psL = m.ps("psL")[:, 0:B * E].rearrange("p (b e) -> p b e", e=E)
        loaded, rev_made, l_ready = m.sem("loaded"), m.sem("rev_made"), m.sem("l_ready")
        capped, e_done, step = m.sem("capped"), m.sem("e_done"), m.sem("step")
        shifted = m.sem("shifted")
        norm = Normalized(m, st, xT, [m.ps(f"turn{j}") for j in range(4)])
        block = ctx.enter_context(nc.Block())

        @block.sync
        def _(sp):
            sp.dma_start(wg[:], io["L2_ffn_wgT"].rearrange("(c p) e -> p c e", p=P)).then_inc(loaded, 16)

        @block.gpsimd
        def _(pool):
            for e in range(E):
                pool.memset(z["rev"][:, :, e:e + 1], float(E - e)).then_inc(rev_made, 1)
            norm.gpsimd(pool)

        @block.tensor
        def _(pe):
            norm.tensor(pe)
            norm.wait(pe)
            pe.wait_ge(loaded, 16)
            for b in range(B):
                for k in range(DC):
                    mm = pe.matmul(psL[0:T, b, :], xT[:, k, b * T:(b + 1) * T], wg[:, k, :],
                                   start=(k == 0), stop=(k == DC - 1))
            mm.then_inc(l_ready, 1)

        @block.scalar
        def _(act):
            act.wait_ge(l_ready, 1)
            act.activation(z["capped"][:], psL[0:T, :, :], ACT.Tanh, scale=1.0 / CAP).then_inc(capped, 1)
            act.wait_ge(shifted, 1)
            act.activation(z["e"][:], z["shifted"][:], ACT.Exp, scale=CAP).then_inc(e_done, 1)

        @block.vector
        def _(dve):
            done = 0

            def wide(c):
                return c[:].unsqueeze(2).to_broadcast([T, B, E])

            norm.vector_statistics(dve)
            norm.vector_output(dve)
            dve.wait_ge(capped, 1)
            dve.tensor_reduce(col["max"][:], z["capped"][:], AX, ALU.max).then_inc(step, 1)
            dve.wait_ge(step, 1)
            dve.tensor_tensor(z["shifted"][:], z["capped"][:], wide(col["max"]), ALU.subtract).then_inc(shifted, 1)
            dve.wait_ge(e_done, 1)
            dve.tensor_reduce(col["sum"][:], z["e"][:], AX, ALU.add).then_inc(step, 1)
            dve.wait_ge(step, 2)
            dve.reciprocal(col["inv"][:], col["sum"][:]).then_inc(step, 1)
            dve.wait_ge(step, 3)
            dve.tensor_tensor(z["p"][:], z["e"][:], wide(col["inv"]), ALU.mult).then_inc(step, 1)
            dve.wait_ge(rev_made, E)
            done = 4
            for p, mx, eq, w, first, one in (("p", "m1", "eq1", "w1", "i1", "one1"),
                                             ("p2", "m2", "eq2", "w2", "i2", "one2")):
                dve.wait_ge(step, done)
                dve.tensor_reduce(col[mx][:], z[p][:], AX, ALU.max).then_inc(step, 1)
                dve.wait_ge(step, done + 1)
                dve.tensor_tensor(z[eq][:], z[p][:], wide(col[mx]), ALU.is_equal).then_inc(step, 1)
                dve.wait_ge(step, done + 2)
                dve.tensor_tensor(z[w][:], z[eq][:], z["rev"][:], ALU.mult).then_inc(step, 1)
                dve.wait_ge(step, done + 3)
                dve.tensor_reduce(col[first][:], z[w][:], AX, ALU.max).then_inc(step, 1)
                dve.wait_ge(step, done + 4)
                dve.tensor_tensor(z[one][:], z[w][:], wide(col[first]), ALU.is_equal).then_inc(step, 1)
                done += 5
                dve.wait_ge(step, done)
                if p == "p":
                    dve.scalar_tensor_tensor(z["p2"][:], z["one1"][:], -2.0, z["p"][:], ALU.mult,
                                             ALU.add).then_inc(step, 1)
                    done += 1
            dve.tensor_tensor(z["sel"][:], z["one1"][:], z["one2"][:], ALU.add).then_inc(step, 1)
            dve.tensor_tensor(col["top"][:], col["m1"][:], col["m2"][:], ALU.add).then_inc(step, 1)
            dve.wait_ge(step, done + 2)
            dve.reciprocal(col["itop"][:], col["top"][:]).then_inc(step, 1)
            dve.tensor_tensor(z["sel"][:], z["sel"][:], z["p"][:], ALU.mult).then_inc(step, 1)
            dve.wait_ge(step, done + 4)
            dve.tensor_tensor(route[:], z["sel"][:], wide(col["itop"]), ALU.mult).then_inc(step, 1)
            dve.wait_ge(step, done + 5)
            dve.tensor_scalar(route[:], route[:], st["tanh_g"][0:T, 6:7], None, ALU.mult).then_inc(step, 1)


def expert_ffn(nc, st, xT, io):
    x = st["x"]
    E, _, I = io["L2_ffn_w1T"].shape
    IC = I // P
    HB = B // 2
    UPS = 2 * IC
    SLAB = DC * I
    with ExitStack() as ctx:
        route = ctx.enter_context(nc.sbuf_tensor("f2_route", [T, B, E], F32))
        route_phase(nc, st, xT, io, route)
        m = Memory(nc, ctx, st, "f2x", words=2 * SLAB + 4 * HALF + 2)
        xs = [m.rounded(f"x_{k}", [P, DC, R]) for k in ("high", "low")]
        up_w = [[m.rounded(f"up{u}_{k}", [P, 2, DC, I]) for k in ("high", "low")] for u in range(2)]
        down_w = [[m.rounded(f"down{u}_{k}", [P, IC, D]) for k in ("high", "low")] for u in range(2)]
        hs = [[m.rounded(f"h{f}_{k}", [P, IC, HALF]) for k in ("high", "low")] for f in range(2)]
        raw = [m.sb(f"raw{j}", [P, SLAB]) for j in range(2)]
        gel = [m.sb(f"gel{j}", [P, HALF]) for j in range(2)]
        gated = [m.sb(f"gated{j}", [P, HALF]) for j in range(2)]
        spacer = m.sb("spacer", [P, 1])
        ps1 = [m.ps(f"ps1_{j}") for j in range(2)]
        ps3 = [m.ps(f"ps3_{j}") for j in range(2)]
        psY = [m.ps(f"psY{j}") for j in range(2)]
        raw_loaded = [m.sem(f"raw_loaded{j}") for j in range(2)]
        x_high, x_low, w_high, w_low = (m.sem(n) for n in ("x_high", "x_low", "w_high", "w_low"))
        up_ready, gel_done, gated_done = m.sem("up_ready"), m.sem("gel_done"), m.sem("gated_done")
        h_high, h_low = m.sem("h_high"), m.sem("h_low")
        y_ready, y_added = m.sem("y_ready"), m.sem("y_added")
        block = ctx.enter_context(nc.Block())

        def slab_parts(u, k):
            if k == 2:
                return [w[:].rearrange("p c d -> p (c d)") for w in down_w[u]]
            return [w[:, k].rearrange("p c i -> p (c i)") for w in up_w[u]]

        @block.sync
        def _(sp):
            def run(e, u, first, last):
                for k, z in enumerate(("L2_ffn_w1T", "L2_ffn_w3T", "L2_ffn_w2T")):
                    n, j = e * 3 + k, (u + k) % 2
                    after(sp, w_low, n - 1)
                    dst = raw[j].rearrange("p (c i) -> p c i", c=DC if k < 2 else IC)
                    sp.dma_start(dst, io[z][bass.ds(e, 1)].rearrange("e (c p) i -> p (e c) i", p=P)
                                 ).then_inc(raw_loaded[j], 16)

            in_pairs(sp, run)

        @block.gpsimd
        def _(pool):
            def low(e, u, k):
                n, j = e * 3 + k, (u + k) % 2
                high, rest = slab_parts(u, k)
                pool.wait_ge(w_high, n + 1)
                pool.tensor_tensor(rest, raw[j], high.bitcast(F32), ALU.subtract).then_inc(w_low, 1)

            for k in range(3):
                low(0, 0, k)

            def run(e, u, first, last):
                if not last:
                    for k in range(3):
                        low(e + 1, 1 - u, k)

            in_pairs(pool, run)

        @block.tensor
        def _(pe):
            def up(e, u, f, c):
                n = e * UPS + f * IC + c
                if c == 0 and f == 0:
                    pe.wait_ge(w_low, e * 3 + 2)
                after(pe, gated_done, n - 1)
                for k3, ps in enumerate((ps1, ps3)):
                    for k in range(DC):
                        mm = split_product(pe, ps[c % 2][:, 0:HALF],
                                           [w[:, k3, k, c * P:(c + 1) * P] for w in up_w[u]],
                                           [z[:, k, f * HALF:(f + 1) * HALF] for z in xs],
                                           start=(k == 0), stop=(k == DC - 1))
                mm.then_inc(up_ready, 1)

            def down(e, u, f, j):
                n = e * B + f * HB + j
                if j == 0:
                    pe.wait_ge(w_low, e * 3 + 3)
                    pe.wait_ge(h_low, e * UPS + (f + 1) * IC)
                pe.wait_ge(y_added, n + 1)
                for c in range(IC):
                    mm = split_product(pe, psY[j % 2][0:T, 0:D],
                                       [h[:, c, j * T:(j + 1) * T] for h in hs[f]],
                                       [w[:, c, :] for w in down_w[u]], start=(c == 0), stop=(c == IC - 1))
                mm.then_inc(y_ready, 1)

            pe.wait_ge(x_low, 1)

            def run(e, u, first, last):
                for f in range(2):
                    for c in range(IC):
                        up(e, u, f, c)
                        if c % 2 and f == 1:
                            down(e, u, 0, c // 2)
                        elif c % 2 and not first:
                            down(e - 1, 1 - u, 1, c // 2)

            in_pairs(pe, run)
            for j in range(HB):
                down(E - 1, 1, 1, j)

        @block.scalar
        def _(act):
            def split(e, u, k):
                n, j = e * 3 + k, (u + k) % 2
                act.wait_ge(raw_loaded[j], (n - j) * 8 + 16)
                if not (isinstance(e, int) and e < 2):
                    if k < 2:
                        act.wait_ge(up_ready, (e - 1) * UPS)
                    else:
                        act.wait_ge(y_ready, (e - 1) * B)
                act.copy(slab_parts(u, k)[0], raw[j]).then_inc(w_high, 1)

            def high(e, f, c):
                n = e * UPS + f * IC + c
                act.wait_ge(gated_done, n + 1)
                act.copy(hs[f][0][:, c, :], gated[c % 2]).then_inc(h_high, 1)

            act.copy(xs[0][:], xT[:]).then_inc(x_high, 1)
            for k in range(3):
                split(0, 0, k)

            def run(e, u, first, last):
                for f in range(2):
                    for c in range(IC):
                        n = e * UPS + f * IC + c
                        act.wait_ge(up_ready, n + 1)
                        act.activation(gel[c % 2], ps1[c % 2][:, 0:HALF], ACT.Gelu).then_inc(gel_done, 1)
                        if c:
                            high(e, f, c - 1)
                        elif f:
                            high(e, 0, IC - 1)
                        elif not first:
                            high(e - 1, 1, IC - 1)
                        if not last and (f, c) in ((0, 2), (0, 5), (1, 2)):
                            split(e + 1, 1 - u, ((0, 2), (0, 5), (1, 2)).index((f, c)))

            in_pairs(act, run)
            high(E - 1, 1, IC - 1)

        @block.vector
        def _(dve):
            def low(e, f, c):
                n = e * UPS + f * IC + c
                high, rest = hs[f]
                dve.wait_ge(h_high, n + 1)
                dve.tensor_tensor(rest[:, c, :], gated[c % 2], high[:, c, :].bitcast(F32),
                                  ALU.subtract).then_inc(h_low, 1)

            def add(e, f, j):
                b = f * HB + j
                dve.wait_ge(y_ready, e * B + b + 1)
                dve.scalar_tensor_tensor(x[:, b, :], psY[j % 2][0:T, 0:D], route[:, b, bass.ds(e, 1)], x[:, b, :],
                                         ALU.mult, ALU.add).then_inc(y_added, 1)

            dve.wait_ge(x_high, 1)
            dve.tensor_tensor(xs[1][:], xT[:], xs[0][:].bitcast(F32), ALU.subtract).then_inc(x_low, 1)
            dve.memset(spacer, 0.0).then_inc(y_added, 2)

            def run(e, u, first, last):
                for f in range(2):
                    for c in range(IC):
                        n = e * UPS + f * IC + c
                        after(dve, h_low, n - 1)
                        dve.wait_ge(gel_done, n + 1)
                        dve.tensor_tensor(gated[c % 2], ps3[c % 2][:, 0:HALF], gel[c % 2],
                                          ALU.mult).then_inc(gated_done, 1)
                        if c:
                            low(e, f, c - 1)
                        elif f:
                            low(e, 0, IC - 1)
                        elif not first:
                            low(e - 1, 1, IC - 1)
                        if c % 2 and f == 1:
                            add(e, 0, c // 2)
                        elif c % 2 and not first:
                            add(e - 1, 1, c // 2)

            in_pairs(dve, run)
            low(E - 1, 1, IC - 1)
            for j in range(HB):
                add(E - 1, 1, j)


def quantized_ffn(nc, st, io, gate=7):
    x, ident, tg = st["x"], st["ident"], st["tanh_g"]
    HID = io["L3_ffn_w1T"].shape[1]
    HC = HID // P
    HB = B // 2
    ROUND = 1.5 * 2.0 ** 23
    with ExitStack() as ctx:
        m = Memory(nc, ctx, st, "f3")
        w = [m.sb("w1", [P, DC * HID]), m.sb("w2", [P, HC * D])]
        q = [m.sb("q1", [P, DC * HID], BF16), m.sb("q2", [P, HC * D], BF16)]
        q1 = q[0].rearrange("p (c n) -> p c n", c=DC)
        q2 = q[1].rearrange("p (c n) -> p c n", c=HC)
        ones = m.sb("ones", [P, P])
        half = m.sb("half", [T, 1])
        shift = m.sb("shift", [P, 2])
        identb = m.sb("identb", [P, P], BF16)
        spacer = m.sb("spacer", [T, 1])
        wsum = m.sb("wsum", [P, 2])
        wmean = m.sb("wmean", [P, 2])
        wscale = m.sb("wscale", [P, 2])
        gmean = m.sb("gmean", [P, 1])
        g1, c1 = m.sb("g1", [T, D]), m.sb("c1", [T, D])
        g2, c2 = m.sb("g2", [T, HID]), m.sb("c2", [T, HID])
        b1, b2 = m.sb("b1", [T, HID]), m.sb("b2", [T, D])
        hB = m.sb("hB", [T, B, D], BF16)
        hT = m.sb("hT", [P, DC, R], BF16)
        top1, unit1, scale1, back1 = (m.sb(n + "1", [T, B]) for n in ("top", "unit", "scale", "back"))
        top2, unit2, scale2, back2 = (m.sb(n + "2", [T, 2]) for n in ("top", "unit", "scale", "back"))
        z = [m.sb(f"z{u}", [T, HID]) for u in range(2)]
        zq = [m.sb(f"zq{u}", [T, HID], BF16) for u in range(2)]
        zT = [m.sb(f"zT{u}", [P, HC, T], BF16) for u in range(2)]
        stats = m.sb("stats", [T, 2, 12])
        mv = m.sb("mv", [T, 2, 2])
        ve = m.sb("ve", [T, 2])
        rstd = m.sb("rstd", [T, 2])
        psU = [m.ps(f"psU{j}", 2) for j in range(2)]
        psX = [m.ps(f"psX{j}").bitcast(BF16)[:, 0:DC * HB * T].rearrange("p (c r) -> p c r", c=DC)
               for j in range(2)]
        psZ = m.ps("psZ").bitcast(BF16)[:, 0:HC * T].rearrange("p (c t) -> p c t", t=T)
        bank = m.ps("psY")
        psY, psW = bank[:, 0:D], bank[:, 0:2]
        w_loaded, v_loaded, made = m.sem("w_loaded"), m.sem("v_loaded"), m.sem("made")
        w_summed, w_total, w_step = m.sem("w_summed"), m.sem("w_total"), m.sem("w_step")
        w_shifted, w_clipped, w_quantized = m.sem("w_shifted"), m.sem("w_clipped"), m.sem("w_quantized")
        h_step, h_scaled, h_shifted, h_clipped = (m.sem(n) for n in ("h_step", "h_scaled", "h_shifted", "h_clipped"))
        h_quantized, h_turned, h_copied = m.sem("h_quantized"), m.sem("h_turned"), m.sem("h_copied")
        u_ready, u_biased, gelu_done = m.sem("u_ready"), m.sem("u_biased"), m.sem("gelu_done")
        step, ve_done, rstd_done = m.sem("step"), m.sem("ve_done"), m.sem("rstd_done")
        z_scaled, z_shifted, z_clipped = m.sem("z_scaled"), m.sem("z_shifted"), m.sem("z_clipped")
        z_quantized, z_turned, z_copied = m.sem("z_quantized"), m.sem("z_turned"), m.sem("z_copied")
        y_ready, y_added, x_biased = m.sem("y_ready"), m.sem("y_added"), m.sem("x_biased")
        norm = Normalized(m, st, None, [], rounds=2)
        h = norm.xn
        block = ctx.enter_context(nc.Block())

        @block.sync
        def _(sp):
            sp.dma_start(w[0].rearrange("p (c n) -> p c n", c=DC),
                         io["L3_ffn_w1T"].rearrange("(c p) n -> p c n", p=P)).then_inc(w_loaded, 16)
            sp.dma_start(w[1].rearrange("p (c n) -> p c n", c=HC),
                         io["L3_ffn_w2T"].rearrange("(c p) n -> p c n", p=P)).then_inc(w_loaded, 16)
            for t, n in ((g1, "ln1_g"), (c1, "ln1_b"), (b2, "b2"), (b1, "b1"), (g2, "ln2_g"), (c2, "ln2_b")):
                sp.dma_start(t[:], broadcast_rows(io["L3_ffn_" + n], T)).then_inc(v_loaded, 16)

        @block.gpsimd
        def _(pool):
            norm.gpsimd_start(pool)
            pool.memset(ones[:], 1.0).then_inc(made, 1)
            pool.memset(half[:], -0.5).then_inc(made, 1)
            pool.memset(shift[:, 0:1], ROUND).then_inc(made, 1)
            pool.memset(shift[:, 1:2], -ROUND).then_inc(made, 1)
            pool.tensor_copy(identb[:], ident[:]).then_inc(made, 1)
            pool.wait_ge(made, 5)
            norm.gpsimd_powers(pool)
            pool.wait_ge(v_loaded, 96)
            pool.wait_ge(norm.xn_done, B)
            pool.tensor_scalar(b2[:], b2[:], tg[0:T, gate:gate + 1], None, ALU.mult).then_inc(x_biased, 1)
            pool.wait_ge(x_biased, 1)
            pool.tensor_tensor(x[:], x[:], b2[:].unsqueeze(1).to_broadcast([T, B, D]), ALU.add
                               ).then_inc(x_biased, 1)

            def run(b, u, first, last):
                pool.wait_ge(ve_done, b + 1)
                pool.tensor_tensor(rstd[:, u:u + 1], ve[:, u:u + 1], half[:], ALU.pow).then_inc(rstd_done, 1)

            in_pairs(pool, run)

        @block.tensor
        def _(pe):
            def up(b, u):
                after(pe, u_biased, b - 1)
                for f in range(2):
                    for k in range(DC):
                        mm = pe.matmul(psU[u][0:T, f, :], hT[:, k, bass.ds(b * T, T)],
                                       q1[:, k, f * 512:(f + 1) * 512], start=(k == 0), stop=(k == DC - 1))
                mm.then_inc(u_ready, 1)

            pe.wait_ge(made, 5)
            pe.wait_ge(w_summed, 2)
            pe.matmul(psW, ones[:], wsum[:], start=True, stop=True).then_inc(w_total, 1)
            for j in range(2):
                pe.wait_ge(h_quantized, j + 1)
                for c in range(DC):
                    for i in range(HB):
                        mm = pe.transpose(psX[j][:, c, i * T:(i + 1) * T], hB[:, j * HB + i, c * P:(c + 1) * P],
                                          identb[0:T, 0:T])
                mm.then_inc(h_turned, 1)
            pe.wait_ge(w_quantized, 1)
            pe.wait_ge(h_copied, 2)
            up(0, 0)
            pe.wait_ge(w_quantized, 2)

            def run(b, u, first, last):
                if not last:
                    up(b + 1, 1 - u)
                pe.wait_ge(z_quantized, b + 1)
                for c in range(HC):
                    mm = pe.transpose(psZ[:, c, :], zq[u][:, c * P:(c + 1) * P], identb[0:T, 0:T])
                mm.then_inc(z_turned, 1)
                pe.wait_ge(z_copied, b + 1)
                after(pe, y_added, b)
                for c in range(HC):
                    mm = pe.matmul(psY[0:T, :], zT[u][:, c, :], q2[:, c, :], start=(c == 0), stop=(c == HC - 1))
                mm.then_inc(y_ready, 1)

            in_pairs(pe, run)

        @block.scalar
        def _(act):
            def integers(j):
                act.wait_ge(w_clipped, j + 1)
                act.activation(q[j], w[j], ACT.Identity, bias=shift[:, 1:2]).then_inc(w_quantized, 1)

            def gelu(b, u):
                act.wait_ge(u_biased, b + 1)
                act.activation(z[u][:], z[u][:], ACT.Gelu).then_inc(gelu_done, 1)

            act.wait_ge(w_loaded, 32)
            for j in range(2):
                act.activation(q[j], w[j], ACT.Abs, accum_out=wsum[:, j:j + 1]).then_inc(w_summed, 1)
            act.wait_ge(made, 5)
            act.wait_ge(w_step, 2)
            act.wait_ge(w_summed, 2)
            for j in range(2):
                act.activation(w[j], w[j], ACT.Identity, bias=shift[:, 0:1], scale=wscale[:, j:j + 1]
                               ).then_inc(w_shifted, 1)
            integers(0)
            act.wait_ge(h_scaled, 1)
            for b in range(B):
                act.activation(h[:, b, :], h[:, b, :], ACT.Identity, bias=shift[0:T, 0:1],
                               scale=scale1[:, b:b + 1]).then_inc(h_shifted, 1)
            for j in range(2):
                act.wait_ge(h_clipped, j + 1)
                act.activation(hB[:, j * HB:(j + 1) * HB, :], h[:, j * HB:(j + 1) * HB, :], ACT.Identity,
                               bias=shift[0:T, 1:2]).then_inc(h_quantized, 1)
                if j:
                    integers(1)
            for j in range(2):
                act.wait_ge(h_turned, j + 1)
                act.copy(hT[:, :, j * HB * T:(j + 1) * HB * T], psX[j]).then_inc(h_copied, 1)
            gelu(0, 0)

            def run(b, u, first, last):
                act.wait_ge(z_scaled, b + 1)
                act.activation(z[u][:], z[u][:], ACT.Identity, bias=shift[0:T, 0:1], scale=scale2[:, u:u + 1]
                               ).then_inc(z_shifted, 1)
                if not last:
                    gelu(b + 1, 1 - u)
                act.wait_ge(z_clipped, b + 1)
                act.activation(zq[u][:], z[u][:], ACT.Identity, bias=shift[0:T, 1:2]).then_inc(z_quantized, 1)
                act.wait_ge(z_turned, b + 1)
                act.copy(zT[u][:], psZ).then_inc(z_copied, 1)

            in_pairs(act, run)

        @block.vector
        def _(dve):
            norm.vector_statistics(dve)
            norm.vector_rows(dve)
            dve.wait_ge(w_total, 1)
            dve.tensor_scalar(wmean[:], psW, 1.0 / (D * HID), 1e-5, ALU.mult, ALU.max).then_inc(w_step, 1)
            dve.wait_ge(w_step, 1)
            dve.reciprocal(wscale[:], wmean[:]).then_inc(w_step, 1)
            dve.tensor_scalar(gmean[:], wmean[:, 1:2], tg[:, gate:gate + 1], None, ALU.mult).then_inc(w_step, 1)
            dve.wait_ge(v_loaded, 96)
            dve.wait_ge(norm.xn_done, 2 * B)
            for n, (v, op) in enumerate(((g1, ALU.mult), (c1, ALU.add))):
                dve.tensor_tensor(h[:], h[:], v[:].unsqueeze(1).to_broadcast([T, B, D]), op).then_inc(h_step, 1)
                dve.wait_ge(h_step, n + 1)
            for j in range(2):
                dve.wait_ge(w_shifted, j + 1)
                dve.tensor_scalar(w[j], w[j], ROUND + 1, ROUND - 1, ALU.min, ALU.max).then_inc(w_clipped, 1)
                if j == 0:
                    dve.tensor_reduce(top1[:], h[:], AX, ALU.max, apply_absolute_value=True).then_inc(h_step, 1)
                    dve.wait_ge(h_step, 3)
                    dve.tensor_scalar(unit1[:], top1[:], 1e-5, 1.0 / 127.0, ALU.max, ALU.mult).then_inc(h_step, 1)
                    dve.wait_ge(h_step, 4)
                    dve.reciprocal(scale1[:], unit1[:]).then_inc(h_scaled, 1)
                    dve.tensor_scalar(back1[:], unit1[:], wmean[0:T, 0:1], None, ALU.mult).then_inc(h_step, 1)
            for j in range(2):
                hh = h[:, j * HB:(j + 1) * HB, :]
                dve.wait_ge(h_shifted, HB * (j + 1))
                dve.tensor_scalar(hh, hh, ROUND + 127, ROUND - 128, ALU.min, ALU.max).then_inc(h_clipped, 1)
            dve.wait_ge(h_step, 5)
            dve.wait_ge(w_step, 3)

            STEPS = 8

            def biased(b, u):
                dve.wait_ge(u_ready, b + 1)
                after(dve, z_quantized, b - 1)
                dve.scalar_tensor_tensor(z[u][:], psU[u][0:T, :, :].rearrange("t f n -> t (f n)"),
                                         back1[:, bass.ds(b, 1)], b1[:], ALU.mult, ALU.add).then_inc(u_biased, 1)

            def scaled(b, u):
                done = b * STEPS
                zs = z[u][:]
                dve.wait_ge(gelu_done, b + 1)
                dve.bn_stats(stats[:, u, 0:6], zs[:, 0:512]).then_inc(step, 1)
                dve.bn_stats(stats[:, u, 6:12], zs[:, 512:HID]).then_inc(step, 1)
                dve.wait_ge(step, done + 2)
                dve.memset(spacer[:], 0.0)
                dve.bn_aggr(mv[:, u, :], stats[:, u, :]).then_inc(step, 1)
                dve.wait_ge(step, done + 3)
                dve.tensor_scalar(ve[:, u:u + 1], mv[:, u, 1:2], EPS, None, ALU.add).then_inc(ve_done, 1)
                dve.scalar_tensor_tensor(zs, zs, mv[:, u, 0:1], g2[:], ALU.subtract, ALU.mult).then_inc(step, 1)
                dve.wait_ge(rstd_done, b + 1)
                dve.wait_ge(step, done + 4)
                dve.scalar_tensor_tensor(zs, zs, rstd[:, u:u + 1], c2[:], ALU.mult, ALU.add).then_inc(step, 1)
                dve.wait_ge(step, done + 5)
                dve.tensor_reduce(top2[:, u:u + 1], zs, AX, ALU.max, apply_absolute_value=True).then_inc(step, 1)
                dve.wait_ge(step, done + 6)
                dve.tensor_scalar(unit2[:, u:u + 1], top2[:, u:u + 1], 1e-5, 1.0 / 127.0, ALU.max, ALU.mult
                                  ).then_inc(step, 1)
                dve.wait_ge(step, done + 7)
                dve.reciprocal(scale2[:, u:u + 1], unit2[:, u:u + 1]).then_inc(z_scaled, 1)
                dve.tensor_scalar(back2[:, u:u + 1], unit2[:, u:u + 1], gmean[0:T, :], None, ALU.mult
                                  ).then_inc(step, 1)

            def clipped(b, u):
                dve.wait_ge(z_shifted, b + 1)
                dve.tensor_scalar(z[u][:], z[u][:], ROUND + 127, ROUND - 128, ALU.min, ALU.max
                                  ).then_inc(z_clipped, 1)

            def add(b, u):
                dve.wait_ge(y_ready, b + 1)
                dve.wait_ge(step, b * STEPS + STEPS)
                dve.scalar_tensor_tensor(x[:, bass.ds(b, 1), :], psY[0:T, :].unsqueeze(1), back2[:, u:u + 1],
                                         x[:, bass.ds(b, 1), :], ALU.mult, ALU.add).then_inc(y_added, 1)

            biased(0, 0)
            dve.wait_ge(x_biased, 2)

            def run(b, u, first, last):
                scaled(b, u)
                if not last:
                    biased(b + 1, 1 - u)
                if not first:
                    add(b - 1, 1 - u)
                clipped(b, u)

            in_pairs(dve, run)
            add(B - 1, 1)


FFN = {1: low_rank_ffn, 3: shift_ffn, 5: expert_ffn, 7: lambda nc, st, xT, io: quantized_ffn(nc, st, io)}


A0 = Shape(heads=16, width=64, keys=S2 + T, scale=0.125, look=2)
A1 = Shape(heads=1, width=256, keys=S2, scale=1.0 / 16, look=0)
A2 = Shape(heads=16, width=16, keys=S2, scale=0.25, look=2)


def start_phase(nc, st, io):
    x, ident, tg, headmask = st["x"], st["ident"], st["tanh_g"], st["headmask"]
    with ExitStack() as ctx:
        m = Memory(nc, ctx, st, "start")
        g = m.sb("g", [P, 8])
        loaded, made, done = m.sem("loaded"), m.sem("made"), m.sem("done")
        block = ctx.enter_context(nc.Block())

        @block.sync
        def _(sp):
            sp.dma_start(x[:], io["x"].rearrange("b t d -> t b d")).then_inc(loaded, 16)
            sp.dma_start(g[:, 0:4], broadcast_rows(io["g_xattn"], P)).then_inc(loaded, 16)
            sp.dma_start(g[:, 4:8], broadcast_rows(io["g_ffn"], P)).then_inc(loaded, 16)

        @block.gpsimd
        def _(pool):
            pool.memset(ident[:], 0.0).then_inc(made, 1)
            pool.memset(headmask[:], 1.0).then_inc(made, 1)
            pool.wait_ge(made, 2)
            pool.affine_select(out=ident[:], in_=ident[:], compare_op=ALU.not_equal, fill=1.0, base=0,
                               pattern=[[-1, P]], channel_multiplier=1).then_inc(made, 1)
            pool.affine_select(out=headmask[:], in_=headmask[:], compare_op=ALU.is_ge, fill=0.0, base=0,
                               pattern=[[-16, 8]], channel_multiplier=1).then_inc(made, 1)
            pool.wait_ge(made, 4)
            pool.affine_select(out=headmask[:], in_=headmask[:], compare_op=ALU.is_ge, fill=0.0, base=15,
                               pattern=[[16, 8]], channel_multiplier=-1).then_inc(made, 1)

        @block.scalar
        def _(act):
            act.wait_ge(loaded, 48)
            act.activation(tg[:], g[:], ACT.Tanh).then_inc(done, 1)


def store_phase(nc, st, out):
    with ExitStack() as ctx:
        m = Memory(nc, ctx, st, "store")
        stored = m.sem("stored")
        block = ctx.enter_context(nc.Block())

        @block.sync
        def _(sp):
            sp.dma_start(out.rearrange("b t d -> t b d"), st["x"][:]).then_inc(stored, 16)
            sp.wait_ge(stored, 16)


def flamingo_program(nc, io, out, layers=range(8)):
    with ExitStack() as ctx:
        def sb(name, shape):
            return ctx.enter_context(nc.sbuf_tensor(name, shape, F32))

        st = dict(x=sb("x", [T, B, D]), ident=sb("ident", [P, P]), tanh_g=sb("tanh_g", [P, 8]),
                  headmask=sb("headmask", [P, 8]),
                  banks=ctx.enter_context(nc.psum_tensor("banks", [P, 8, 512], F32)),
                  semaphores=[])
        xT = sb("xT", [P, DC, R])
        start_phase(nc, st, io)
        for n in layers:
            recycle_semaphores(nc, st)
            if n == 0:
                attention_phase(nc, st, "a0", A0, xT, io["L0_xattn_Wq"], io["L0_xattn_Wkv"][:, 0:A0.inner],
                                io["L0_xattn_Wkv"][:, A0.inner:2 * A0.inner], wo=io["L0_xattn_Wo"],
                                ctx_rows=io["ctx"], ctx_gb=(io["L0_xattn_ln1_g"], io["L0_xattn_ln1_b"]), gate=0,
                                rounds=2, affine=(io["L0_xattn_ln2_g"], io["L0_xattn_ln2_b"]))
            elif n == 2:
                attention_phase(nc, st, "a1", A1, xT, io["L1_xattn_Wq"], io["L1_xattn_Wkv"][:, 0:D],
                                io["L1_xattn_Wkv"][:, D:2 * D], ctxT=io["ctxT"], gate=1)
            elif n == 4:
                attention_phase(nc, st, "a2", A2, xT, io["L2_xattn_wq_k"], io["L2_xattn_wk_k"],
                                io["L2_xattn_wv_k"], wo=io["L2_xattn_wo_k"], qb=io["L2_xattn_wq_b"],
                                kb=io["L2_xattn_wk_b"], vb=io["L2_xattn_wv_b"], ob=io["L2_xattn_wo_b"],
                                ctxT=io["ctxT"], group=io["fside_BxSxS2_0"], mask=io["mask_BxSxS2_ik1"], gate=2)
            elif n == 6:
                attention_phase(nc, st, "a3", A2, xT, io["L3_xattn_WqT"], io["L3_xattn_WkT"],
                                io["L3_xattn_WvT"], wo=io["L3_xattn_WoT"], qb=io["L3_xattn_bq"],
                                kb=io["L3_xattn_bk"], vb=io["L3_xattn_bv"], ob=io["L3_xattn_bo"],
                                ctxT=io["ctxT"], gate=3)
            else:
                FFN[n](nc, st, xT, io)
        store_phase(nc, st, out)


def laid_out(inputs):
    import numpy as np

    swap = {"L1_ffn_W_r": (1, 0), "L1_ffn_W_k": (1, 0), "L1_ffn_W_v": (1, 0),
            "L2_ffn_wg": (1, 0), "L2_ffn_w1": (0, 2, 1), "L2_ffn_w3": (0, 2, 1), "L2_ffn_w2": (0, 2, 1),
            "L3_xattn_Wq": (1, 0), "L3_xattn_Wk": (1, 0), "L3_xattn_Wv": (1, 0), "L3_xattn_Wo": (1, 0),
            "L3_ffn_w1": (1, 0), "L3_ffn_w2": (1, 0)}
    arrays = {}
    for name, a in inputs.items():
        a = np.asarray(a)
        if name == "ctx_1024":
            arrays["ctx"] = np.ascontiguousarray(a)
            arrays["ctxT"] = np.ascontiguousarray(np.transpose(a, (2, 0, 1)))
        elif name in swap:
            arrays[name + "T"] = np.ascontiguousarray(np.transpose(a, swap[name]))
        else:
            arrays[name] = np.ascontiguousarray(a)
    return arrays


def kernel(**inputs):
    import numpy as _np
    import concourse.bacc as _bacc
    from concourse import mybir as _mybir
    from concourse.bass_utils import run_bass_kernel_spmd as _run

    nc = _bacc.Bacc("TRN2", target_bir_lowering=False, num_devices=1)
    arrays = laid_out(inputs)
    io = {name: nc.dram_tensor(f"in_{name}", a.shape, _mybir.dt.from_np(a.dtype), kind="ExternalInput").ap()
          for name, a in arrays.items()}
    out = nc.dram_tensor("out_x", (B, T, D), _mybir.dt.float32, kind="ExternalOutput").ap()
    flamingo_program(nc, io, out)
    r = _run(nc, [{f"in_{name}": a for name, a in arrays.items()}], core_ids=[0])
    return r.results[0]["out_x"]
```

```python
from contextlib import ExitStack

import concourse.bass as bass
from concourse import mybir

ALU = mybir.AluOpType
ACT = mybir.ActivationFunctionType
AX = mybir.AxisListType.X
F32 = mybir.dt.float32
F32R = mybir.dt.float32r
BF16 = mybir.dt.bfloat16
I32 = mybir.dt.int32

P = 128
B = 8
T = 112
S2 = 375
D = 256
DC = D // P
R = B * T
CR = S2 // 3
EPS = 1e-5
LARGEST = 3.4028234663852886e38
ARENA = 47000


def after(eng, sem, count):
    if isinstance(count, int) and count <= 0:
        return
    eng.wait_ge(sem, count)


class Memory:

    def __init__(self, nc, ctx, st, phase, words=ARENA):
        self.nc, self.ctx, self.phase, self.words = nc, ctx, phase, words
        self.arena = ctx.enter_context(nc.sbuf_tensor(f"{phase}_arena", [P, words], F32)) if words else None
        self.banks = st["banks"]
        self.at, self.bank = 0, 0
        self.used = st["semaphores"]

    def sb(self, name, shape, dt=F32):
        size = 1
        for n in shape[1:]:
            size *= n
        words = size if dt != BF16 else size // 2
        view = self.arena[0:shape[0], self.at:self.at + words]
        self.at += words + words % 2
        assert self.at <= self.words, (self.phase, name, self.at)
        if dt != F32:
            view = view.bitcast(dt)
        if len(shape) > 2:
            names = "abcd"[:len(shape) - 1]
            view = view.rearrange(f"p ({' '.join(names)}) -> p {' '.join(names)}",
                                  **dict(zip(names, shape[1:])))
        return view

    def rounded(self, name, shape):
        return self.ctx.enter_context(self.nc.sbuf_tensor(f"{self.phase}_{name}", shape, F32R))

    def ps(self, name, banks=1):
        first = self.bank
        self.bank += banks
        assert self.bank <= 8
        return self.banks[:, first, :] if banks == 1 else self.banks[:, first:first + banks, :]

    def sem(self, name):
        self.used.append(self.nc.alloc_semaphore(name=f"{self.phase}_{name}"))
        return self.used[-1]


def recycle_semaphores(nc, st, most=90):
    if len(st["semaphores"]) > most:
        nc.clear_and_free_semaphores(st["semaphores"])
        nc.all_engine_barrier()
        st["semaphores"].clear()


def in_pairs(loop_engine, run):
    run(0, 0, True, False)
    with loop_engine.Fori(0, (B - 2) // 2) as i:
        run(i * 2 + 1, 1, False, False)
        run(i * 2 + 2, 0, False, False)
    run(B - 1, (B - 1) % 2, False, True)


def split_product(pe, out, stationary, moving, start, stop):
    (sh, sl), (mh, ml) = stationary, moving
    pe.matmul(out, sh, mh, start=start, stop=False)
    pe.matmul(out, sh, ml, start=False, stop=False)
    return pe.matmul(out, sl, mh, start=False, stop=stop)


def broadcast_rows(ap, rows):
    return bass.AP(tensor=ap.tensor, offset=ap.offset, ap=[[0, rows], *[list(d) for d in ap.ap]])


class Normalized:

    def __init__(self, m, st, out, banks, rounds=1, affine=None, place=None):
        self.x, self.ident, self.out = st["x"], st["ident"], out
        self.rounds, self.affine = rounds, affine
        self.stats = m.sb("n_stats", [T, B, 6])
        self.mv = m.sb("n_mv", [T, B, 2])
        self.ve, self.rstd, self.half = (m.sb(n, [T, B]) for n in ("n_ve", "n_rstd", "n_half"))
        self.xn = place if place is not None else m.sb("n_xn", [T, B, D])
        self.held = self.xn.shape[1]
        self.banks = [ps[:, 0:4 * T].rearrange("p (b t) -> p b t", b=4) for ps in banks]
        self.gb = m.sb("n_gb", [P, 2, DC]) if affine else None
        self.half_set, self.gb_loaded = m.sem("n_half_set"), m.sem("n_gb_loaded")
        self.stats_done, self.mv_done, self.ve_done = m.sem("n_stats_done"), m.sem("n_mv_done"), m.sem("n_ve_done")
        self.rstd_done, self.xn_done = m.sem("n_rstd_done"), m.sem("n_xn_done")
        self.turned, self.evacuated = m.sem("n_turned"), m.sem("n_evacuated")

    def wait(self, eng):
        eng.wait_ge(self.evacuated, 2 * DC)

    def sync(self, sp):
        if self.affine:
            for n, v in enumerate(self.affine):
                sp.dma_start(self.gb[:, n, :], v.rearrange("(c p) -> p c", p=P),
                             allow_slow_non_contiguous=True).then_inc(self.gb_loaded, 16)

    def gpsimd(self, pool):
        self.gpsimd_start(pool)
        for r in range(self.rounds):
            self.gpsimd_power(pool, r)

    def gpsimd_start(self, pool):
        pool.memset(self.half, -0.5).then_inc(self.half_set, 1)

    def gpsimd_power(self, pool, r):
        pool.wait_ge(self.half_set, 1)
        pool.wait_ge(self.ve_done, r + 1)
        pool.tensor_tensor(self.rstd, self.ve, self.half, ALU.pow).then_inc(self.rstd_done, 1)

    def vector_statistics(self, dve, r=0):
        src = self.x if r == 0 else self.xn
        for b in range(B):
            if r:
                dve.wait_ge(self.xn_done, B * (r - 1) + b + 1)
            dve.bn_stats(self.stats[:, b, :], src[:, b, :]).then_inc(self.stats_done, 1)
        for b in range(B):
            dve.wait_ge(self.stats_done, B * r + b + 1)
            dve.bn_aggr(self.mv[:, b, :], self.stats[:, b, :]).then_inc(self.mv_done, 1)
        dve.wait_ge(self.mv_done, B * (r + 1))
        dve.tensor_scalar(self.ve, self.mv[:, :, 1], EPS, None, ALU.add).then_inc(self.ve_done, 1)

    def vector_rows(self, dve):
        for r in range(self.rounds):
            if r:
                self.vector_statistics(dve, r)
            src = self.x if r == 0 else self.xn
            dve.wait_ge(self.rstd_done, r + 1)
            for b in range(B):
                if b == self.held:
                    dve.wait_ge(self.turned, DC)
                dve.tensor_scalar(self.xn[:, b % self.held, :], src[:, b, :], self.mv[:, b, 0:1], self.rstd[:, b:b + 1],
                                  ALU.subtract, ALU.mult).then_inc(self.xn_done, 1)

    def vector_output(self, dve):
        self.vector_rows(dve)
        if self.affine:
            dve.wait_ge(self.gb_loaded, 32)
        for n in range(2 * DC):
            k, c = n // 2, n % 2
            dst = self.out[:, c, 4 * k * T:4 * (k + 1) * T].rearrange("p (b t) -> p b t", b=4)
            dve.wait_ge(self.turned, n + 1)
            if self.affine:
                dve.tensor_scalar(dst, self.banks[n], self.gb[:, 0, c:c + 1], self.gb[:, 1, c:c + 1],
                                  ALU.mult, ALU.add).then_inc(self.evacuated, 1)
            else:
                dve.tensor_copy(dst, self.banks[n]).then_inc(self.evacuated, 1)

    def tensor(self, pe):
        for n in range(2 * DC):
            k, c = n // 2, n % 2
            pe.wait_ge(self.xn_done, B * (self.rounds - 1) + 4 * (k + 1))
            for j in range(4):
                mm = pe.transpose(self.banks[n][:, j, :], self.xn[:, (4 * k + j) % self.held, c * P:(c + 1) * P],
                                  self.ident[0:T, 0:T])
            mm.then_inc(self.turned, 1)


class Shape:

    def __init__(self, heads, width, keys, scale, look):
        self.heads, self.scale, self.look = heads, scale, look
        self.inner = heads * width
        self.width = width
        self.keys = keys
        n = -(-keys // P)
        size = -(-keys // n)
        size += size % 2
        self.even = keys + keys % 2
        self.chunks = [(c * size, min(size, keys - c * size)) for c in range(n)]
        self.size = size
        self.mc = self.inner // P


def attention_phase(nc, st, phase, A, xT, wq, wk, wv, wo=None, qb=None, kb=None, vb=None, ob=None,
                    ctxT=None, ctx_rows=None, ctx_gb=None, group=None, mask=None, gate=0,
                    rounds=1, affine=None):
    x, ident, tg = st["x"], st["ident"], st["tanh_g"]
    H, LA, NC, MC = A.heads, A.look, len(A.chunks), A.mc
    KEYS, SZ, EVEN = A.keys, A.size, A.even
    RP = 4 if H % 4 == 0 else 2
    narrow = A.width < 64
    single = H == 1
    HG = P // A.width if narrow else 1
    VN = min(512, A.inner)

    pieces = []
    if ctx_rows is not None:
        pieces += [("C", 0), ("C", 1)]
    QG = min(4, MC)
    queries = [("Q", j) for j in range(MC // QG)]
    keys = [("K", m) for m in range(MC)]
    pieces += keys + queries if single else queries + keys
    pieces += [("V", (c, f)) for c in range(NC) for f in range(A.inner // VN)]
    first_pieces = sorted(pieces, key=lambda p: ("CKVQ" if ctx_rows is None else "CQKV").index(p[0]))
    kq_end0 = len(first_pieces)
    if wo is not None:
        pieces.insert(3 if ctx_rows is not None else 2, ("O", 0))
    NP, NP0 = len(pieces), len(first_pieces)
    OUT = [p[0] for p in pieces].index("O") if wo is not None else None
    HAS_OUT = int(wo is not None)
    kq_end = 1 + max(j for j, p in enumerate(pieces) if p[0] in "KQ")
    start = 0 if single else 2
    at_step = [[] for _ in range(H)]
    for j in range(NP):
        at_step[start + j * (H - LA - start) // NP].append(j)

    def count_of(b, j, first, last):
        if first:
            return NP0 + j - (HAS_OUT and j > OUT)
        return NP0 - HAS_OUT + NP * b + (0 if last else j)

    def ring_of(u, j, first, last):
        return count_of(u if not first else 0, j, first, last) % 2

    def steps_pieces(h, first, last):
        found = []
        for j in at_step[h]:
            kind, arg = pieces[j]
            if kind == "O" and first or kind != "O" and last:
                continue
            found.append((j, kind, arg))
        return found

    def halves(found):
        cut = sum(kind != "V" for j, kind, arg in found) if single else len(found)
        return found[:cut], found[cut:]

    def some_piece(act_on, j, kind, arg, b, u, first, last):
        count, ring = count_of(b, j, first, last), ring_of(u, j, first, last)
        if kind == "O":
            act_on(kind, arg, b - 1, 1 - u, count, ring)
        else:
            act_on(kind, arg, b + 1, 1 - u, count, ring)

    def done_of(b, end, end0):
        if isinstance(b, int) and b == 0:
            return end0
        if isinstance(b, int) and b == 1 and wo is not None and end <= OUT:
            return NP0 + end
        return NP0 - HAS_OUT + NP * (b - 1) + end

    with ExitStack() as ctx:
        hq = H // MC if not single else 1
        rounded_words = 4 * DC * (A.inner + EVEN) + (4 * MC * (EVEN + hq * T) + 2 * MC * T) * narrow
        m = Memory(nc, ctx, st, phase, words=ARENA - rounded_words)
        wqs = m.sb("wq", [P, DC, A.inner])
        wks, wvs = ([m.rounded(f"{n}_{k}", [P, DC, A.inner]) for k in ("high", "low")] for n in ("wk", "wv"))
        wos = m.sb("wo", [P, MC, D]) if wo is not None else None
        kvT = [[m.rounded(f"kvT{u}_{k}", [P, DC, EVEN]) for k in ("high", "low")] for u in range(2)]
        if ctx_rows is None:
            raw = [m.sb(f"raw{u}", [P, DC, S2]) for u in range(2)]
        else:
            raw = [m.sb("raw", [P, DC, S2])] * 2
        if narrow:
            kT = [[m.rounded(f"kT{u}_{k}", [P, MC, EVEN]) for k in ("high", "low")] for u in range(2)]
            qm = [[m.rounded(f"qm{u}_{k}", [P, MC, hq, T]) for k in ("high", "low")] for u in range(2)]
            qs = [m.sb(f"qs{u}", [P, MC, T]) for u in range(2)]
            q_parts = [m.rounded(f"q_{k}", [P, MC, T]) for k in ("high", "low")]
            v = [m.sb(f"v{u}", [SZ, NC, MC, HG, P]) for u in range(2)]
        else:
            kT = [m.sb(f"kT{u}", [P, MC, KEYS]) for u in range(2)]
            qm = [m.sb(f"qm{u}", [P, MC, hq, T]) for u in range(2)]
            v_places = [m.sb(f"v{u}", [P, NC * A.inner]) for u in range(2)]
            v = [z[0:SZ, :].rearrange("p (c n) -> p c n", c=NC) for z in v_places]
        if ctx_rows is not None:
            xn_place = v_places[0][0:T, 0:B * D].rearrange("p (b d) -> p b d", b=B)
            w_raw = [v_places[1][:, j * DC * A.inner:(j + 1) * DC * A.inner].rearrange("p (c n) -> p c n", c=DC)
                     for j in range(2)]
        else:
            xn_place = None
            w_raw = [m.sb(f"w_raw{j}", [P, DC, A.inner]) for j in range(2)]
        prob = [m.sb(f"prob{j}", [T, KEYS]) for j in range(RP)]
        probT = [m.sb(f"probT{j}", [SZ, NC, T]) for j in range(2)]
        oT = m.sb("oT", [P, MC, T]) if wo is not None else None
        negmax = m.sb("negmax", [T, RP])
        rowmax = m.sb("rowmax", [T, RP])
        total = m.sb("total", [T, RP])
        inv = m.sb("inv", [T, RP])
        qbs = m.sb("qb", [P, MC]) if qb is not None else None
        kbs = m.sb("kb", [P, MC]) if kb is not None else None
        vbs = m.sb("vb", [P, A.inner]) if vb is not None else None
        obs = m.sb("ob", [T, D]) if ob is not None else None
        if ctx_rows is not None:
            rows = [m.sb(f"rows{u}", [CR, 3, D]) for u in range(2)]
            cn = [m.sb(f"cn{u}", [CR, 3, D]) for u in range(2)]
            cstats = [m.sb(f"cstats{u}", [CR, 3, 6]) for u in range(2)]
            cmv = [m.sb(f"cmv{u}", [CR, 3, 2]) for u in range(2)]
            cve, crstd = ([m.sb(f"{n}{u}", [CR, 3]) for u in range(2)] for n in ("cve", "crstd"))
            chalf = m.sb("chalf", [CR, 3])
            cgb = m.sb("cgb", [P, 2, DC])
        if group is not None:
            gp = [m.sb(f"gp{u}", [T, KEYS]) for u in range(2)]
            mk = [m.sb(f"mk{u}", [T, KEYS], I32) for u in range(2)]
            neg = [m.sb(f"neg{u}", [T, KEYS]) for u in range(2)]
            spacers = m.sb("spacers", [P, RP])
            scored = [m.sb(f"scored{j}", [T, KEYS]) for j in range(RP)]
        psS = [m.ps(f"psS{j}") for j in range(2)]
        psT = [m.ps(f"psT{j}") for j in range(2)]
        psO = [m.ps(f"psO{j}") for j in range(2)]
        psP = [m.ps(f"psP{j}") for j in range(2)]

        w_loaded = {n: m.sem(f"w_{n}_loaded") for n in ("k", "q", "v", "o")}
        small_loaded, zeroed, zero_made = m.sem("small_loaded"), m.sem("zeroed"), m.sem("zero_made")
        zero, spacer = m.sb("zero", [P, 1]), m.sb("spacer", [P, 1])
        w_high, w_low, ctx_high, ctx_low = (m.sem(n) for n in ("w_high", "w_low", "ctx_high", "ctx_low"))
        lat_high, lat_low, q_high, q_low, qm_made = (
            m.sem(n) for n in ("lat_high", "lat_low", "q_high", "q_low", "qm_made"))
        k_high, evened = m.sem("k_high"), m.sem("evened")
        norm = Normalized(m, st, xT, psS + psT, rounds, affine, xn_place)
        ctx_loaded = [m.sem(f"ctx_loaded{u}") for u in range(2)]
        group_loaded = [m.sem(f"group_loaded{u}") for u in range(2)]
        rows_loaded = [m.sem(f"rows_loaded{u}") for u in range(2)]
        cstats_done, cmv_done, cve_done = m.sem("cstats_done"), m.sem("cmv_done"), m.sem("cve_done")
        crstd_done, cn_done = m.sem("crstd_done"), m.sem("cn_done")
        piece_ready, piece_evac, q_moved = m.sem("piece_ready"), m.sem("piece_evac"), m.sem("q_moved")
        s_ready, max_ready = m.sem("s_ready"), m.sem("max_ready")
        exp_done, inv_done, p_ready = m.sem("exp_done"), m.sem("inv_done"), m.sem("p_ready")
        t_ready, pt_copied, pv_done = m.sem("t_ready"), m.sem("pt_copied"), m.sem("pv_done")
        o_copied, neg_made = m.sem("o_copied"), m.sem("neg_made")
        biased, q_part, v_part = m.sem("biased"), m.sem("q_part"), m.sem("v_part")
        turn_cleared = m.sem("turn_cleared")
        headmask = st["headmask"]
        LAST_OUT = NP0 - HAS_OUT + NP * (B - 1) + 1
        ZEROED = 2 * (not single)
        padded = v if narrow else qm
        UNEVEN = A.chunks[-1][1] != SZ

        def ring2(u, h):
            return u if single else h % 2

        def ring4(u, h):
            return u if single else h % 4

        def diagonal(flat, n, width):
            dims = [list(d) for d in flat.ap]
            return bass.AP(tensor=flat.tensor, offset=flat.offset,
                           ap=[dims[0], [P + width, n], [1, width]])

        block = ctx.enter_context(nc.Block())
        SMALL = sum(z is not None for z in (qb, kb, vb, ob)) + 2 * (ctx_gb is not None)
        G = MC if not single else 1
        GROUPS = 2 if not single else 1

        def later_batches(loop_engine, run):
            run(2, 0)
            with loop_engine.Fori(0, (B - 4) // 2) as i:
                run(i * 2 + 3, 1)
                run(i * 2 + 4, 0)
            run(B - 1, 1)

        @block.sync
        def _(sp):
            def load_rows(b, u):
                sp.dma_start(rows[u], ctx_rows[bass.ds(b, 1)].rearrange("b (c p) d -> p (b c) d", p=CR)
                             ).then_inc(rows_loaded[u], 16)

            norm.sync(sp)
            if ctx_rows is not None:
                load_rows(0, 0)
                for n, z in enumerate(ctx_gb):
                    sp.dma_start(cgb[:, n, :], z.rearrange("(c p) -> p c", p=P),
                                 allow_slow_non_contiguous=True).then_inc(small_loaded, 16)
            else:
                for b in range(2):
                    sp.dma_start(raw[b][:], ctxT[:, b].rearrange("(c p) s -> p c s", p=P)
                                 ).then_inc(ctx_loaded[b], 16)
            for z, t in ((qb, qbs), (kb, kbs)):
                if z is not None:
                    sp.dma_start(t[:], z.rearrange("(c p) -> p c", p=P),
                                 allow_slow_non_contiguous=True).then_inc(small_loaded, 16)
            if vb is not None:
                sp.dma_start(vbs[:], broadcast_rows(vb, P)).then_inc(small_loaded, 16)
            if ob is not None:
                sp.dma_start(obs[:], broadcast_rows(ob, T)).then_inc(small_loaded, 16)
            for n, t, z in (("k", w_raw[0], wk), ("v", w_raw[1], wv), ("q", wqs, wq), ("o", wos, wo)):
                if z is not None:
                    sp.dma_start(t[:], z.rearrange("(c p) n -> p c n", p=P)).then_inc(w_loaded[n], 16)
            if ctx_rows is not None:
                load_rows(1, 1)

            def loads(b, u):
                if ctx_rows is not None:
                    sp.wait_ge(cn_done, (b - 1) * 3)
                    load_rows(b, u)
                else:
                    sp.wait_ge(ctx_low, b - 1)
                    sp.dma_start(raw[u][:], ctxT[:, bass.ds(b, 1)].rearrange(
                        "(c p) b s -> p c (b s)", p=P)).then_inc(ctx_loaded[u], 16)
                if group is not None:
                    sp.wait_ge(p_ready, (b - 1) * H)
                    sp.dma_start(gp[u][:], group[bass.ds(b, 1)].rearrange("b t s -> (b t) s")
                                 ).then_inc(group_loaded[u], 16)
                    sp.dma_start(mk[u][:], mask[bass.ds(b, 1)].rearrange("b t s -> (b t) s")
                                 ).then_inc(group_loaded[u], 16)

            if group is not None:
                for b in range(2):
                    sp.dma_start(gp[b][:], group[b]).then_inc(group_loaded[b], 16)
                    sp.dma_start(mk[b][:], mask[b]).then_inc(group_loaded[b], 16)
            later_batches(sp, loads)

        @block.gpsimd
        def _(pool):
            def low(rest, whole, high, sem):
                pool.tensor_tensor(rest, whole, high.bitcast(F32), ALU.subtract).then_inc(sem, 1)

            def split_weights(j):
                pool.wait_ge(w_high, j + 1)
                low((wks, wvs)[j][1][:], w_raw[j], (wks, wvs)[j][0][:], w_low)

            def split_context(b, u):
                pool.wait_ge(ctx_high, b + 1)
                low(kvT[u][1][:, :, 0:S2], raw[u][:], kvT[u][0][:, :, 0:S2], ctx_low)

            def split_latents(b, u):
                pool.wait_ge(lat_high, b + 1)
                low(kvT[u][1][:, :, S2:KEYS], xT[:, :, bass.ds(b * T, T)], kvT[u][0][:, :, S2:KEYS], lat_low)

            def power(b, u):
                pool.wait_ge(cve_done, b + 1)
                pool.tensor_tensor(crstd[u], cve[u], chalf, ALU.pow).then_inc(crstd_done, 1)

            def split_queries(b, u):
                pool.wait_ge(q_high, b + 1)
                low(q_parts[1][:], qs[u][:], q_parts[0][:], q_low)
                pool.wait_ge(q_low, b + 1)
                if not isinstance(b, int) or b > 1:
                    pool.wait_ge(s_ready, b * H - H)
                for j in range(MC):
                    for part, masked_part in zip(q_parts, qm[u]):
                        pool.tensor_tensor(masked_part[:, j, :, :],
                                           part[:, j, :].bitcast(F32).unsqueeze(1).to_broadcast([P, hq, T]),
                                           headmask[:, :].unsqueeze(2).to_broadcast([P, hq, T]), ALU.mult
                                           ).then_inc(qm_made, 1)

            pool.memset(zero, 0.0).then_inc(zero_made, 1)
            norm.gpsimd_start(pool)
            if ctx_rows is None:
                split_context(0, 0)
                split_weights(0)
                norm.gpsimd_power(pool, 0)
                split_weights(1)
                if narrow:
                    split_queries(0, 0)
                split_context(1, 1)
                if narrow:
                    split_queries(1, 1)
            else:
                pool.memset(chalf[:], -0.5).then_inc(zero_made, 1)
                norm.gpsimd_power(pool, 0)
                pool.wait_ge(zero_made, 2)
                power(0, 0)
                split_weights(0)
                norm.gpsimd_power(pool, 1)
                split_weights(1)
                norm.wait(pool)
                split_latents(0, 0)
                split_context(0, 0)
                power(1, 1)
                split_latents(1, 1)
                split_context(1, 1)

            def later(b, u):
                if ctx_rows is not None:
                    power(b, u)
                    split_latents(b, u)
                split_context(b, u)
                if narrow:
                    split_queries(b, u)

            later_batches(pool, later)

        @block.tensor
        def _(pe):
            def piece(kind, arg, b, u, count, ring):
                ps = psP[ring]
                after(pe, piece_evac, count - 1)
                if kind == "C":
                    pe.wait_ge(cn_done, b * 3 + 3)
                    for r in range(3):
                        mm = pe.transpose(ps[:, CR * r:CR * r + CR], cn[u][:, r, P * arg:P * arg + P],
                                          ident[0:CR, 0:CR])
                elif kind == "K":
                    if arg == 0:
                        pe.wait_ge(ctx_low, b + 1)
                        if ctx_rows is not None:
                            pe.wait_ge(lat_low, b + 1)
                    for k in range(DC):
                        mm = split_product(pe, ps[:, 0:EVEN], [w[:, k, P * arg:P * arg + P] for w in wks],
                                           [z[:, k, :] for z in kvT[u]], start=(k == 0), stop=(k == DC - 1))
                elif kind == "Q":
                    for j in range(QG):
                        mq = QG * arg + j
                        for k in range(DC):
                            mm = pe.matmul(ps[:, j * T:(j + 1) * T], wqs[:, k, P * mq:P * mq + P],
                                           xT[:, k, bass.ds(b * T, T)],
                                           start=(k == 0), stop=(k == DC - 1))
                elif kind == "V":
                    (c, f) = arg
                    k0, ks = A.chunks[c]
                    ke = ks + ks % 2
                    for k in range(DC):
                        mm = split_product(pe, ps[0:ke, 0:VN], [z[:, k, k0:k0 + ke] for z in kvT[u]],
                                           [w[:, k, VN * f:VN * f + VN] for w in wvs],
                                           start=(k == 0), stop=(k == DC - 1))
                else:
                    pe.wait_ge(o_copied, b * GROUPS + GROUPS)
                    for c in range(MC):
                        mm = pe.matmul(ps[0:T, 0:D], oT[:, c, :], wos[:, c, :],
                                       start=(c == 0), stop=(c == MC - 1))
                mm.then_inc(piece_ready, 1)

            def scores(b, u, h):
                n = b * H + h
                if h == 0:
                    pe.wait_ge(piece_evac, done_of(b, kq_end, kq_end0))
                if narrow and h % hq == 0:
                    pe.wait_ge(qm_made, b * 2 * MC + 2 * (h // hq + 1))
                if not single:
                    after(pe, exp_done, n - 1)
                else:
                    after(pe, exp_done, n)
                out = psS[ring2(u, h)][0:T, 0:EVEN if narrow else KEYS]
                if single:
                    for c in range(MC):
                        mm = pe.matmul(out, qm[u][:, c, 0, :], kT[u][:, c, :], start=(c == 0),
                                       stop=(c == MC - 1))
                elif narrow:
                    mm = split_product(pe, out, [z[:, h // hq, h % hq, :] for z in qm[u]],
                                       [z[:, h // hq, :] for z in kT[u]], start=True, stop=True)
                else:
                    mm = pe.matmul(out, qm[u][:, h // hq, h % hq, :], kT[u][:, h // hq, :],
                                   start=True, stop=True)
                mm.then_inc(s_ready, 1)

            def turn(b, u, h):
                n = b * H + h
                pe.wait_ge(p_ready, n + 1)
                if not single:
                    after(pe, pt_copied, n - 1)
                for c, (k0, ks) in enumerate(A.chunks):
                    mm = pe.transpose(psT[ring2(u, h)][0:ks, c * T:(c + 1) * T],
                                      prob[ring4(u, h)][:, k0:k0 + ks], ident[0:T, 0:T])
                mm.then_inc(t_ready, 1)

            def weigh(b, u, h):
                n = b * H + h
                if h == 0:
                    pe.wait_ge(piece_evac, done_of(b, NP, NP0))
                pe.wait_ge(pt_copied, n + 1)
                g = 0 if single else h // (H // 2)
                if not single and h % (H // 2) == 0:
                    after(pe, o_copied, (b - 1) * GROUPS + g + 1)
                for c, (k0, ks) in enumerate(A.chunks):
                    pt = probT[ring2(u, h)][0:ks, c, :]
                    if single:
                        mm = pe.matmul(psO[u][0:T, 0:D], pt, v[u][0:ks, c, :],
                                       start=(c == 0), stop=(c == NC - 1))
                    elif narrow:
                        mm = pe.matmul(psO[g][:, 0:T], v[u][0:ks, c, g, h % HG, :], pt,
                                       start=(c == 0 and h % HG == 0),
                                       stop=(c == NC - 1 and h % HG == HG - 1))
                    else:
                        p0 = A.width * (h % 2)
                        col = (h // 2) % (MC // 2) * T
                        mm = pe.matmul(psO[g][p0:p0 + A.width, col:col + T],
                                       v[u][0:ks, c, A.width * h:A.width * (h + 1)], pt,
                                       start=(c == 0), stop=(c == NC - 1))
                mm.then_inc(pv_done, 1)

            if UNEVEN:
                pe.wait_ge(turn_cleared, 2)
            early = 0
            if ctx_rows is None:
                early = sum(kind in "KV" for kind, arg in first_pieces)
            else:
                norm.tensor(pe)
                norm.wait(pe)
            pe.wait_ge(evened, 4)
            for j, (kind, arg) in enumerate(first_pieces):
                if j == early and early:
                    norm.tensor(pe)
                    norm.wait(pe)
                if kind in "KQV" and (j == 0 or first_pieces[j - 1][0] != kind):
                    if kind == "Q":
                        pe.wait_ge(w_loaded["q"], 16)
                    else:
                        pe.wait_ge(w_low, "KV".index(kind) + 1)
                piece(kind, arg, 0, 0, j, j % 2)
            if wo is not None:
                pe.wait_ge(w_loaded["o"], 16)
            after(pe, zeroed, ZEROED)
            for h in range(LA):
                scores(0, 0, h)

            def run(b, u, first, last):
                for h in range(H):
                    if LA == 0:
                        scores(b, u, h)
                    elif h + LA < H:
                        scores(b, u, h + LA)
                    elif not last:
                        scores(b + 1, 1 - u, h + LA - H)
                    early, late = halves(steps_pieces(h, first, last))
                    for j, kind, arg in early:
                        some_piece(piece, j, kind, arg, b, u, first, last)
                    turn(b, u, h)
                    for j, kind, arg in late:
                        some_piece(piece, j, kind, arg, b, u, first, last)
                    if LA == 0:
                        weigh(b, u, h)
                    elif h:
                        weigh(b, u, h - 1)
                    elif not first:
                        weigh(b - 1, 1 - u, H - 1)

            in_pairs(pe, run)
            if LA:
                weigh(B - 1, 1, H - 1)
            if wo is not None:
                piece("O", 0, B - 1, 1, LAST_OUT, LAST_OUT % 2)

        @block.vector
        def _(dve):
            def evacuate(kind, arg, b, u, count, ring):
                ps = psP[ring]
                dve.wait_ge(piece_ready, count + 1)
                if kind == "C":
                    if arg == 0:
                        after(dve, ctx_low, b)
                    op = dve.tensor_scalar(raw[u][:, arg, :], ps[:, 0:S2], cgb[:, 0, arg:arg + 1],
                                           cgb[:, 1, arg:arg + 1], ALU.mult, ALU.add)
                elif kind == "K":
                    if narrow:
                        high, rest = (z[:, arg, :] for z in kT[u])
                        bias = kbs[:, arg:arg + 1]
                        dve.tensor_scalar(high, ps[:, 0:EVEN], bias, None, ALU.add).then_inc(k_high, 1)
                        dve.wait_ge(k_high, b * MC + arg + 1)
                        op = dve.scalar_tensor_tensor(rest, ps[:, 0:EVEN], bias, high.bitcast(F32), ALU.add,
                                                      ALU.subtract)
                    else:
                        op = dve.tensor_copy(kT[u][:, arg, :], ps[:, 0:KEYS])
                elif kind == "Q":
                    q = ps[:, 0:QG * T].rearrange("p (m t) -> p m t", m=QG)
                    ms = slice(QG * arg, QG * arg + QG)
                    if narrow:
                        if not isinstance(b, int) or b > 1:
                            dve.wait_ge(q_low, b - 1)
                        for j in range(QG):
                            dve.tensor_scalar(qs[u][:, j, :], q[:, j, :], qbs[:, j:j + 1], A.scale,
                                              ALU.add, ALU.mult).then_inc(q_moved, 1)
                        dve.wait_ge(q_moved, b * MC + MC)
                        op = dve.memset(spacer, 0.0)
                    elif single:
                        op = dve.tensor_scalar(qm[u][:, ms, 0, :], q, A.scale, None, ALU.mult)
                    else:
                        dve.tensor_scalar(qm[u][0:64, ms, 0, :], q[0:64], A.scale, None,
                                          ALU.mult).then_inc(q_part, 1)
                        op = dve.tensor_scalar(qm[u][64:128, ms, 1, :], q[64:128], A.scale, None, ALU.mult)
                        dve.wait_ge(q_part, b * (MC // QG) + arg + 1)
                elif kind == "V":
                    (c, f) = arg
                    ks = A.chunks[c][1]
                    if narrow:
                        for g in range(MC):
                            dst = v[u][0:ks, c, g, :, :].rearrange("k h n -> k (h n)")
                            dst = diagonal(dst, HG, A.width)
                            src = ps[0:ks, P * g:P * g + P].rearrange("k (h n) -> k h n", h=HG)
                            bias = vbs[0:ks, P * g:P * g + P].rearrange("k (h n) -> k h n", h=HG)
                            op = dve.tensor_tensor(dst, src, bias, ALU.add)
                            if g < MC - 1:
                                op.then_inc(v_part, 1)
                    else:
                        op = dve.tensor_copy(v[u][0:ks, c, VN * f:VN * f + VN], ps[0:ks, 0:VN])
                else:
                    op = dve.scalar_tensor_tensor(x[:, bass.ds(b, 1), :], ps[0:T, 0:D].unsqueeze(1),
                                                  tg[0:T, gate:gate + 1], x[:, bass.ds(b, 1), :],
                                                  ALU.mult, ALU.add)
                op.then_inc(piece_evac, 1)

            def context_statistics(b, u):
                dve.wait_ge(rows_loaded[u], (b - u) * 8 + 16)
                for r in range(3):
                    dve.bn_stats(cstats[u][:, r, :], rows[u][:, r, :]).then_inc(cstats_done, 1)
                dve.wait_ge(cstats_done, b * 3 + 3)
                dve.memset(spacer, 0.0)
                for r in range(3):
                    dve.bn_aggr(cmv[u][:, r, :], cstats[u][:, r, :]).then_inc(cmv_done, 1)
                dve.wait_ge(cmv_done, b * 3 + 3)
                dve.tensor_scalar(cve[u], cmv[u][:, :, 1], EPS, None, ALU.add).then_inc(cve_done, 1)

            def context_rows(b, u):
                dve.wait_ge(crstd_done, b + 1)
                for r in range(3):
                    dve.tensor_scalar(cn[u][:, r, :], rows[u][:, r, :], cmv[u][:, r, 0:1], crstd[u][:, r:r + 1],
                                      ALU.subtract, ALU.mult).then_inc(cn_done, 1)

            def masked(b, u):
                dve.wait_ge(group_loaded[u], (b - u) * 16 + 32)
                dve.tensor_scalar(neg[u][:], mk[u][:], -1.0, 1e9, ALU.add, ALU.mult).then_inc(neg_made, 1)

            def maximum(b, u, h):
                n, j = b * H + h, ring4(u, h)
                dve.wait_ge(s_ready, n + 1)
                src = psS[ring2(u, h)][0:T, 0:KEYS]
                if group is not None:
                    if h == 0:
                        dve.wait_ge(neg_made, b + 1)
                    dve.memset(spacers[:, j:j + 1], 0.0)
                    dve.tensor_tensor_reduce(scored[j][:], src, neg[u][:], -1.0, LARGEST, ALU.add, ALU.min,
                                             negmax[:, j:j + 1]).then_inc(max_ready, 1)
                else:
                    dve.tensor_reduce(negmax[:, j:j + 1], src, AX, ALU.max, negate=True).then_inc(max_ready, 1)

            def normalize(b, u, h):
                n, j = b * H + h, ring4(u, h)
                dve.wait_ge(exp_done, n + 1)
                dve.reciprocal(inv[:, j:j + 1], total[:, j:j + 1]).then_inc(inv_done, 1)
                dve.wait_ge(inv_done, n + 1)
                if group is not None:
                    op = dve.scalar_tensor_tensor(prob[j][:], prob[j][:], inv[:, j:j + 1], gp[u][:],
                                                  ALU.mult, ALU.mult)
                else:
                    op = dve.tensor_scalar(prob[j][:], prob[j][:], inv[:, j:j + 1], None, ALU.mult)
                op.then_inc(p_ready, 1)

            if UNEVEN:
                for j in range(2):
                    dve.memset(psT[j][:], 0.0).then_inc(turn_cleared, 1)
            norm.vector_statistics(dve)
            if ctx_rows is not None:
                context_statistics(0, 0)
                norm.vector_output(dve)
                context_rows(0, 0)
            after(dve, small_loaded, 16 * SMALL)
            after(dve, zeroed, ZEROED - 1)
            early = 0 if ctx_rows is not None else sum(kind in "KV" for kind, arg in first_pieces)
            for j, (kind, arg) in enumerate(first_pieces):
                if j == early and early:
                    norm.vector_output(dve)
                evacuate(kind, arg, 0, 0, j, j % 2)
            after(dve, zeroed, ZEROED)
            if ob is not None:
                dve.tensor_scalar(obs[:], obs[:], tg[0:T, gate:gate + 1], None,
                                  ALU.mult).then_inc(biased, 1)
                dve.wait_ge(biased, 1)
                dve.tensor_tensor(x[:], x[:], obs[:].unsqueeze(1).to_broadcast([T, B, D]),
                                  ALU.add).then_inc(biased, 1)
                dve.wait_ge(biased, 2)
            if group is not None:
                masked(0, 0)
            for h in range(LA):
                maximum(0, 0, h)
            if LA:
                normalize(0, 0, 0)

            def run(b, u, first, last):
                if ctx_rows is not None and not last:
                    context_statistics(b + 1, 1 - u)
                if group is not None and not last:
                    masked(b + 1, 1 - u)
                for h in range(H):
                    if LA == 0:
                        maximum(b, u, h)
                    elif h + LA < H:
                        maximum(b, u, h + LA)
                    elif not last:
                        maximum(b + 1, 1 - u, h + LA - H)
                    if ctx_rows is not None and not last and h == 1:
                        context_rows(b + 1, 1 - u)
                    if LA and h + 1 < H:
                        normalize(b, u, h + 1)
                    elif LA and not last:
                        normalize(b + 1, 1 - u, 0)
                    early, late = halves(steps_pieces(h, first, last))
                    for j, kind, arg in early:
                        some_piece(evacuate, j, kind, arg, b, u, first, last)
                    if LA == 0:
                        normalize(b, u, h)
                    for j, kind, arg in late:
                        some_piece(evacuate, j, kind, arg, b, u, first, last)
                    if LA == 0:
                        dve.wait_ge(pv_done, b + 1)
                        dve.scalar_tensor_tensor(x[:, bass.ds(b, 1), :], psO[u][0:T, 0:D].unsqueeze(1),
                                                 tg[0:T, gate:gate + 1], x[:, bass.ds(b, 1), :],
                                                 ALU.mult, ALU.add).then_inc(o_copied, 1)

            in_pairs(dve, run)
            if wo is not None:
                evacuate("O", 0, B - 1, 1, LAST_OUT, LAST_OUT % 2)

        @block.scalar
        def _(act):
            def exponent(b, u, h):
                n, j = b * H + h, ring4(u, h)
                act.wait_ge(max_ready, n + 1)
                if LA:
                    after(act, t_ready, n - RP + 1)
                src = scored[j][:] if group is not None else psS[ring2(u, h)][0:T, 0:KEYS]
                act.activation(prob[j][:], src, ACT.Exp, bias=negmax[:, j:j + 1],
                               scale=1.0 if group is None else -1.0, accum_out=total[:, j:j + 1]).then_inc(exp_done, 1)

            def copy_turned(b, u, h):
                n, r = b * H + h, ring2(u, h)
                act.wait_ge(t_ready, n + 1)
                if LA:
                    after(act, pv_done, n - 1)
                act.copy(probT[r][:].rearrange("k c t -> k (c t)"), psT[r][0:SZ, 0:NC * T]
                         ).then_inc(pt_copied, 1)

            def copy_out(b, g):
                act.wait_ge(pv_done, b * H + (g + 1) * (H // 2))
                act.copy(oT[:, g * (MC // 2):(g + 1) * (MC // 2), :],
                         psO[g][:, 0:MC // 2 * T].rearrange("p (m t) -> p m t", t=T)
                         ).then_inc(o_copied, 1)

            def high_weights(j):
                act.wait_ge(w_loaded["kv"[j]], 16)
                act.copy((wks, wvs)[j][0][:], w_raw[j]).then_inc(w_high, 1)

            def clear(u):
                if not single:
                    dims = "abcd"[:len(padded[u].shape) - 1]
                    flat = padded[u].rearrange(f"p {' '.join(dims)} -> p ({' '.join(dims)})")
                    act.copy(flat, zero[0:flat.shape[0], :].to_broadcast(list(flat.shape))).then_inc(zeroed, 1)

            def slot_read(b):
                if not isinstance(b, int) or b > 1:
                    act.wait_ge(piece_evac, done_of(b - 2, NP, NP0))

            def high_context(b, u):
                if ctx_rows is None:
                    act.wait_ge(ctx_loaded[u], (b - u) * 8 + 16)
                else:
                    act.wait_ge(piece_evac, done_of(b, 2, 2) if isinstance(b, int) else NP0 - 1 + NP * (b - 1) + 3)
                slot_read(b)
                act.copy(kvT[u][0][:, :, 0:S2], raw[u][:]).then_inc(ctx_high, 1)

            def high_latents(b, u):
                slot_read(b)
                act.copy(kvT[u][0][:, :, S2:KEYS], xT[:, :, bass.ds(b * T, T)]).then_inc(lat_high, 1)

            def high_queries(b, u):
                act.wait_ge(q_moved, b * MC + MC)
                after(act, qm_made, b * 2 * MC)
                act.copy(q_parts[0][:], qs[u][:]).then_inc(q_high, 1)

            act.wait_ge(zero_made, 1)
            for z in (z for slot in kvT for z in slot):
                act.copy(z[:, :, KEYS:EVEN], zero.unsqueeze(1).to_broadcast([P, DC, 1])).then_inc(evened, 1)
            clear(0)
            if ctx_rows is None:
                high_context(0, 0)
            high_weights(0)
            high_weights(1)
            if ctx_rows is not None:
                norm.wait(act)
                high_latents(0, 0)
                high_context(0, 0)
            clear(1)
            if narrow:
                high_queries(0, 0)
            for h in range(LA):
                exponent(0, 0, h)

            def run(b, u, first, last):
                for h in range(H):
                    if not last:
                        if ctx_rows is not None and h == 0:
                            high_latents(b + 1, 1 - u)
                        if h == (3 if ctx_rows is not None else 0):
                            high_context(b + 1, 1 - u)
                        if narrow and h == 4:
                            high_queries(b + 1, 1 - u)
                    if LA == 0:
                        exponent(b, u, h)
                    elif h + LA < H:
                        exponent(b, u, h + LA)
                    elif not last:
                        exponent(b + 1, 1 - u, h + LA - H)
                    copy_turned(b, u, h)
                    if LA and h == H // 2:
                        copy_out(b, 0)
                    elif LA and h == 0 and not first:
                        copy_out(b - 1, 1)

            in_pairs(act, run)
            if LA:
                copy_out(B - 1, 1)


HALF = R // 2


def columns(v):
    return v.rearrange("(c p) -> p c", p=P)


def add_bias(dve, st, bias, gate, sem):
    x, tg = st["x"], st["tanh_g"]
    dve.tensor_scalar(bias[:], bias[:], tg[0:T, gate:gate + 1], None, ALU.mult).then_inc(sem, 1)
    dve.wait_ge(sem, 1)
    dve.tensor_tensor(x[:], x[:], bias[:].unsqueeze(1).to_broadcast([T, B, D]), ALU.add).then_inc(sem, 1)
    dve.wait_ge(sem, 2)


def low_rank_ffn(nc, st, xT, io, gate=4):
    x, tg = st["x"], st["tanh_g"]
    RANK = io["L0_ffn_U1"].shape[1]
    FC = io["L0_ffn_V1"].shape[1] // P
    with ExitStack() as ctx:
        m = Memory(nc, ctx, st, "f0")
        u1 = m.sb("u1", [P, DC, RANK])
        v1 = m.sb("v1", [P, FC * P])
        b1 = m.sb("b1", [P, FC])
        u2 = m.sb("u2", [P, FC, RANK])
        v2 = m.sb("v2", [P, D])
        b2 = m.sb("b2", [T, D])
        pT = m.sb("pT", [P, R])
        qT = m.sb("qT", [P, R])
        hT = m.sb("hT", [P, FC, R])
        psA = [m.ps(f"psA{j}") for j in range(4)]
        psQ = [m.ps(f"psQ{j}") for j in range(2)]
        loaded, cleared, biased = m.sem("loaded"), m.sem("cleared"), m.sem("biased")
        p_ready, p_copied = m.sem("p_ready"), m.sem("p_copied")
        h_ready, h_done, q_ready, q_copied = m.sem("h_ready"), m.sem("h_done"), m.sem("q_ready"), m.sem("q_copied")
        y_ready, y_added = m.sem("y_ready"), m.sem("y_added")
        norm = Normalized(m, st, xT, psA)
        block = ctx.enter_context(nc.Block())

        @block.sync
        def _(sp):
            sp.dma_start(u1[:], io["L0_ffn_U1"].rearrange("(c p) r -> p c r", p=P)).then_inc(loaded, 16)
            sp.dma_start(v1[0:RANK, :], io["L0_ffn_V1"]).then_inc(loaded, 16)
            sp.dma_start(b1[:], columns(io["L0_ffn_b1"]), allow_slow_non_contiguous=True).then_inc(loaded, 16)
            sp.dma_start(u2[:], io["L0_ffn_U2"].rearrange("(c p) r -> p c r", p=P)).then_inc(loaded, 16)
            sp.dma_start(v2[0:RANK, :], io["L0_ffn_V2"]).then_inc(loaded, 16)
            sp.dma_start(b2[:], broadcast_rows(io["L0_ffn_b2"], T)).then_inc(loaded, 16)

        @block.gpsimd
        def _(pool):
            for t in (v1, v2, pT, qT):
                pool.memset(t[RANK:P, :], 0.0).then_inc(cleared, 1)
            pool.wait_ge(cleared, 4)
            norm.gpsimd(pool)

        @block.tensor
        def _(pe):
            pe.wait_ge(loaded, 96)
            pe.wait_ge(cleared, 4)
            norm.tensor(pe)
            norm.wait(pe)
            for f in range(2):
                for k in range(DC):
                    mm = pe.matmul(psQ[f][0:RANK, 0:HALF], u1[:, k, :], xT[:, k, f * HALF:(f + 1) * HALF],
                                   start=(k == 0), stop=(k == DC - 1))
                mm.then_inc(p_ready, 1)
            for n in range(2 * FC):
                c, f = n // 2, n % 2
                pe.wait_ge(p_copied, f + 1)
                after(pe, h_done, n - 3)
                pe.matmul(psA[n % 4][:, 0:HALF], v1[:, c * P:(c + 1) * P], pT[:, f * HALF:(f + 1) * HALF],
                          start=True, stop=True).then_inc(h_ready, 1)
            for f in range(2):
                for c in range(FC):
                    pe.wait_ge(h_done, 2 * c + f + 1)
                    mm = pe.matmul(psQ[f][0:RANK, 0:HALF], u2[:, c, :], hT[:, c, f * HALF:(f + 1) * HALF],
                                   start=(c == 0), stop=(c == FC - 1))
                mm.then_inc(q_ready, 1)
            for b in range(B):
                pe.wait_ge(q_copied, b // (B // 2) + 1)
                after(pe, y_added, b - 3)
                pe.matmul(psA[b % 4][0:T, 0:D], qT[:, b * T:(b + 1) * T], v2[:],
                          start=True, stop=True).then_inc(y_ready, 1)

        @block.scalar
        def _(act):
            act.wait_ge(loaded, 96)
            for n in range(2 * FC):
                c, f = n // 2, n % 2
                act.wait_ge(h_ready, n + 1)
                act.activation(hT[:, c, f * HALF:(f + 1) * HALF], psA[n % 4][:, 0:HALF],
                               ACT.Gelu_apprx_tanh, bias=b1[:, c:c + 1]).then_inc(h_done, 1)

        @block.vector
        def _(dve):
            norm.vector_statistics(dve)
            norm.vector_output(dve)
            for f in range(2):
                dve.wait_ge(p_ready, f + 1)
                dve.tensor_copy(pT[0:RANK, f * HALF:(f + 1) * HALF], psQ[f][0:RANK, 0:HALF]).then_inc(p_copied, 1)
            dve.wait_ge(loaded, 96)
            add_bias(dve, st, b2, gate, biased)
            for f in range(2):
                dve.wait_ge(q_ready, f + 1)
                dve.tensor_copy(qT[0:RANK, f * HALF:(f + 1) * HALF], psQ[f][0:RANK, 0:HALF]).then_inc(q_copied, 1)
            for b in range(B):
                dve.wait_ge(y_ready, b + 1)
                dve.scalar_tensor_tensor(x[:, b, :], psA[b % 4][0:T, 0:D], tg[0:T, gate:gate + 1], x[:, b, :],
                                         ALU.mult, ALU.add).then_inc(y_added, 1)


def shift_ffn(nc, st, xT, io, gate=5):
    x, tg = st["x"], st["tanh_g"]
    with ExitStack() as ctx:
        m = Memory(nc, ctx, st, "f1")
        wr, wk, wv = (m.sb(n, [P, DC, D]) for n in ("wr", "wk", "wv"))
        mu = m.sb("mu", [P, 2, DC])
        rest = m.sb("rest", [P, 2, DC])
        mixed = [m.sb(f"mixed{j}", [P, DC, R]) for j in range(2)]
        relu = m.sb("relu", [P, 4, HALF])
        kT = m.sb("kT", [P, DC, R])
        r = m.sb("r", [T, B, D])
        y = m.sb("y", [T, 2, D])
        psA = [m.ps(f"psA{j}") for j in range(4)]
        psR = [m.ps(f"psR{j}") for j in range(4)]
        loaded, rest_made = m.sem("loaded"), m.sem("rest_made")
        scaled, mix_done = m.sem("scaled"), m.sem("mix_done")
        k_ready, relu_done, k_done = m.sem("k_ready"), m.sem("relu_done"), m.sem("k_done")
        r_ready, r_done, v_ready, y_made, y_added = (m.sem(n) for n in (
            "r_ready", "r_done", "v_ready", "y_made", "y_added"))
        norm = Normalized(m, st, xT, psA)
        block = ctx.enter_context(nc.Block())

        @block.sync
        def _(sp):
            for n, z in enumerate(("L1_ffn_mu_r", "L1_ffn_mu_k")):
                sp.dma_start(mu[:, n, :], columns(io[z]), allow_slow_non_contiguous=True).then_inc(loaded, 16)
            for t, z in ((wk, "L1_ffn_W_kT"), (wr, "L1_ffn_W_rT"), (wv, "L1_ffn_W_vT")):
                sp.dma_start(t[:], io[z].rearrange("(c p) n -> p c n", p=P)).then_inc(loaded, 16)

        @block.gpsimd
        def _(pool):
            norm.gpsimd(pool)

        @block.vector
        def _(dve):
            norm.vector_statistics(dve)
            norm.vector_output(dve)
            norm.wait(dve)
            dve.wait_ge(loaded, 80)
            dve.tensor_scalar(rest[:], mu[:], -1.0, 1.0, ALU.mult, ALU.add).then_inc(rest_made, 1)
            for n, j in enumerate((1, 0)):
                for c in range(DC):
                    dve.tensor_scalar(mixed[j][:, c, :], xT[:, c, :], mu[:, j, c:c + 1], None,
                                      ALU.mult).then_inc(scaled, 1)
                dve.wait_ge(rest_made, 1)
                dve.wait_ge(scaled, 2 * n + 2)
                for c in range(DC):
                    new = mixed[j][:, c, :].rearrange("p (b t) -> p b t", t=T)[:, :, 1:T]
                    old = xT[:, c, :].rearrange("p (b t) -> p b t", t=T)[:, :, 0:T - 1]
                    dve.scalar_tensor_tensor(new, old, rest[:, j, c:c + 1], new, ALU.mult,
                                             ALU.add).then_inc(mix_done, 1)
            for n in range(4):
                c, f = n // 2, n % 2
                dve.wait_ge(relu_done, n + 1)
                dve.tensor_tensor(kT[:, c, f * HALF:(f + 1) * HALF], relu[:, n, :], relu[:, n, :],
                                  ALU.mult).then_inc(k_done, 1)
            for b in range(B):
                dve.wait_ge(r_done, b + 1)
                dve.wait_ge(v_ready, b + 1)
                dve.tensor_tensor(y[:, b % 2, :], psA[b % 4][0:T, 0:D], r[:, b, :], ALU.mult).then_inc(y_made, 1)
                dve.wait_ge(y_made, b + 1)
                dve.scalar_tensor_tensor(x[:, b, :], y[:, b % 2, :], tg[0:T, gate:gate + 1], x[:, b, :],
                                         ALU.mult, ALU.add).then_inc(y_added, 1)

        @block.tensor
        def _(pe):
            norm.tensor(pe)
            pe.wait_ge(mix_done, DC)
            for n in range(4):
                c, f = n // 2, n % 2
                for k in range(DC):
                    mm = pe.matmul(psA[n][:, 0:HALF], wk[:, k, c * P:(c + 1) * P],
                                   mixed[1][:, k, f * HALF:(f + 1) * HALF], start=(k == 0), stop=(k == DC - 1))
                mm.then_inc(k_ready, 1)
            pe.wait_ge(mix_done, 2 * DC)
            for b in range(B):
                after(pe, r_done, b - 3)
                for k in range(DC):
                    mm = pe.matmul(psR[b % 4][0:T, 0:D], mixed[0][:, k, b * T:(b + 1) * T], wr[:, k, :],
                                   start=(k == 0), stop=(k == DC - 1))
                mm.then_inc(r_ready, 1)
            pe.wait_ge(k_done, 4)
            for b in range(B):
                after(pe, y_made, b - 3)
                for k in range(DC):
                    mm = pe.matmul(psA[b % 4][0:T, 0:D], kT[:, k, b * T:(b + 1) * T], wv[:, k, :],
                                   start=(k == 0), stop=(k == DC - 1))
                mm.then_inc(v_ready, 1)

        @block.scalar
        def _(act):
            for n in range(4):
                act.wait_ge(k_ready, n + 1)
                act.activation(relu[:, n, :], psA[n][:, 0:HALF], ACT.Relu).then_inc(relu_done, 1)
            for b in range(B):
                act.wait_ge(r_ready, b + 1)
                act.activation(r[:, b, :], psR[b % 4][0:T, 0:D], ACT.Sigmoid).then_inc(r_done, 1)


CAP = 30.0


class Route:

    def __init__(self, m, st, xT, wgT, psL, place):
        self.wgT, self.xT, self.st = wgT, xT, st
        self.E = E = wgT.shape[1]
        self.wg = m.sb("r_wg", [P, DC, E])
        names = ("capped", "shifted", "e", "p", "eq1", "w1", "one1", "p2", "eq2", "w2", "one2", "rev", "sel")
        self.z = {n: place[0:T, j * B * E:(j + 1) * B * E].rearrange("t (b e) -> t b e", b=B)
                  for j, n in enumerate(names)}
        self.col = {n: m.sb("r_c_" + n, [T, B])
                    for n in ("max", "sum", "inv", "m1", "i1", "m2", "i2", "top", "itop")}
        self.weight = m.sb("r_weight", [T, B, E])
        self.psL = psL[:, 0:B * E].rearrange("p (b e) -> p b e", e=E)
        self.loaded, self.rev_made, self.l_ready = m.sem("r_loaded"), m.sem("r_rev_made"), m.sem("r_l_ready")
        self.capped, self.e_done, self.step = m.sem("r_capped"), m.sem("r_e_done"), m.sem("r_step")
        self.shifted = m.sem("r_shifted")

    def sync(self, sp):
        sp.dma_start(self.wg[:], self.wgT.rearrange("(c p) e -> p c e", p=P)).then_inc(self.loaded, 16)

    def gpsimd(self, pool):
        for e in range(self.E):
            pool.memset(self.z["rev"][:, :, e:e + 1], float(self.E - e)).then_inc(self.rev_made, 1)

    def tensor(self, pe):
        pe.wait_ge(self.loaded, 16)
        for b in range(B):
            for k in range(DC):
                mm = pe.matmul(self.psL[0:T, b, :], self.xT[:, k, b * T:(b + 1) * T], self.wg[:, k, :],
                               start=(k == 0), stop=(k == DC - 1))
        mm.then_inc(self.l_ready, 1)

    def scalar(self, act):
        act.wait_ge(self.l_ready, 1)
        act.activation(self.z["capped"][:], self.psL[0:T, :, :], ACT.Tanh, scale=1.0 / CAP).then_inc(self.capped, 1)
        act.wait_ge(self.shifted, 1)
        act.activation(self.z["e"][:], self.z["shifted"][:], ACT.Exp, scale=CAP).then_inc(self.e_done, 1)

    def vector(self, dve):
        z, col, step, E = self.z, self.col, self.step, self.E

        def wide(c):
            return c[:].unsqueeze(2).to_broadcast([T, B, E])

        weight = self.weight
        dve.wait_ge(self.capped, 1)
        dve.tensor_reduce(col["max"][:], z["capped"][:], AX, ALU.max).then_inc(step, 1)
        dve.wait_ge(step, 1)
        dve.tensor_tensor(z["shifted"][:], z["capped"][:], wide(col["max"]), ALU.subtract).then_inc(self.shifted, 1)
        dve.wait_ge(self.e_done, 1)
        dve.tensor_reduce(col["sum"][:], z["e"][:], AX, ALU.add).then_inc(step, 1)
        dve.wait_ge(step, 2)
        dve.reciprocal(col["inv"][:], col["sum"][:]).then_inc(step, 1)
        dve.wait_ge(step, 3)
        dve.tensor_tensor(z["p"][:], z["e"][:], wide(col["inv"]), ALU.mult).then_inc(step, 1)
        dve.wait_ge(self.rev_made, E)
        done = 4
        for p, mx, eq, w, first, one in (("p", "m1", "eq1", "w1", "i1", "one1"),
                                         ("p2", "m2", "eq2", "w2", "i2", "one2")):
            dve.wait_ge(step, done)
            dve.tensor_reduce(col[mx][:], z[p][:], AX, ALU.max).then_inc(step, 1)
            dve.wait_ge(step, done + 1)
            dve.tensor_tensor(z[eq][:], z[p][:], wide(col[mx]), ALU.is_equal).then_inc(step, 1)
            dve.wait_ge(step, done + 2)
            dve.tensor_tensor(z[w][:], z[eq][:], z["rev"][:], ALU.mult).then_inc(step, 1)
            dve.wait_ge(step, done + 3)
            dve.tensor_reduce(col[first][:], z[w][:], AX, ALU.max).then_inc(step, 1)
            dve.wait_ge(step, done + 4)
            dve.tensor_tensor(z[one][:], z[w][:], wide(col[first]), ALU.is_equal).then_inc(step, 1)
            done += 5
            dve.wait_ge(step, done)
            if p == "p":
                dve.scalar_tensor_tensor(z["p2"][:], z["one1"][:], -2.0, z["p"][:], ALU.mult,
                                         ALU.add).then_inc(step, 1)
                done += 1
        dve.tensor_tensor(z["sel"][:], z["one1"][:], z["one2"][:], ALU.add).then_inc(step, 1)
        dve.tensor_tensor(col["top"][:], col["m1"][:], col["m2"][:], ALU.add).then_inc(step, 1)
        dve.wait_ge(step, done + 2)
        dve.reciprocal(col["itop"][:], col["top"][:]).then_inc(step, 1)
        dve.tensor_tensor(z["sel"][:], z["sel"][:], z["p"][:], ALU.mult).then_inc(step, 1)
        dve.wait_ge(step, done + 4)
        dve.tensor_tensor(weight[:], z["sel"][:], wide(col["itop"]), ALU.mult).then_inc(step, 1)
        dve.wait_ge(step, done + 5)
        dve.tensor_scalar(weight[:], weight[:], self.st["tanh_g"][0:T, 6:7], None, ALU.mult).then_inc(step, 1)


def expert_ffn(nc, st, xT, io):
    x = st["x"]
    E, _, I = io["L2_ffn_w1T"].shape
    IC = I // P
    HB = B // 2
    UPS = 2 * IC
    SLAB = DC * I
    with ExitStack() as ctx:
        m = Memory(nc, ctx, st, "f2", words=2 * SLAB + 4 * HALF + 600)
        xs = [m.rounded(f"x_{k}", [P, DC, R]) for k in ("high", "low")]
        up_w = [[m.rounded(f"up{u}_{k}", [P, 2, DC, I]) for k in ("high", "low")] for u in range(2)]
        down_w = [[m.rounded(f"down{u}_{k}", [P, IC, D]) for k in ("high", "low")] for u in range(2)]
        hs = [[m.rounded(f"h{f}_{k}", [P, IC, HALF]) for k in ("high", "low")] for f in range(2)]
        raw = [m.sb(f"raw{j}", [P, SLAB]) for j in range(2)]
        gel_place, gated_place = m.sb("gel", [P, HB * D]), m.sb("gated", [P, 2 * HALF])
        gel, gated = ([z[:, j * HALF:(j + 1) * HALF] for j in range(2)] for z in (gel_place, gated_place))
        spacer = m.sb("spacer", [P, 1])
        ps1 = [m.ps(f"ps1_{j}") for j in range(2)]
        ps3 = [m.ps(f"ps3_{j}") for j in range(2)]
        psY = [m.ps(f"psY{j}") for j in range(2)]
        norm = Normalized(m, st, xT, ps1 + ps3, place=gel_place[0:T, :].rearrange("t (b d) -> t b d", b=HB))
        routing = Route(m, st, xT, io["L2_ffn_wgT"], m.ps("psL"), gated_place)
        raw_loaded = [m.sem(f"raw_loaded{j}") for j in range(2)]
        x_high, x_low, w_high, w_low = (m.sem(n) for n in ("x_high", "x_low", "w_high", "w_low"))
        up_ready, gel_done, gated_done = m.sem("up_ready"), m.sem("gel_done"), m.sem("gated_done")
        h_high, h_low = m.sem("h_high"), m.sem("h_low")
        y_ready, y_added = m.sem("y_ready"), m.sem("y_added")
        block = ctx.enter_context(nc.Block())

        def slab_parts(u, k):
            if k == 2:
                return [w[:].rearrange("p c d -> p (c d)") for w in down_w[u]]
            return [w[:, k].rearrange("p c i -> p (c i)") for w in up_w[u]]

        @block.sync
        def _(sp):
            def run(e, u, first, last):
                for k, z in enumerate(("L2_ffn_w1T", "L2_ffn_w3T", "L2_ffn_w2T")):
                    n, j = e * 3 + k, (u + k) % 2
                    after(sp, w_low, n - 1)
                    dst = raw[j].rearrange("p (c i) -> p c i", c=DC if k < 2 else IC)
                    sp.dma_start(dst, io[z][bass.ds(e, 1)].rearrange("e (c p) i -> p (e c) i", p=P)
                                 ).then_inc(raw_loaded[j], 16)

            routing.sync(sp)
            in_pairs(sp, run)

        @block.gpsimd
        def _(pool):
            def low(e, u, k):
                n, j = e * 3 + k, (u + k) % 2
                high, rest = slab_parts(u, k)
                pool.wait_ge(w_high, n + 1)
                pool.tensor_tensor(rest, raw[j], high.bitcast(F32), ALU.subtract).then_inc(w_low, 1)

            norm.gpsimd(pool)
            routing.gpsimd(pool)
            for k in range(3):
                low(0, 0, k)

            def run(e, u, first, last):
                if not last:
                    for k in range(3):
                        low(e + 1, 1 - u, k)

            in_pairs(pool, run)

        @block.tensor
        def _(pe):
            def up(e, u, f, c):
                n = e * UPS + f * IC + c
                if c == 0 and f == 0:
                    pe.wait_ge(w_low, e * 3 + 2)
                after(pe, gated_done, n - 1)
                for k3, ps in enumerate((ps1, ps3)):
                    for k in range(DC):
                        mm = split_product(pe, ps[c % 2][:, 0:HALF],
                                           [w[:, k3, k, c * P:(c + 1) * P] for w in up_w[u]],
                                           [z[:, k, f * HALF:(f + 1) * HALF] for z in xs],
                                           start=(k == 0), stop=(k == DC - 1))
                mm.then_inc(up_ready, 1)

            def down(e, u, f, j):
                n = e * B + f * HB + j
                if j == 0:
                    pe.wait_ge(w_low, e * 3 + 3)
                    pe.wait_ge(h_low, e * UPS + (f + 1) * IC)
                pe.wait_ge(y_added, n + 1)
                for c in range(IC):
                    mm = split_product(pe, psY[j % 2][0:T, 0:D],
                                       [h[:, c, j * T:(j + 1) * T] for h in hs[f]],
                                       [w[:, c, :] for w in down_w[u]], start=(c == 0), stop=(c == IC - 1))
                mm.then_inc(y_ready, 1)

            norm.tensor(pe)
            norm.wait(pe)
            routing.tensor(pe)
            pe.wait_ge(x_low, 1)

            def run(e, u, first, last):
                for f in range(2):
                    for c in range(IC):
                        up(e, u, f, c)
                        if c % 2 and f == 1:
                            down(e, u, 0, c // 2)
                        elif c % 2 and not first:
                            down(e - 1, 1 - u, 1, c // 2)

            in_pairs(pe, run)
            for j in range(HB):
                down(E - 1, 1, 1, j)

        @block.scalar
        def _(act):
            def split(e, u, k):
                n, j = e * 3 + k, (u + k) % 2
                act.wait_ge(raw_loaded[j], (n - j) * 8 + 16)
                if not (isinstance(e, int) and e < 2):
                    if k < 2:
                        act.wait_ge(up_ready, (e - 1) * UPS)
                    else:
                        act.wait_ge(y_ready, (e - 1) * B)
                act.copy(slab_parts(u, k)[0], raw[j]).then_inc(w_high, 1)

            def high(e, f, c):
                n = e * UPS + f * IC + c
                act.wait_ge(gated_done, n + 1)
                act.copy(hs[f][0][:, c, :], gated[c % 2]).then_inc(h_high, 1)

            for k in range(2):
                split(0, 0, k)
            norm.wait(act)
            act.copy(xs[0][:], xT[:]).then_inc(x_high, 1)
            routing.scalar(act)
            split(0, 0, 2)

            def run(e, u, first, last):
                for f in range(2):
                    for c in range(IC):
                        n = e * UPS + f * IC + c
                        act.wait_ge(up_ready, n + 1)
                        act.activation(gel[c % 2], ps1[c % 2][:, 0:HALF], ACT.Gelu).then_inc(gel_done, 1)
                        if c:
                            high(e, f, c - 1)
                        elif f:
                            high(e, 0, IC - 1)
                        elif not first:
                            high(e - 1, 1, IC - 1)
                        if not last and (f, c) in ((0, 2), (0, 5), (1, 2)):
                            split(e + 1, 1 - u, ((0, 2), (0, 5), (1, 2)).index((f, c)))

            in_pairs(act, run)
            high(E - 1, 1, IC - 1)

        @block.vector
        def _(dve):
            def low(e, f, c):
                n = e * UPS + f * IC + c
                high, rest = hs[f]
                dve.wait_ge(h_high, n + 1)
                dve.tensor_tensor(rest[:, c, :], gated[c % 2], high[:, c, :].bitcast(F32),
                                  ALU.subtract).then_inc(h_low, 1)

            def add(e, f, j):
                b = f * HB + j
                dve.wait_ge(y_ready, e * B + b + 1)
                dve.scalar_tensor_tensor(x[:, b, :], psY[j % 2][0:T, 0:D], routing.weight[:, b, bass.ds(e, 1)], x[:, b, :],
                                         ALU.mult, ALU.add).then_inc(y_added, 1)

            norm.vector_statistics(dve)
            norm.vector_output(dve)
            dve.wait_ge(x_high, 1)
            dve.tensor_tensor(xs[1][:], xT[:], xs[0][:].bitcast(F32), ALU.subtract).then_inc(x_low, 1)
            dve.memset(spacer, 0.0).then_inc(y_added, 2)
            routing.vector(dve)

            def run(e, u, first, last):
                for f in range(2):
                    for c in range(IC):
                        n = e * UPS + f * IC + c
                        after(dve, h_low, n - 1)
                        dve.wait_ge(gel_done, n + 1)
                        dve.tensor_tensor(gated[c % 2], ps3[c % 2][:, 0:HALF], gel[c % 2],
                                          ALU.mult).then_inc(gated_done, 1)
                        if c:
                            low(e, f, c - 1)
                        elif f:
                            low(e, 0, IC - 1)
                        elif not first:
                            low(e - 1, 1, IC - 1)
                        if c % 2 and f == 1:
                            add(e, 0, c // 2)
                        elif c % 2 and not first:
                            add(e - 1, 1, c // 2)

            in_pairs(dve, run)
            low(E - 1, 1, IC - 1)
            for j in range(HB):
                add(E - 1, 1, j)


def quantized_ffn(nc, st, io, gate=7):
    x, ident, tg = st["x"], st["ident"], st["tanh_g"]
    HID = io["L3_ffn_w1T"].shape[1]
    HC = HID // P
    HB = B // 2
    ROUND = 1.5 * 2.0 ** 23
    with ExitStack() as ctx:
        m = Memory(nc, ctx, st, "f3")
        w = [m.sb("w1", [P, DC * HID]), m.sb("w2", [P, HC * D])]
        q = [m.sb("q1", [P, DC * HID], BF16), m.sb("q2", [P, HC * D], BF16)]
        q1 = q[0].rearrange("p (c n) -> p c n", c=DC)
        q2 = q[1].rearrange("p (c n) -> p c n", c=HC)
        ones = m.sb("ones", [P, P])
        half = m.sb("half", [T, 1])
        shift = m.sb("shift", [P, 2])
        identb = m.sb("identb", [P, P], BF16)
        spacer = m.sb("spacer", [T, 1])
        wsum = m.sb("wsum", [P, 2])
        wmean = m.sb("wmean", [P, 2])
        wscale = m.sb("wscale", [P, 2])
        gmean = m.sb("gmean", [P, 1])
        g1, c1 = m.sb("g1", [T, D]), m.sb("c1", [T, D])
        g2, c2 = m.sb("g2", [T, HID]), m.sb("c2", [T, HID])
        b1, b2 = m.sb("b1", [T, HID]), m.sb("b2", [T, D])
        hB = m.sb("hB", [T, B, D], BF16)
        hT = m.sb("hT", [P, DC, R], BF16)
        top1, unit1, scale1, back1 = (m.sb(n + "1", [T, B]) for n in ("top", "unit", "scale", "back"))
        top2, unit2, scale2, back2 = (m.sb(n + "2", [T, 2]) for n in ("top", "unit", "scale", "back"))
        z = [m.sb(f"z{u}", [T, HID]) for u in range(2)]
        zq = [m.sb(f"zq{u}", [T, HID], BF16) for u in range(2)]
        zT = [m.sb(f"zT{u}", [P, HC, T], BF16) for u in range(2)]
        stats = m.sb("stats", [T, 2, 12])
        mv = m.sb("mv", [T, 2, 2])
        ve = m.sb("ve", [T, 2])
        rstd = m.sb("rstd", [T, 2])
        psU = [m.ps(f"psU{j}", 2) for j in range(2)]
        psX = [m.ps(f"psX{j}").bitcast(BF16)[:, 0:DC * HB * T].rearrange("p (c r) -> p c r", c=DC)
               for j in range(2)]
        psZ = m.ps("psZ").bitcast(BF16)[:, 0:HC * T].rearrange("p (c t) -> p c t", t=T)
        bank = m.ps("psY")
        psY, psW = bank[:, 0:D], bank[:, 0:2]
        w_loaded, v_loaded, made = m.sem("w_loaded"), m.sem("v_loaded"), m.sem("made")
        w_summed, w_total, w_step = m.sem("w_summed"), m.sem("w_total"), m.sem("w_step")
        w_shifted, w_clipped, w_quantized = m.sem("w_shifted"), m.sem("w_clipped"), m.sem("w_quantized")
        h_step, h_scaled, h_shifted, h_clipped = (m.sem(n) for n in ("h_step", "h_scaled", "h_shifted", "h_clipped"))
        h_quantized, h_turned, h_copied = m.sem("h_quantized"), m.sem("h_turned"), m.sem("h_copied")
        u_ready, u_biased, gelu_done = m.sem("u_ready"), m.sem("u_biased"), m.sem("gelu_done")
        step, ve_done, rstd_done = m.sem("step"), m.sem("ve_done"), m.sem("rstd_done")
        z_scaled, z_shifted, z_clipped = m.sem("z_scaled"), m.sem("z_shifted"), m.sem("z_clipped")
        z_quantized, z_turned, z_copied = m.sem("z_quantized"), m.sem("z_turned"), m.sem("z_copied")
        y_ready, y_added, x_biased = m.sem("y_ready"), m.sem("y_added"), m.sem("x_biased")
        norm = Normalized(m, st, None, [], rounds=2)
        h = norm.xn
        block = ctx.enter_context(nc.Block())

        @block.sync
        def _(sp):
            sp.dma_start(w[0].rearrange("p (c n) -> p c n", c=DC),
                         io["L3_ffn_w1T"].rearrange("(c p) n -> p c n", p=P)).then_inc(w_loaded, 16)
            sp.dma_start(w[1].rearrange("p (c n) -> p c n", c=HC),
                         io["L3_ffn_w2T"].rearrange("(c p) n -> p c n", p=P)).then_inc(w_loaded, 16)
            for t, n in ((g1, "ln1_g"), (c1, "ln1_b"), (b2, "b2"), (b1, "b1"), (g2, "ln2_g"), (c2, "ln2_b")):
                sp.dma_start(t[:], broadcast_rows(io["L3_ffn_" + n], T)).then_inc(v_loaded, 16)

        @block.gpsimd
        def _(pool):
            norm.gpsimd_start(pool)
            pool.memset(ones[:], 1.0).then_inc(made, 1)
            pool.memset(half[:], -0.5).then_inc(made, 1)
            pool.memset(shift[:, 0:1], ROUND).then_inc(made, 1)
            pool.memset(shift[:, 1:2], -ROUND).then_inc(made, 1)
            pool.tensor_copy(identb[:], ident[:]).then_inc(made, 1)
            pool.wait_ge(made, 5)
            for r in range(2):
                norm.gpsimd_power(pool, r)
            pool.wait_ge(v_loaded, 96)
            pool.wait_ge(norm.xn_done, B)
            pool.tensor_scalar(b2[:], b2[:], tg[0:T, gate:gate + 1], None, ALU.mult).then_inc(x_biased, 1)
            pool.wait_ge(x_biased, 1)
            pool.tensor_tensor(x[:], x[:], b2[:].unsqueeze(1).to_broadcast([T, B, D]), ALU.add
                               ).then_inc(x_biased, 1)

            def run(b, u, first, last):
                pool.wait_ge(ve_done, b + 1)
                pool.tensor_tensor(rstd[:, u:u + 1], ve[:, u:u + 1], half[:], ALU.pow).then_inc(rstd_done, 1)

            in_pairs(pool, run)

        @block.tensor
        def _(pe):
            def up(b, u):
                after(pe, u_biased, b - 1)
                for f in range(2):
                    for k in range(DC):
                        mm = pe.matmul(psU[u][0:T, f, :], hT[:, k, bass.ds(b * T, T)],
                                       q1[:, k, f * 512:(f + 1) * 512], start=(k == 0), stop=(k == DC - 1))
                mm.then_inc(u_ready, 1)

            pe.wait_ge(made, 5)
            pe.wait_ge(w_summed, 2)
            pe.matmul(psW, ones[:], wsum[:], start=True, stop=True).then_inc(w_total, 1)
            for j in range(2):
                pe.wait_ge(h_quantized, j + 1)
                for c in range(DC):
                    for i in range(HB):
                        mm = pe.transpose(psX[j][:, c, i * T:(i + 1) * T], hB[:, j * HB + i, c * P:(c + 1) * P],
                                          identb[0:T, 0:T])
                mm.then_inc(h_turned, 1)
            pe.wait_ge(w_quantized, 1)
            pe.wait_ge(h_copied, 1)
            up(0, 0)
            pe.wait_ge(h_copied, 2)

            def run(b, u, first, last):
                if not last:
                    up(b + 1, 1 - u)
                if first:
                    pe.wait_ge(w_quantized, 2)
                pe.wait_ge(z_quantized, b + 1)
                for c in range(HC):
                    mm = pe.transpose(psZ[:, c, :], zq[u][:, c * P:(c + 1) * P], identb[0:T, 0:T])
                mm.then_inc(z_turned, 1)
                pe.wait_ge(z_copied, b + 1)
                after(pe, y_added, b)
                for c in range(HC):
                    mm = pe.matmul(psY[0:T, :], zT[u][:, c, :], q2[:, c, :], start=(c == 0), stop=(c == HC - 1))
                mm.then_inc(y_ready, 1)

            in_pairs(pe, run)

        @block.scalar
        def _(act):
            def integers(j):
                act.wait_ge(w_clipped, j + 1)
                act.activation(q[j], w[j], ACT.Identity, bias=shift[:, 1:2]).then_inc(w_quantized, 1)

            def gelu(b, u):
                act.wait_ge(u_biased, b + 1)
                act.activation(z[u][:], z[u][:], ACT.Gelu).then_inc(gelu_done, 1)

            act.wait_ge(w_loaded, 32)
            for j in range(2):
                act.activation(q[j], w[j], ACT.Abs, accum_out=wsum[:, j:j + 1]).then_inc(w_summed, 1)
            act.wait_ge(made, 5)
            act.wait_ge(w_step, 2)
            act.wait_ge(w_summed, 2)
            for j in range(2):
                act.activation(w[j], w[j], ACT.Identity, bias=shift[:, 0:1], scale=wscale[:, j:j + 1]
                               ).then_inc(w_shifted, 1)
            act.wait_ge(h_scaled, 1)
            for b in range(B):
                act.activation(h[:, b, :], h[:, b, :], ACT.Identity, bias=shift[0:T, 0:1],
                               scale=scale1[:, b:b + 1]).then_inc(h_shifted, 1)
            for j in range(2):
                act.wait_ge(h_clipped, j + 1)
                act.activation(hB[:, j * HB:(j + 1) * HB, :], h[:, j * HB:(j + 1) * HB, :], ACT.Identity,
                               bias=shift[0:T, 1:2]).then_inc(h_quantized, 1)
                if j == 0:
                    integers(0)
            for j in range(2):
                act.wait_ge(h_turned, j + 1)
                act.copy(hT[:, :, j * HB * T:(j + 1) * HB * T], psX[j]).then_inc(h_copied, 1)
            gelu(0, 0)
            integers(1)

            def run(b, u, first, last):
                act.wait_ge(z_scaled, b + 1)
                act.activation(z[u][:], z[u][:], ACT.Identity, bias=shift[0:T, 0:1], scale=scale2[:, u:u + 1]
                               ).then_inc(z_shifted, 1)
                if not last:
                    gelu(b + 1, 1 - u)
                act.wait_ge(z_clipped, b + 1)
                act.activation(zq[u][:], z[u][:], ACT.Identity, bias=shift[0:T, 1:2]).then_inc(z_quantized, 1)
                act.wait_ge(z_turned, b + 1)
                act.copy(zT[u][:], psZ).then_inc(z_copied, 1)

            in_pairs(act, run)

        @block.vector
        def _(dve):
            norm.vector_statistics(dve)
            norm.vector_rows(dve)
            dve.wait_ge(w_total, 1)
            dve.tensor_scalar(wmean[:], psW, 1.0 / (D * HID), 1e-5, ALU.mult, ALU.max).then_inc(w_step, 1)
            dve.wait_ge(w_step, 1)
            dve.reciprocal(wscale[:], wmean[:]).then_inc(w_step, 1)
            dve.tensor_scalar(gmean[:], wmean[:, 1:2], tg[:, gate:gate + 1], None, ALU.mult).then_inc(w_step, 1)
            dve.wait_ge(v_loaded, 96)
            dve.wait_ge(norm.xn_done, 2 * B)
            for n, (v, op) in enumerate(((g1, ALU.mult), (c1, ALU.add))):
                dve.tensor_tensor(h[:], h[:], v[:].unsqueeze(1).to_broadcast([T, B, D]), op).then_inc(h_step, 1)
                dve.wait_ge(h_step, n + 1)
            dve.tensor_reduce(top1[:], h[:], AX, ALU.max, apply_absolute_value=True).then_inc(h_step, 1)
            dve.wait_ge(h_step, 3)
            dve.tensor_scalar(unit1[:], top1[:], 1e-5, 1.0 / 127.0, ALU.max, ALU.mult).then_inc(h_step, 1)
            dve.wait_ge(h_step, 4)
            dve.reciprocal(scale1[:], unit1[:]).then_inc(h_scaled, 1)
            dve.tensor_scalar(back1[:], unit1[:], wmean[0:T, 0:1], None, ALU.mult).then_inc(h_step, 1)

            def clip_weights(j):
                dve.wait_ge(w_shifted, j + 1)
                dve.tensor_scalar(w[j], w[j], ROUND + 1, ROUND - 1, ALU.min, ALU.max).then_inc(w_clipped, 1)

            clip_weights(0)
            for j in range(2):
                hh = h[:, j * HB:(j + 1) * HB, :]
                dve.wait_ge(h_shifted, HB * (j + 1))
                dve.tensor_scalar(hh, hh, ROUND + 127, ROUND - 128, ALU.min, ALU.max).then_inc(h_clipped, 1)
            clip_weights(1)
            dve.wait_ge(h_step, 5)
            dve.wait_ge(w_step, 3)

            STEPS = 8

            def biased(b, u):
                dve.wait_ge(u_ready, b + 1)
                after(dve, z_quantized, b - 1)
                dve.scalar_tensor_tensor(z[u][:], psU[u][0:T, :, :].rearrange("t f n -> t (f n)"),
                                         back1[:, bass.ds(b, 1)], b1[:], ALU.mult, ALU.add).then_inc(u_biased, 1)

            def scaled(b, u):
                done = b * STEPS
                zs = z[u][:]
                dve.wait_ge(gelu_done, b + 1)
                dve.bn_stats(stats[:, u, 0:6], zs[:, 0:512]).then_inc(step, 1)
                dve.bn_stats(stats[:, u, 6:12], zs[:, 512:HID]).then_inc(step, 1)
                dve.wait_ge(step, done + 2)
                dve.memset(spacer[:], 0.0)
                dve.bn_aggr(mv[:, u, :], stats[:, u, :]).then_inc(step, 1)
                dve.wait_ge(step, done + 3)
                dve.tensor_scalar(ve[:, u:u + 1], mv[:, u, 1:2], EPS, None, ALU.add).then_inc(ve_done, 1)
                dve.scalar_tensor_tensor(zs, zs, mv[:, u, 0:1], g2[:], ALU.subtract, ALU.mult).then_inc(step, 1)
                dve.wait_ge(rstd_done, b + 1)
                dve.wait_ge(step, done + 4)
                dve.scalar_tensor_tensor(zs, zs, rstd[:, u:u + 1], c2[:], ALU.mult, ALU.add).then_inc(step, 1)
                dve.wait_ge(step, done + 5)
                dve.tensor_reduce(top2[:, u:u + 1], zs, AX, ALU.max, apply_absolute_value=True).then_inc(step, 1)
                dve.wait_ge(step, done + 6)
                dve.tensor_scalar(unit2[:, u:u + 1], top2[:, u:u + 1], 1e-5, 1.0 / 127.0, ALU.max, ALU.mult
                                  ).then_inc(step, 1)
                dve.wait_ge(step, done + 7)
                dve.reciprocal(scale2[:, u:u + 1], unit2[:, u:u + 1]).then_inc(z_scaled, 1)
                dve.tensor_scalar(back2[:, u:u + 1], unit2[:, u:u + 1], gmean[0:T, :], None, ALU.mult
                                  ).then_inc(step, 1)

            def clipped(b, u):
                dve.wait_ge(z_shifted, b + 1)
                dve.tensor_scalar(z[u][:], z[u][:], ROUND + 127, ROUND - 128, ALU.min, ALU.max
                                  ).then_inc(z_clipped, 1)

            def add(b, u):
                dve.wait_ge(y_ready, b + 1)
                dve.wait_ge(step, b * STEPS + STEPS)
                dve.scalar_tensor_tensor(x[:, bass.ds(b, 1), :], psY[0:T, :].unsqueeze(1), back2[:, u:u + 1],
                                         x[:, bass.ds(b, 1), :], ALU.mult, ALU.add).then_inc(y_added, 1)

            biased(0, 0)
            dve.wait_ge(x_biased, 2)

            def run(b, u, first, last):
                scaled(b, u)
                if not last:
                    biased(b + 1, 1 - u)
                if not first:
                    add(b - 1, 1 - u)
                clipped(b, u)

            in_pairs(dve, run)
            add(B - 1, 1)


FFN = {1: low_rank_ffn, 3: shift_ffn, 5: expert_ffn, 7: lambda nc, st, xT, io: quantized_ffn(nc, st, io)}


A0 = Shape(heads=16, width=64, keys=S2 + T, scale=0.125, look=2)
A1 = Shape(heads=1, width=256, keys=S2, scale=1.0 / 16, look=0)
A2 = Shape(heads=16, width=16, keys=S2, scale=0.25, look=2)


def start_phase(nc, st, io):
    x, ident, tg, headmask = st["x"], st["ident"], st["tanh_g"], st["headmask"]
    with ExitStack() as ctx:
        m = Memory(nc, ctx, st, "start")
        g = m.sb("g", [P, 8])
        loaded, made, done = m.sem("loaded"), m.sem("made"), m.sem("done")
        block = ctx.enter_context(nc.Block())

        @block.sync
        def _(sp):
            sp.dma_start(x[:], io["x"].rearrange("b t d -> t b d")).then_inc(loaded, 16)
            sp.dma_start(g[:, 0:4], broadcast_rows(io["g_xattn"], P)).then_inc(loaded, 16)
            sp.dma_start(g[:, 4:8], broadcast_rows(io["g_ffn"], P)).then_inc(loaded, 16)

        @block.gpsimd
        def _(pool):
            pool.memset(ident[:], 0.0).then_inc(made, 1)
            pool.memset(headmask[:], 1.0).then_inc(made, 1)
            pool.wait_ge(made, 2)
            pool.affine_select(out=ident[:], in_=ident[:], compare_op=ALU.not_equal, fill=1.0, base=0,
                               pattern=[[-1, P]], channel_multiplier=1).then_inc(made, 1)
            pool.affine_select(out=headmask[:], in_=headmask[:], compare_op=ALU.is_ge, fill=0.0, base=0,
                               pattern=[[-16, 8]], channel_multiplier=1).then_inc(made, 1)
            pool.wait_ge(made, 4)
            pool.affine_select(out=headmask[:], in_=headmask[:], compare_op=ALU.is_ge, fill=0.0, base=15,
                               pattern=[[16, 8]], channel_multiplier=-1).then_inc(made, 1)

        @block.scalar
        def _(act):
            act.wait_ge(loaded, 48)
            act.activation(tg[:], g[:], ACT.Tanh).then_inc(done, 1)


def store_phase(nc, st, out):
    with ExitStack() as ctx:
        m = Memory(nc, ctx, st, "store")
        stored = m.sem("stored")
        block = ctx.enter_context(nc.Block())

        @block.sync
        def _(sp):
            sp.dma_start(out.rearrange("b t d -> t b d"), st["x"][:]).then_inc(stored, 16)
            sp.wait_ge(stored, 16)


def flamingo_program(nc, io, out, layers=range(8)):
    with ExitStack() as ctx:
        def sb(name, shape):
            return ctx.enter_context(nc.sbuf_tensor(name, shape, F32))

        st = dict(x=sb("x", [T, B, D]), ident=sb("ident", [P, P]), tanh_g=sb("tanh_g", [P, 8]),
                  headmask=sb("headmask", [P, 8]),
                  banks=ctx.enter_context(nc.psum_tensor("banks", [P, 8, 512], F32)),
                  semaphores=[])
        xT = sb("xT", [P, DC, R])
        start_phase(nc, st, io)
        for n in layers:
            recycle_semaphores(nc, st)
            if n == 0:
                attention_phase(nc, st, "a0", A0, xT, io["L0_xattn_Wq"], io["L0_xattn_Wkv"][:, 0:A0.inner],
                                io["L0_xattn_Wkv"][:, A0.inner:2 * A0.inner], wo=io["L0_xattn_Wo"],
                                ctx_rows=io["ctx"], ctx_gb=(io["L0_xattn_ln1_g"], io["L0_xattn_ln1_b"]), gate=0,
                                rounds=2, affine=(io["L0_xattn_ln2_g"], io["L0_xattn_ln2_b"]))
            elif n == 2:
                attention_phase(nc, st, "a1", A1, xT, io["L1_xattn_Wq"], io["L1_xattn_Wkv"][:, 0:D],
                                io["L1_xattn_Wkv"][:, D:2 * D], ctxT=io["ctxT"], gate=1)
            elif n == 4:
                attention_phase(nc, st, "a2", A2, xT, io["L2_xattn_wq_k"], io["L2_xattn_wk_k"],
                                io["L2_xattn_wv_k"], wo=io["L2_xattn_wo_k"], qb=io["L2_xattn_wq_b"],
                                kb=io["L2_xattn_wk_b"], vb=io["L2_xattn_wv_b"], ob=io["L2_xattn_wo_b"],
                                ctxT=io["ctxT"], group=io["fside_BxSxS2_0"], mask=io["mask_BxSxS2_ik1"], gate=2)
            elif n == 6:
                attention_phase(nc, st, "a3", A2, xT, io["L3_xattn_WqT"], io["L3_xattn_WkT"],
                                io["L3_xattn_WvT"], wo=io["L3_xattn_WoT"], qb=io["L3_xattn_bq"],
                                kb=io["L3_xattn_bk"], vb=io["L3_xattn_bv"], ob=io["L3_xattn_bo"],
                                ctxT=io["ctxT"], gate=3)
            else:
                FFN[n](nc, st, xT, io)
        store_phase(nc, st, out)


def laid_out(inputs):
    import numpy as np

    swap = {"L1_ffn_W_r": (1, 0), "L1_ffn_W_k": (1, 0), "L1_ffn_W_v": (1, 0),
            "L2_ffn_wg": (1, 0), "L2_ffn_w1": (0, 2, 1), "L2_ffn_w3": (0, 2, 1), "L2_ffn_w2": (0, 2, 1),
            "L3_xattn_Wq": (1, 0), "L3_xattn_Wk": (1, 0), "L3_xattn_Wv": (1, 0), "L3_xattn_Wo": (1, 0),
            "L3_ffn_w1": (1, 0), "L3_ffn_w2": (1, 0)}
    arrays = {}
    for name, a in inputs.items():
        a = np.asarray(a)
        if name == "ctx_1024":
            arrays["ctx"] = np.ascontiguousarray(a)
            arrays["ctxT"] = np.ascontiguousarray(np.transpose(a, (2, 0, 1)))
        elif name in swap:
            arrays[name + "T"] = np.ascontiguousarray(np.transpose(a, swap[name]))
        else:
            arrays[name] = np.ascontiguousarray(a)
    return arrays


def kernel(**inputs):
    import numpy as _np
    import concourse.bacc as _bacc
    from concourse import mybir as _mybir
    from concourse.bass_utils import run_bass_kernel_spmd as _run

    nc = _bacc.Bacc("TRN2", target_bir_lowering=False, num_devices=1)
    arrays = laid_out(inputs)
    io = {name: nc.dram_tensor(f"in_{name}", a.shape, _mybir.dt.from_np(a.dtype), kind="ExternalInput").ap()
          for name, a in arrays.items()}
    out = nc.dram_tensor("out_x", (B, T, D), _mybir.dt.float32, kind="ExternalOutput").ap()
    flamingo_program(nc, io, out)
    r = _run(nc, [{f"in_{name}": a for name, a in arrays.items()}], core_ids=[0])
    return r.results[0]["out_x"]
```
